# Optimizing a Trainium2 kernel written in Bass

```python
import numpy as np
import jax
import jax.numpy as jnp

def _softmax(x, axis=-1):
    return jax.nn.softmax(x, axis=axis)

def _gelu(x):
    return jax.nn.gelu(x, approximate=True)

def _silu(x):
    return jax.nn.silu(x)

def _sigmoid(x):
    return jax.nn.sigmoid(x)

def _layernorm(x, axis=-1, eps=1e-05):
    m = jnp.mean(x, axis=axis, keepdims=True)
    v = jnp.var(x, axis=axis, keepdims=True)
    return (x - m) / jnp.sqrt(v + eps)

def _scatter_add(tgt, idx, src, axis=0):
    return tgt.at[idx].add(src)

def _segment_sum(src, seg, n):
    return jax.ops.segment_sum(src, seg, n)
kernel_name = 'mk_seq_preln_d1_jaxref_r4_24bb2b'

def setup_inputs(seed: int=0):
    np.random.seed(seed)
    _w = jnp.asarray

    def _L0_attn_setup():
        import jax, jax.numpy as jnp
        import numpy as np
        import math
        B, S, DIM = (1, 512, 256)
        H, KVH = (16, 4)
        HD = DIM // H
        KV_DIM = KVH * HD

        def _rms_norm(x):
            eps = jnp.finfo(x.dtype).eps
            return x * jax.lax.rsqrt(jnp.mean(x * x, axis=-1, keepdims=True) + eps)

        def _polar_rotary(seq_len, head_dim, dtype):
            angles = jnp.arange(0, head_dim, 2, dtype=jnp.float32) / head_dim * math.pi
            pos = jnp.arange(seq_len, dtype=jnp.float32)
            radius = 1.0 / (1.0 + pos[:, None] * 0.01)
            ang = pos[:, None] * angles[None, :]
            cos = (radius * jnp.cos(ang)).astype(dtype)
            sin = (radius * jnp.sin(ang)).astype(dtype)
            return (cos[None, None], sin[None, None])

        def _apply_rotary(x, cos, sin):
            half = x.shape[-1] // 2
            x1, x2 = (x[..., :half], x[..., half:])
            return jnp.concatenate([x1 * cos + x2 * sin, x1 * -sin + x2 * cos], axis=-1)

        def _causal_attn(q, k, v, scale, mask):
            s = jnp.einsum('bhqd,bhkd->bhqk', q, k) * scale
            s = jnp.where(mask, s, jnp.finfo(s.dtype).min)
            p = jax.nn.softmax(s, axis=-1)
            return jnp.einsum('bhqk,bhkd->bhqd', p, v)
        key = jax.random.key(seed)
        ks = jax.random.split(key, 8)
        std = 0.02
        return {'x': jax.random.normal(ks[0], (B, S, DIM), jnp.float32), 'Wq': jax.random.normal(ks[1], (DIM, DIM), jnp.float32) * std, 'Wk': jax.random.normal(ks[2], (KV_DIM, DIM), jnp.float32) * std, 'Wv': jax.random.normal(ks[3], (KV_DIM, DIM), jnp.float32) * std, 'Wg': jax.random.normal(ks[4], (KV_DIM, DIM), jnp.float32) * std, 'Wo': jax.random.normal(ks[5], (DIM, DIM), jnp.float32) * std, 'q_gain': jnp.full((H,), 1.0, jnp.float32), 'lambda_param': jnp.full((H,), 0.5, jnp.float32)}
    _L0_attn_in = _L0_attn_setup()

    def _L0_ffn_setup():
        import jax, jax.numpy as jnp
        import numpy as np
        DIM = 256
        E = 16
        TOPK = 2
        G = 4
        TOPK_G = 2
        INTER = 128
        N_SHARED = 2
        ROUTE_SCALE = 1.0

        def _gate(xf, gate_w, gate_b):
            scores = xf @ gate_w.T
            scores = jax.nn.softmax(scores.astype(jnp.float32), axis=-1)
            orig = scores
            scores = scores + gate_b
            T = xf.shape[0]
            sg = scores.reshape(T, G, E // G)
            group_scores = jax.lax.top_k(sg, 2)[0].sum(-1)
            _, gidx = jax.lax.top_k(group_scores, TOPK_G)
            keep = jax.nn.one_hot(gidx, G).sum(axis=1) > 0
            sg = jnp.where(keep[:, :, None], sg, -jnp.inf)
            scores = sg.reshape(T, E)
            _, idx = jax.lax.top_k(scores, TOPK)
            weights = jnp.take_along_axis(orig, idx, axis=1)
            weights = (weights * ROUTE_SCALE).astype(xf.dtype)
            return (weights, idx)
        key = jax.random.key(seed)
        ks = jax.random.split(key, 16)
        s = lambda fan_in: 1.0 / np.sqrt(fan_in)
        inp = {'x': jax.random.normal(ks[0], (4, 256, DIM), dtype=jnp.float32), 'gate_w': jax.random.normal(ks[1], (E, DIM), dtype=jnp.float32) * s(DIM), 'gate_b': jnp.zeros((E,), dtype=jnp.float32), 'We1': jax.random.normal(ks[2], (E, DIM, INTER), dtype=jnp.float32) * s(DIM), 'be1': jnp.zeros((E, INTER), dtype=jnp.float32), 'We2': jax.random.normal(ks[3], (E, INTER, DIM), dtype=jnp.float32) * s(INTER), 'be2': jnp.zeros((E, DIM), dtype=jnp.float32), 'We3': jax.random.normal(ks[4], (E, DIM, INTER), dtype=jnp.float32) * s(DIM), 'be3': jnp.zeros((E, INTER), dtype=jnp.float32), 'ws1': jax.random.normal(ks[5], (DIM, N_SHARED * INTER), dtype=jnp.float32) * s(DIM), 'bs1': jnp.zeros((N_SHARED * INTER,), dtype=jnp.float32), 'ws2': jax.random.normal(ks[6], (N_SHARED * INTER, DIM), dtype=jnp.float32) * s(N_SHARED * INTER), 'bs2': jnp.zeros((DIM,), dtype=jnp.float32), 'ws3': jax.random.normal(ks[7], (DIM, N_SHARED * INTER), dtype=jnp.float32) * s(DIM), 'bs3': jnp.zeros((N_SHARED * INTER,), dtype=jnp.float32)}
        return inp
    _L0_ffn_in = _L0_ffn_setup()
    _d = {'L0_attn_x': _L0_attn_in['x'], 'L0_attn_Wq': _L0_attn_in['Wq'], 'L0_attn_Wk': _L0_attn_in['Wk'], 'L0_attn_Wv': _L0_attn_in['Wv'], 'L0_attn_Wg': _L0_attn_in['Wg'], 'L0_attn_Wo': _L0_attn_in['Wo'], 'L0_attn_q_gain': _L0_attn_in['q_gain'], 'L0_attn_lambda_param': _L0_attn_in['lambda_param'], 'L0_ffn_gate_w': _L0_ffn_in['gate_w'], 'L0_ffn_gate_b': _L0_ffn_in['gate_b'], 'L0_ffn_We1': _L0_ffn_in['We1'], 'L0_ffn_be1': _L0_ffn_in['be1'], 'L0_ffn_We2': _L0_ffn_in['We2'], 'L0_ffn_be2': _L0_ffn_in['be2'], 'L0_ffn_We3': _L0_ffn_in['We3'], 'L0_ffn_be3': _L0_ffn_in['be3'], 'L0_ffn_ws1': _L0_ffn_in['ws1'], 'L0_ffn_bs1': _L0_ffn_in['bs1'], 'L0_ffn_ws2': _L0_ffn_in['ws2'], 'L0_ffn_bs2': _L0_ffn_in['bs2'], 'L0_ffn_ws3': _L0_ffn_in['ws3'], 'L0_ffn_bs3': _L0_ffn_in['bs3']}
    _x0 = _d['L0_attn_x']
    _d['L0_attn_x'] = jax.random.normal(jax.random.fold_in(jax.random.key(seed), 1), (2, 2048, 256), dtype=_x0.dtype)
    del _x0
    return _d

def reference(L0_attn_x, L0_attn_Wq, L0_attn_Wk, L0_attn_Wv, L0_attn_Wg, L0_attn_Wo, L0_attn_q_gain, L0_attn_lambda_param, L0_ffn_gate_w, L0_ffn_gate_b, L0_ffn_We1, L0_ffn_be1, L0_ffn_We2, L0_ffn_be2, L0_ffn_We3, L0_ffn_be3, L0_ffn_ws1, L0_ffn_bs1, L0_ffn_ws2, L0_ffn_bs2, L0_ffn_ws3, L0_ffn_bs3):

    def _L0_attn_ref(x, Wq, Wk, Wv, Wg, Wo, q_gain, lambda_param):
        import jax, jax.numpy as jnp
        import numpy as np
        import math
        B, S, DIM = (1, 512, 256)
        H, KVH = (16, 4)
        HD = DIM // H
        KV_DIM = KVH * HD

        def _rms_norm(x):
            eps = jnp.finfo(x.dtype).eps
            return x * jax.lax.rsqrt(jnp.mean(x * x, axis=-1, keepdims=True) + eps)

        def _polar_rotary(seq_len, head_dim, dtype):
            angles = jnp.arange(0, head_dim, 2, dtype=jnp.float32) / head_dim * math.pi
            pos = jnp.arange(seq_len, dtype=jnp.float32)
            radius = 1.0 / (1.0 + pos[:, None] * 0.01)
            ang = pos[:, None] * angles[None, :]
            cos = (radius * jnp.cos(ang)).astype(dtype)
            sin = (radius * jnp.sin(ang)).astype(dtype)
            return (cos[None, None], sin[None, None])

        def _apply_rotary(x, cos, sin):
            half = x.shape[-1] // 2
            x1, x2 = (x[..., :half], x[..., half:])
            return jnp.concatenate([x1 * cos + x2 * sin, x1 * -sin + x2 * cos], axis=-1)

        def _causal_attn(q, k, v, scale, mask):
            s = jnp.einsum('bhqd,bhkd->bhqk', q, k) * scale
            s = jnp.where(mask, s, jnp.finfo(s.dtype).min)
            p = jax.nn.softmax(s, axis=-1)
            return jnp.einsum('bhqk,bhkd->bhqd', p, v)
        bsz, seqlen, dim = x.shape
        q = (x @ Wq.T).reshape(bsz, seqlen, H, HD).transpose(0, 2, 1, 3)
        k = (x @ Wk.T).reshape(bsz, seqlen, KVH, HD).transpose(0, 2, 1, 3)
        v = (x @ Wv.T).reshape(bsz, seqlen, KVH, HD).transpose(0, 2, 1, 3)
        v_g = jax.nn.sigmoid((x @ Wg.T).reshape(bsz, seqlen, KVH, HD).transpose(0, 2, 1, 3))
        v = v * v_g
        q = _rms_norm(q)
        k = _rms_norm(k)
        cos, sin = _polar_rotary(seqlen, HD, q.dtype)
        q = _apply_rotary(q, cos, sin)
        k = _apply_rotary(k, cos, sin)
        q = q * q_gain.astype(q.dtype)[None, :, None, None]
        rep = H // KVH
        k = jnp.repeat(k, rep, axis=1)
        v = jnp.repeat(v, rep, axis=1)
        half = HD // 2
        q1, q2 = (q[..., :half], q[..., half:])
        k1, k2 = (k[..., :half], k[..., half:])
        v1, v2 = (v[..., :half], v[..., half:])
        scale = 1.0 / math.sqrt(half)
        mask = jnp.tril(jnp.ones((seqlen, seqlen), dtype=bool))[None, None]
        a1 = _causal_attn(q1, k1, v1, scale, mask)
        a2 = _causal_attn(q2, k2, v2, scale, mask)
        lp = lambda_param.astype(q.dtype)[None, :, None, None]
        y = jnp.concatenate([a1 - lp * a2, a1 + lp * a2], axis=-1)
        y = y.transpose(0, 2, 1, 3).reshape(bsz, seqlen, dim)
        return y @ Wo.T

    def _L0_ffn_ref(x, gate_w, gate_b, We1, be1, We2, be2, We3, be3, ws1, bs1, ws2, bs2, ws3, bs3):
        import jax, jax.numpy as jnp
        import numpy as np
        DIM = 256
        E = 16
        TOPK = 2
        G = 4
        TOPK_G = 2
        INTER = 128
        N_SHARED = 2
        ROUTE_SCALE = 1.0

        def _gate(xf, gate_w, gate_b):
            scores = xf @ gate_w.T
            scores = jax.nn.softmax(scores.astype(jnp.float32), axis=-1)
            orig = scores
            scores = scores + gate_b
            T = xf.shape[0]
            sg = scores.reshape(T, G, E // G)
            group_scores = jax.lax.top_k(sg, 2)[0].sum(-1)
            _, gidx = jax.lax.top_k(group_scores, TOPK_G)
            keep = jax.nn.one_hot(gidx, G).sum(axis=1) > 0
            sg = jnp.where(keep[:, :, None], sg, -jnp.inf)
            scores = sg.reshape(T, E)
            _, idx = jax.lax.top_k(scores, TOPK)
            weights = jnp.take_along_axis(orig, idx, axis=1)
            weights = (weights * ROUTE_SCALE).astype(xf.dtype)
            return (weights, idx)
        shape = x.shape
        xf = x.reshape(-1, DIM)
        weights, idx = _gate(xf, gate_w, gate_b)
        combine = (jax.nn.one_hot(idx, E, dtype=xf.dtype) * weights[..., None]).sum(1)
        h1 = jnp.einsum('td,edi->tei', xf, We1) + be1
        h3 = jnp.einsum('td,edi->tei', xf, We3) + be3
        h = jax.nn.silu(h1) * h3
        yo = jnp.einsum('tei,eid->ted', h, We2) + be2
        y = jnp.einsum('te,ted->td', combine, yo)
        z = jax.nn.silu(xf @ ws1 + bs1) * (xf @ ws3 + bs3) @ ws2 + bs2
        return (y + z).reshape(shape)
    x = L0_attn_x
    x = x + _L0_attn_ref(_layernorm(x, axis=-1), L0_attn_Wq, L0_attn_Wk, L0_attn_Wv, L0_attn_Wg, L0_attn_Wo, L0_attn_q_gain, L0_attn_lambda_param)
    x = x + _L0_ffn_ref(_layernorm(x, axis=-1), L0_ffn_gate_w, L0_ffn_gate_b, L0_ffn_We1, L0_ffn_be1, L0_ffn_We2, L0_ffn_be2, L0_ffn_We3, L0_ffn_be3, L0_ffn_ws1, L0_ffn_bs1, L0_ffn_ws2, L0_ffn_bs2, L0_ffn_ws3, L0_ffn_bs3)
    return x

_drawn_inputs = setup_inputs


def setup_inputs(seed=0):
    import zlib

    import numpy as np

    out = dict(_drawn_inputs(seed))
    spreads = {'L0_attn_q_gain': (1.0, 0.6),
     'L0_attn_lambda_param': (0.5, 0.6),
     'L0_ffn_gate_b': (0.0, 0.1),
     'L0_ffn_be1': (0.0, 0.567),
     'L0_ffn_be2': (0.0, 0.353),
     'L0_ffn_be3': (0.0, 0.57),
     'L0_ffn_bs1': (0.0, 0.1),
     'L0_ffn_bs2': (0.0, 0.1),
     'L0_ffn_bs3': (0.0, 0.1)}
    factors = {'L0_attn_Wq': 8.0,
     'L0_attn_Wk': 8.0,
     'L0_attn_Wv': 8.0,
     'L0_attn_Wg': 8.0,
     'L0_attn_Wo': 8.0}
    for name, (base, spread) in spreads.items():
        noise = np.random.default_rng([zlib.crc32(name.encode()), seed]).standard_normal(out[name].shape)
        drawn = base * np.exp(spread * noise) if base else spread * noise
        out[name] = jnp.asarray(drawn.astype(out[name].dtype))
    for name, factor in factors.items():
        out[name] = (out[name] * factor).astype(out[name].dtype)
    return out
```

```python
from contextlib import ExitStack

import numpy as np

import concourse.bass as bass
from concourse import mybir

ALU = mybir.AluOpType
ACT = mybir.ActivationFunctionType
F32 = mybir.dt.float32
BF16 = mybir.dt.bfloat16
AX = mybir.AxisListType

P = 128
BATCH, SEQ, DIM = 2, 2048, 256
HEADS, KV_HEADS, HD = 16, 4, 16
REP = HEADS // KV_HEADS
HALF = HD // 2
TOKENS = BATCH * SEQ
TILES = TOKENS // P
BLK = 512
BT = BLK // P
BLOCKS = TOKENS // BLK
BPB = SEQ // BLK
DC = DIM // P
NORMED = HEADS + KV_HEADS
QK = NORMED * HD
KV = KV_HEADS * HD
COLS = QK + 2 * KV
PARTS = 3
ROWS = PARTS * PARTS * HALF
ROWSM = ROWS + PARTS
VC = 32
EXPERTS, GROUPS, INTER = 16, 4, 128
SHARED = 2
ALL_EXPERTS = EXPERTS + SHARED
LN_EPS = 1e-5
RMS_EPS = float(np.finfo(np.float32).eps)
SCALE = 1.0 / float(np.sqrt(HALF))
BIG = 1e30


def project(nc, w, X, V, psum, q_parts, k_parts):
    with ExitStack() as ctx:
        def sb(name, shape, dt=F32):
            return ctx.enter_context(nc.sbuf_tensor(name, shape, dt))

        def sem(name):
            return ctx.enter_context(nc.semaphore(name))

        wt = sb("p_wt", [P, DC, COLS])
        ident = sb("p_ident", [P, P])
        identb = sb("p_identb", [P, P], BF16)
        rot = sb("p_rot", [P, TILES, 2 * HD])
        gain = sb("p_gain", [P, HEADS])
        stats = sb("p_stats", [P, BT, 6])
        mv = sb("p_mv", [P, BT, 2])
        vare = sb("p_vare", [P, BT])
        std = sb("p_std", [P, BT])
        rstd = sb("p_rstd", [P, BT])
        xn = sb("p_xn", [P, BT, DIM])
        xnT = sb("p_xnT", [P, DC, BLK])
        sq = sb("p_sq", [P, BT, QK])
        ss = sb("p_ss", [P, BT * NORMED])
        sse = sb("p_sse", [P, BT * NORMED])
        rms = sb("p_rms", [P, BT * NORMED])
        rr = sb("p_rr", [P, BT, NORMED])
        sg = sb("p_sg", [P, BT, KV])
        qn = sb("p_qn", [P, BT, NORMED, HD])
        ra = sb("p_ra", [P, BT, NORMED, HD])
        rb = sb("p_rb", [P, BT, NORMED, HD])
        f = sb("p_f", [P, BT, QK])
        r = sb("p_r", [P, BT, QK])
        part = sb("p_part", [P, PARTS, BT, QK], BF16)
        outq = sb("p_outq", [P, PARTS, 2, BLK], BF16)
        outk = sb("p_outk", [KV, PARTS, BLK], BF16)

        waited = sem("p_waited")
        const_in, x_in, v_set = sem("p_const_in"), sem("p_x_in"), sem("p_v_set")
        var_rdy, std_rdy, xn_rdy = sem("p_var_rdy"), sem("p_std_rdy"), sem("p_xn_rdy")
        xT_rdy, xT_used, pj_rdy, pj_used = sem("p_xT_rdy"), sem("p_xT_used"), sem("p_pj_rdy"), sem("p_pj_used")
        sq_rdy, sg_rdy, ss_rdy, rms_rdy = sem("p_sq_rdy"), sem("p_sg_rdy"), sem("p_ss_rdy"), sem("p_rms_rdy")
        qn_rdy, rb_rdy, f_rdy, r_rdy = sem("p_qn_rdy"), sem("p_rb_rdy"), sem("p_f_rdy"), sem("p_r_rdy")
        hi_rdy, mid_rdy, lo_rdy = sem("p_hi_rdy"), sem("p_mid_rdy"), sem("p_lo_rdy")
        tr_rdy, tr_used, parts_out = sem("p_tr_rdy"), sem("p_tr_used"), sem("p_parts_out")
        dve_step = sem("p_dve_step")

        xT = psum[:, 0:2, :]
        pj = psum[:, 2:6, :]
        pj_qk = pj[:, :, 0:QK]
        trb = [psum[:, 6 + s, :].bitcast(BF16).rearrange("p (c n) -> p c n", c=2) for s in range(2)]
        x_dram = w["x"].rearrange("b (t p) d -> p (b t) d", p=P)
        CONSTS = 6
        DVE_STEPS = 7

        block = ctx.enter_context(nc.Block())

        @block.sync
        def _(sp):
            for dst, src in ((wt[:], w["w_qkvg"].rearrange("(c p) n -> p c n", p=P)), (ident[:], w["ident"]),
                             (identb[:], w["identb"]), (gain[:], w["q_gain"].partition_broadcast(P)),
                             (rot[:, 0:TILES // 2, :], w["rot"].rearrange("(t p) n -> p t n", p=P)),
                             (rot[:, TILES // 2:TILES, :], w["rot"].rearrange("(t p) n -> p t n", p=P))):
                sp.dma_start(dst, src).then_inc(const_in, 16)
            with sp.Fori(0, BLOCKS) as i:
                sp.dma_start(X[:, bass.ds(i * BT, BT), :], x_dram[:, bass.ds(i * BT, BT), :]).then_inc(x_in, 16)
                sp.wait_ge(x_in, i * 16 + 16)
                sp.sem_inc(waited, 1)
            sp.sem_inc(parts_out, 16)
            with sp.Fori(0, BATCH) as b:
                with sp.Fori(0, BPB) as j:
                    tok = bass.ds(j * BLK, BLK)
                    for p in range(PARTS):
                        done = b * (BPB * 6) + j * 6 + 2 * p
                        sp.wait_ge(tr_used, done + 3)
                        for c in range(2):
                            sp.dma_start(q_parts[bass.ds(b, 1), c * 16:(c + 1) * 16, p, :, tok],
                                         outq[:, p, c, :]).then_inc(parts_out, 16)
                        sp.wait_ge(tr_used, done + 4)
                        sp.dma_start(k_parts[bass.ds(b, 1), :, p, :, tok], outk[:, p]).then_inc(parts_out, 16)
            sp.wait_ge(parts_out, 16 + BLOCKS * PARTS * 3 * 16)

        @block.gpsimd
        def _(pool):
            v5 = V[:].rearrange("p (n c) -> p n c", c=VC)
            nc.gpsimd.memset(v5[:, :, 0:HALF], 0.0)
            nc.gpsimd.memset(v5[:, :, HALF:HALF + 1], 1.0)
            nc.gpsimd.memset(v5[:, :, HALF + 1:VC], 0.0).then_inc(v_set, 1)
            pool.wait_ge(const_in, 16 * CONSTS)
            with pool.Fori(0, BLOCKS) as i:
                pool.wait_ge(qn_rdy, i + 1)
                for h, o in ((0, 1), (1, 0)):
                    last = nc.gpsimd.tensor_tensor(
                        rb[:, :, :, h * HALF:(h + 1) * HALF], qn[:, :, :, o * HALF:(o + 1) * HALF],
                        rot[:, bass.ds(i * BT, BT), None, HD + h * HALF:HD + (h + 1) * HALF]
                        .to_broadcast([P, BT, NORMED, HALF]), ALU.mult)
                last.then_inc(rb_rdy, 1)

        @block.scalar
        def _(act):
            act.sem_inc(tr_used, 2)
            with act.Fori(0, BLOCKS) as i:
                act.wait_ge(var_rdy, i + 1)
                nc.scalar.activation(std[:], vare[:], ACT.Sqrt).then_inc(std_rdy, 1)
                act.wait_ge(xT_rdy, i + 2)
                act.wait_ge(pj_rdy, i + 1)
                nc.scalar.copy(xnT[:], xT).then_inc(xT_used, 1)
                act.wait_ge(pj_rdy, i + 2)
                nc.scalar.activation(sq[:], pj_qk, ACT.Square).then_inc(sq_rdy, 1)
                nc.scalar.activation(sg[:], pj[:, :, QK + KV:COLS], ACT.Sigmoid).then_inc(sg_rdy, 1)
                act.wait_ge(ss_rdy, i + 1)
                nc.scalar.activation(rms[:], sse[:], ACT.Sqrt).then_inc(rms_rdy, 1)
                act.wait_ge(f_rdy, i + 1)
                act.wait_ge(tr_rdy, i * 6 + 1)
                nc.scalar.copy(part[:, 0], f[:]).then_inc(hi_rdy, 1)
                act.wait_ge(r_rdy, i + 1)
                nc.scalar.copy(part[:, 1], r[:]).then_inc(mid_rdy, 1)
                act.wait_ge(parts_out, i * 144 + 16)
                for p in range(PARTS):
                    act.wait_ge(tr_rdy, i * 6 + 2 * p + 2)
                    nc.scalar.copy(outq[:, p], trb[0]).then_inc(tr_used, 1)
                    act.wait_ge(tr_rdy, i * 6 + 2 * p + 3)
                    nc.scalar.copy(outk[:, p], trb[1][0:KV, 0, :]).then_inc(tr_used, 1)

        @block.vector
        def _(dve):
            dve.sem_inc(pj_used, 1)
            dve.wait_ge(const_in, 16 * CONSTS)
            dve.wait_ge(v_set, 1)
            with dve.Fori(0, BLOCKS) as i:
                steps = [0]

                def then(ins):
                    steps[0] += 1
                    ins.then_inc(dve_step, 1)
                    dve.wait_ge(dve_step, i * DVE_STEPS + steps[0])

                dve.wait_ge(x_in, i * 16 + 16)
                dve.sem_inc(waited, 1)
                for t in range(BT):
                    last = nc.vector.bn_stats(stats[:, t, :], X[:, bass.ds(i * BT + t, 1), :])
                then(last)
                dve.sem_inc(waited, 1)
                for t in range(BT):
                    last = nc.vector.bn_aggr(mv[:, t, :], stats[:, t, :])
                then(last)
                nc.vector.tensor_scalar(vare[:], mv[:, :, 1], LN_EPS, None, ALU.add).then_inc(var_rdy, 1)
                dve.wait_ge(std_rdy, i + 1)
                then(nc.vector.reciprocal(rstd[:], std[:]))
                dve.wait_ge(xT_rdy, i + 1)
                for t in range(BT):
                    last = nc.vector.tensor_scalar(xn[:, t, :], X[:, bass.ds(i * BT + t, 1), :], mv[:, t, 0:1],
                                                   rstd[:, t:t + 1], ALU.subtract, ALU.mult)
                last.then_inc(xn_rdy, 1)
                dve.wait_ge(sq_rdy, i + 1)
                then(nc.vector.tensor_reduce(ss[:], sq[:].rearrange("p t (h d) -> p (t h) d", d=HD), AX.X, ALU.add))
                nc.vector.tensor_scalar(sse[:], ss[:], 1.0 / HD, RMS_EPS, ALU.mult, ALU.add).then_inc(ss_rdy, 1)
                dve.wait_ge(rms_rdy, i + 1)
                then(nc.vector.reciprocal(rr[:].rearrange("p t h -> p (t h)"), rms[:]))
                then(nc.vector.tensor_tensor(rr[:, :, 0:HEADS], rr[:, :, 0:HEADS],
                                             gain[:, None, :].to_broadcast([P, BT, HEADS]), ALU.mult))
                dve.wait_ge(sg_rdy, i + 1)
                nc.vector.tensor_tensor(qn[:], pj_qk.rearrange("p t (h d) -> p t h d", d=HD),
                                        rr[:, :, :, None].to_broadcast([P, BT, NORMED, HD]),
                                        ALU.mult).then_inc(qn_rdy, 1)
                for t in range(BT):
                    last = nc.vector.tensor_tensor(
                        V[:, bass.ds((i * BT + t) * 2 * KV_HEADS * VC, 2 * KV_HEADS * VC)]
                        .rearrange("p (n c) -> p n c", c=VC)[:, :, 0:HALF],
                        pj[:, t, QK:QK + KV].rearrange("p (n c) -> p n c", c=HALF),
                        sg[:, t, :].rearrange("p (n c) -> p n c", c=HALF), ALU.mult)
                last.then_inc(pj_used, 1)
                dve.wait_ge(qn_rdy, i + 1)
                then(nc.vector.tensor_tensor(
                    ra[:], qn[:], rot[:, bass.ds(i * BT, BT), None, 0:HD].to_broadcast([P, BT, NORMED, HD]), ALU.mult))
                dve.wait_ge(rb_rdy, i + 1)
                nc.vector.tensor_tensor(f[:], ra[:].rearrange("p t h d -> p t (h d)"),
                                        rb[:].rearrange("p t h d -> p t (h d)"), ALU.add).then_inc(f_rdy, 1)
                dve.wait_ge(hi_rdy, i + 1)
                nc.vector.tensor_tensor(r[:], f[:], part[:, 0], ALU.subtract).then_inc(r_rdy, 1)
                dve.wait_ge(mid_rdy, i + 1)
                nc.vector.tensor_tensor(part[:, 2], r[:], part[:, 1], ALU.subtract).then_inc(lo_rdy, 1)
                assert steps[0] == DVE_STEPS, steps

        @block.tensor
        def _(pe):
            pe.sem_inc(xT_rdy, 1)
            pe.sem_inc(pj_rdy, 1)
            pe.sem_inc(tr_rdy, 1)
            pe.wait_ge(const_in, 16 * CONSTS)
            with pe.Fori(0, BLOCKS) as i:
                pe.wait_ge(xn_rdy, i + 1)
                for t in range(BT):
                    for c in range(DC):
                        last = nc.tensor.transpose(xT[:, c, t * P:(t + 1) * P], xn[:, t, c * P:(c + 1) * P], ident[:])
                last.then_inc(xT_rdy, 1)
                pe.wait_ge(xT_used, i + 1)
                pe.wait_ge(pj_used, i + 1)
                for t in range(BT):
                    for c in range(DC):
                        last = nc.tensor.matmul(pj[:, t, 0:COLS], xnT[:, c, t * P:(t + 1) * P], wt[:, c, :],
                                                start=(c == 0), stop=(c == DC - 1))
                last.then_inc(pj_rdy, 1)
                for p, ready in enumerate((hi_rdy, mid_rdy, lo_rdy)):
                    pe.wait_ge(ready, i + 1)
                    for g in range(2):
                        pe.wait_ge(tr_used, i * 6 + 2 * p + g + 1)
                        pe.sem_inc(waited, 1)
                        for c in range(2 if g == 0 else 1):
                            for t in range(BT):
                                cols = (c * P, (c + 1) * P) if g == 0 else (HEADS * HD, QK)
                                last = nc.tensor.transpose(trb[g][0:cols[1] - cols[0], c, t * P:(t + 1) * P],
                                                           part[:, p, t, cols[0]:cols[1]], identb[:])
                        last.then_inc(tr_rdy, 1)

def attend(nc, w, V, Y, psum, q_parts, k_parts):
    with ExitStack() as ctx:
        def sb(name, shape, dt=F32):
            return ctx.enter_context(nc.sbuf_tensor(name, shape, dt))

        def sem(name):
            return ctx.enter_context(nc.semaphore(name))

        QT = SEQ // P
        NQ = SEQ // BLK
        RUNS = BATCH * KV_HEADS
        PAIRS = REP // 2
        S_BUFS, P_BUFS = 3, 4
        units = [(J, i) for J in range(NQ) for i in range((J + 1) * BT)]
        UNITS = len(units)
        last_unit = [max(t for t, (j, _) in enumerate(units) if j == J) for J in range(NQ)]
        MAXES = REP * QT

        ident = sb("a_ident", [P, P])
        identb = sb("a_identb", [P, P], BF16)
        mask = sb("a_mask", [P, P], BF16)
        lam = sb("a_lam", [P, HEADS])
        qrows = [sb(f"a_qrows{h}", [ROWSM, REP, SEQ], BF16) for h in range(2)]
        krows = [sb(f"a_krows{h}", [ROWSM, SEQ], BF16) for h in range(2)]
        vals = [sb(f"a_vals{h}", [P, QT, VC]) for h in range(2)]
        probs = sb("a_probs", [P, P_BUFS, 2, BLK])
        negmax = sb("a_negmax", [P, MAXES])
        rest = sb("a_rest", [P, MAXES])
        maxpart = sb("a_maxpart", [P, PARTS, MAXES], BF16)
        maxT = sb("a_maxT", [MAXES, PARTS, P], BF16)
        outT = sb("a_outT", [P, 2, BLK])
        inv = sb("a_inv", [P, BT, REP])
        invl = sb("a_invl", [P, BT, REP])
        a1 = sb("a_a1", [P, QT, REP, HALF])
        a2 = sb("a_a2", [P, BT, REP, HALF])

        waited = sem("a_waited")
        const_in = sem("a_const_in")
        rows_in = [sem(f"a_rows_in{h}") for h in range(2)]
        max_in = [sem(f"a_max_in{h}") for h in range(2)]
        step_done = [sem(f"a_step_done{h}") for h in range(2)]
        vals_rdy = sem("a_vals_rdy")
        mx_rdy, mx_used = sem("a_mx_rdy"), sem("a_mx_used")
        mp_rdy, mt_rdy, mt_sb = sem("a_mp_rdy"), sem("a_mt_rdy"), sem("a_mt_sb")
        s_rdy, exp_rdy, av_done = sem("a_s_rdy"), sem("a_exp_rdy"), sem("a_av_done")
        ot_rdy, tm_rdy, tm_used = sem("a_ot_rdy"), sem("a_tm_rdy"), sem("a_tm_used")
        dve_step = sem("a_dve_step")
        CONSTS = 6

        q_src = q_parts.rearrange("b (k r h) p d s -> (b k) h (p d) r s", k=KV_HEADS, h=2)
        k_src = k_parts.rearrange("b (k h) p d s -> (b k) h p d s", h=2)
        V4 = V[:].rearrange("p (t n c) -> p t n c", n=2 * KV_HEADS, c=VC)

        block = ctx.enter_context(nc.Block())

        @block.sync
        def _(sp):
            ones = w["ones_rows"]
            for dst, src in ((ident[:], w["ident"]), (identb[:], w["identb"]), (mask[:], w["mask"]),
                             (lam[:], w["lam"].partition_broadcast(P)),
                             (krows[0][ROWS:ROWSM, :], ones[:, 0:SEQ]), (krows[1][ROWS:ROWSM, :], ones[:, SEQ:])):
                sp.dma_start(dst, src).then_inc(const_in, 16)
            for h in range(2):
                sp.sem_inc(step_done[h], 1)
            with sp.Fori(0, RUNS) as n:
                for h in range(2):
                    sp.wait_ge(step_done[h], n + 1)
                    for a in range(PARTS):
                        rows = slice(a * PARTS * HALF, (a + 1) * PARTS * HALF)
                        sp.dma_start(qrows[h][rows, :, :], q_src[bass.ds(n, 1), h]).then_inc(rows_in[h], 16)
                        for p in range(PARTS):
                            row = (a * PARTS + p) * HALF
                            sp.dma_start(krows[h][row:row + HALF, :], k_src[bass.ds(n, 1), h, a, :, :]
                                         ).then_inc(rows_in[h], 16)

        @block.gpsimd
        def _(pool):
            with pool.Fori(0, BATCH) as b:
                with pool.Fori(0, KV_HEADS) as k:
                    for h in range(2):
                        pool.wait_ge(step_done[h], b * KV_HEADS + k + 1)
                        nc.gpsimd.tensor_copy(
                            vals[h][:], V4[:, bass.ds(b * QT, QT), bass.ds(k * 2 + h, 1), :]).then_inc(vals_rdy, 1)

        @block.scalar
        def _(act):
            with act.Fori(0, RUNS) as n:
                for h in range(2):
                    step = n * 2 + h
                    act.wait_ge(mt_rdy, step + 1)
                    nc.scalar.copy(maxT[:], psum[0:MAXES, 0, 0:PARTS * P // 2].bitcast(BF16)
                                   .rearrange("m (a q) -> m a q", a=PARTS)).then_inc(mt_sb, 1)
                    act.wait_ge(mt_sb, step + 1)
                    for a in range(PARTS):
                        act.dma_start(qrows[h][ROWS + a:ROWS + a + 1, :, :], maxT[:, a, :]).then_inc(max_in[h], 16)
                    for t, (J, i) in enumerate(units):
                        N = BLK - max(0, i - J * BT) * P
                        act.wait_ge(av_done, step * UNITS + t + 1)
                        for g in range(PAIRS):
                            u = t * PAIRS + g
                            sb_ = (u % S_BUFS) * 2
                            act.wait_ge(s_rdy, step * UNITS * PAIRS + u + 1)
                            nc.scalar.activation(probs[:, u % P_BUFS, :, 0:N], psum[:, sb_:sb_ + 2, 0:N],
                                                 ACT.Exp, scale=SCALE).then_inc(exp_rdy, 1)

        @block.vector
        def _(dve):
            dve.sem_inc(mx_used, 2)
            dve.sem_inc(tm_used, 2)
            dve.wait_ge(const_in, 16 * CONSTS)
            DVE_STEPS = [3 + NQ, 3 + 3 * NQ]
            with dve.Fori(0, BATCH) as b, dve.Fori(0, KV_HEADS) as k:
                for h in range(2):
                    step = b * (KV_HEADS * 2) + k * 2 + h
                    steps = [0]

                    def then(ins):
                        steps[0] += 1
                        ins.then_inc(dve_step, 1)
                        dve.wait_ge(dve_step, (b * KV_HEADS + k) * sum(DVE_STEPS)
                                    + (DVE_STEPS[0] if h else 0) + steps[0])

                    for m in range(MAXES):
                        q = m % QT
                        dve.wait_ge(mx_rdy, step * MAXES + m + 1)
                        last = nc.vector.tensor_reduce(
                            negmax[:, m:m + 1],
                            psum[:, (m % 2) * 4:(m % 2) * 4 + 4, :].rearrange("p b n -> p (b n)")[:, 0:(q + 1) * P],
                            AX.X, ALU.max, negate=True)
                        last.then_inc(mx_used, 1)
                    dve.wait_ge(mx_used, (step + 1) * MAXES + 2)
                    then(nc.vector.tensor_copy(maxpart[:, 0, :], negmax[:]))
                    then(nc.vector.tensor_tensor(rest[:], negmax[:], maxpart[:, 0, :], ALU.subtract))
                    then(nc.vector.tensor_copy(maxpart[:, 1, :], rest[:]))
                    nc.vector.tensor_tensor(maxpart[:, 2, :], rest[:], maxpart[:, 1, :],
                                            ALU.subtract).then_inc(mp_rdy, 1)
                    for J in range(NQ):
                        bank = 6 + J % 2
                        dve.wait_ge(av_done, step * UNITS + last_unit[J] + 3)
                        nc.vector.tensor_copy(outT[:, J % 2, :], psum[:, bank, :]).then_inc(ot_rdy, 1)
                        tok = psum[:, bank, :].rearrange("p (q h c) -> p q h c", h=REP, c=VC)
                        dve.wait_ge(tm_rdy, step * NQ + J + 1)
                        then(nc.vector.reciprocal(inv[:], tok[:, :, :, HALF]))
                        if h == 0:
                            nc.vector.tensor_tensor(a1[:, J * BT:(J + 1) * BT], tok[:, :, :, 0:HALF],
                                                    inv[:, :, :, None].to_broadcast([P, BT, REP, HALF]),
                                                    ALU.mult).then_inc(tm_used, 1)
                            continue
                        then(nc.vector.tensor_tensor(
                            invl[:], inv[:], lam[:, None, bass.ds(k * REP, REP)].to_broadcast([P, BT, REP]), ALU.mult))
                        ins = nc.vector.tensor_tensor(a2[:], tok[:, :, :, 0:HALF],
                                                      invl[:, :, :, None].to_broadcast([P, BT, REP, HALF]), ALU.mult)
                        ins.then_inc(tm_used, 1)
                        dve.wait_ge(tm_used, step * NQ + J + 3)
                        y = Y[:, bass.ds(b * QT + J * BT, BT), bass.ds(k * KV, KV)] \
                            .rearrange("p t (h c) -> p t h c", c=HD)
                        nc.vector.tensor_tensor(y[:, :, :, 0:HALF], a1[:, J * BT:(J + 1) * BT], a2[:], ALU.subtract)
                        then(nc.vector.tensor_tensor(y[:, :, :, HALF:HD], a1[:, J * BT:(J + 1) * BT], a2[:], ALU.add))
                    assert steps[0] == DVE_STEPS[h], steps

        @block.tensor
        def _(pe):
            pe.sem_inc(exp_rdy, 3)
            pe.sem_inc(av_done, 2)
            pe.wait_ge(const_in, 16 * CONSTS)
            with pe.Fori(0, RUNS) as n:
                for h in range(2):
                    step = n * 2 + h
                    qr, kr = qrows[h], krows[h]

                    pe.wait_ge(rows_in[h], (n + 1) * (PARTS + PARTS * PARTS) * 16)
                    pe.wait_ge(tm_used, step * NQ + 2)
                    for m in range(MAXES):
                        head, q = divmod(m, QT)
                        pe.wait_ge(mx_used, step * MAXES + m + 1)
                        for c in range(0, (q + 1) * P, BLK):
                            N = min(BLK, (q + 1) * P - c)
                            diag = c + N == (q + 1) * P
                            out = psum[:, (m % 2) * 4 + c // BLK, :]
                            last = nc.tensor.matmul(out[:, 0:N], qr[0:ROWS, head, q * P:(q + 1) * P],
                                                    kr[0:ROWS, c:c + N], start=True, stop=not diag)
                            if diag:
                                last = nc.tensor.matmul(out[:, N - P:N], identb[:], mask[:], start=False, stop=True)
                        last.then_inc(mx_rdy, 1)
                    pe.wait_ge(mp_rdy, step + 1)
                    pe.sem_inc(waited, 1)
                    maxt = psum[0:MAXES, 0, 0:PARTS * P // 2].bitcast(BF16).rearrange("m (a q) -> m a q", a=PARTS)
                    for a in range(PARTS):
                        last = nc.tensor.transpose(maxt[:, a, :], maxpart[:, a, :], identb[:])
                    last.then_inc(mt_rdy, 1)
                    pe.wait_ge(max_in[h], (n + 1) * 48)
                    pe.wait_ge(vals_rdy, step + 1)

                    def scores(t):
                        J, i = units[t]
                        lo = max(0, i - J * BT) * P
                        for g in range(PAIRS):
                            u = t * PAIRS + g
                            pe.wait_ge(exp_rdy, step * UNITS * PAIRS + u + 1)
                            for e in range(2):
                                out = psum[:, (u % S_BUFS) * 2 + e, :]
                                last = nc.tensor.matmul(out[:, 0:BLK - lo], kr[:, i * P:(i + 1) * P],
                                                        qr[:, g * 2 + e, J * BLK + lo:(J + 1) * BLK],
                                                        start=True, stop=i < J * BT)
                                if i >= J * BT:
                                    last = nc.tensor.matmul(out[:, 0:P], mask[:], identb[:], start=False, stop=True)
                            last.then_inc(s_rdy, 1)

                    def values(t):
                        J, i = units[t]
                        lo = max(0, i - J * BT) * P
                        if i == 0:
                            pe.wait_ge(tm_used, step * NQ + J + 1)
                        pe.wait_ge(exp_rdy, step * UNITS * PAIRS + t * PAIRS + PAIRS + 3)
                        for head in range(REP):
                            u = t * PAIRS + head // 2
                            last = nc.tensor.matmul(psum[head * VC:(head + 1) * VC, 6 + J % 2, lo:BLK],
                                                    vals[h][:, i, :], probs[:, u % P_BUFS, head % 2, 0:BLK - lo],
                                                    start=(i == 0), stop=(i == (J + 1) * BT - 1))
                        last.then_inc(av_done, 1)
                        return last

                    def turn(J):
                        pe.wait_ge(ot_rdy, step * NQ + J + 1)
                        for q in range(BT):
                            last = nc.tensor.transpose(psum[:, 6 + J % 2, q * P:(q + 1) * P],
                                                       outT[:, J % 2, q * P:(q + 1) * P], ident[:])
                        last.then_inc(tm_rdy, 1)

                    for t in range(UNITS + 1):
                        if t < UNITS:
                            scores(t)
                        if t > 0:
                            values(t - 1)
                        for J in range(NQ - 1):
                            if t == last_unit[J] + 3:
                                turn(J)
                    turn(NQ - 1)
                    pe.wait_ge(av_done, (step + 1) * UNITS + 2)
                    pe.sem_inc(step_done[h], 1)


def finish(nc, w, Y, X, XT, logits, psum):
    with ExitStack() as ctx:
        def sb(name, shape, dt=F32):
            return ctx.enter_context(nc.sbuf_tensor(name, shape, dt))

        def sem(name):
            return ctx.enter_context(nc.semaphore(name))

        wo = sb("f_wo", [P, DC, DIM])
        gw = sb("f_gw", [P, DC, EXPERTS])
        ident = sb("f_ident", [P, P])
        y = sb("f_y", [P, BT, DIM])
        yT = sb("f_yT", [P, DC, BLK])
        stats = sb("f_stats", [P, BT, 6])
        mv = sb("f_mv", [P, BT, 2])
        vare = sb("f_vare", [P, BT])
        std = sb("f_std", [P, BT])
        rstd = sb("f_rstd", [P, BT])
        xn = sb("f_xn", [P, BT, DIM])
        xT = sb("f_xT", [P, DC, BLK])

        waited = sem("f_waited")
        const_in, x_in = sem("f_const_in"), sem("f_x_in")
        y_rdy, yT_rdy, yT_sb, o_rdy, res_rdy = (sem("f_" + n) for n in ("y_rdy", "yT_rdy", "yT_sb", "o_rdy", "res_rdy"))
        var_rdy, std_rdy, xn_rdy, xT_rdy, xT_sb = (
            sem("f_" + n) for n in ("var_rdy", "std_rdy", "xn_rdy", "xT_rdy", "xT_sb"))
        xT_kept, lg_rdy, lg_used, dve_step = (sem("f_" + n) for n in ("xT_kept", "lg_rdy", "lg_used", "dve_step"))
        DVE_STEPS = 3
        CONSTS = 3
        x_dram = w["x"].rearrange("b (t p) d -> p (b t) d", p=P)
        proj = psum[:, 2:4, :].rearrange("p b (t d) -> p (b t) d", d=DIM)
        lg = psum[:, 6, 0:BT * EXPERTS].rearrange("p (t e) -> p t e", e=EXPERTS)

        block = ctx.enter_context(nc.Block())

        @block.sync
        def _(sp):
            for dst, src in ((wo[:], w["w_o"].rearrange("(c p) n -> p c n", p=P)), (ident[:], w["ident"]),
                             (gw[:], w["gate_w"].rearrange("(c p) n -> p c n", p=P))):
                sp.dma_start(dst, src).then_inc(const_in, 16)
            with sp.Fori(0, BLOCKS) as i:
                sp.dma_start(X[:, bass.ds(i * BT, BT), :], x_dram[:, bass.ds(i * BT, BT), :]).then_inc(x_in, 16)
                sp.wait_ge(x_in, i * 16 + 16)
                sp.sem_inc(waited, 1)

        @block.gpsimd
        def _(pool):
            with pool.Fori(0, BLOCKS) as i:
                pool.wait_ge(xT_sb, i + 1)
                nc.gpsimd.tensor_copy(XT[:, :, bass.ds(i * BLK, BLK)], xT[:]).then_inc(xT_kept, 1)

        @block.scalar
        def _(act):
            act.sem_inc(xT_kept, 1)
            act.sem_inc(lg_rdy, 1)
            with act.Fori(0, BLOCKS) as i:
                act.wait_ge(yT_rdy, i + 1)
                nc.scalar.copy(y[:], Y[:, bass.ds(i * BT, BT), :]).then_inc(y_rdy, 1)
                act.wait_ge(yT_rdy, i + 2)
                nc.scalar.copy(yT[:], psum[:, 0:2, :]).then_inc(yT_sb, 1)
                act.wait_ge(var_rdy, i + 1)
                nc.scalar.activation(std[:], vare[:], ACT.Sqrt).then_inc(std_rdy, 1)
                act.wait_ge(xT_rdy, i + 2)
                act.wait_ge(xT_kept, i + 1)
                act.wait_ge(lg_rdy, i + 1)
                nc.scalar.copy(xT[:], psum[:, 4:6, :]).then_inc(xT_sb, 1)

        @block.vector
        def _(dve):
            dve.sem_inc(lg_used, 1)
            with dve.Fori(0, BLOCKS) as i:
                steps = [0]

                def then(ins):
                    steps[0] += 1
                    ins.then_inc(dve_step, 1)
                    dve.wait_ge(dve_step, i * DVE_STEPS + steps[0])

                dve.wait_ge(x_in, i * 16 + 16)
                dve.wait_ge(o_rdy, i + 2)
                nc.vector.tensor_tensor(X[:, bass.ds(i * BT, BT), :], X[:, bass.ds(i * BT, BT), :], proj,
                                        ALU.add).then_inc(res_rdy, 1)
                dve.wait_ge(res_rdy, i + 1)
                dve.sem_inc(waited, 1)
                for t in range(BT):
                    last = nc.vector.bn_stats(stats[:, t, :], X[:, bass.ds(i * BT + t, 1), :])
                then(last)
                dve.sem_inc(waited, 1)
                for t in range(BT):
                    last = nc.vector.bn_aggr(mv[:, t, :], stats[:, t, :])
                then(last)
                nc.vector.tensor_scalar(vare[:], mv[:, :, 1], LN_EPS, None, ALU.add).then_inc(var_rdy, 1)
                dve.wait_ge(std_rdy, i + 1)
                then(nc.vector.reciprocal(rstd[:], std[:]))
                dve.wait_ge(xT_rdy, i + 1)
                for t in range(BT):
                    last = nc.vector.tensor_scalar(xn[:, t, :], X[:, bass.ds(i * BT + t, 1), :], mv[:, t, 0:1],
                                                   rstd[:, t:t + 1], ALU.subtract, ALU.mult)
                last.then_inc(xn_rdy, 1)
                dve.wait_ge(lg_rdy, i + 2)
                nc.vector.tensor_copy(logits[:, bass.ds(i * BT, BT), :], lg).then_inc(lg_used, 1)
                assert steps[0] == DVE_STEPS, steps

        @block.tensor
        def _(pe):
            pe.sem_inc(yT_rdy, 1)
            pe.sem_inc(xT_rdy, 1)
            pe.sem_inc(o_rdy, 1)
            pe.wait_ge(const_in, 16 * CONSTS)
            with pe.Fori(0, BLOCKS) as i:
                pe.wait_ge(y_rdy, i + 1)
                for t in range(BT):
                    for c in range(DC):
                        last = nc.tensor.transpose(psum[:, c, t * P:(t + 1) * P], y[:, t, c * P:(c + 1) * P], ident[:])
                last.then_inc(yT_rdy, 1)
                pe.wait_ge(yT_sb, i + 1)
                for t in range(BT):
                    for c in range(DC):
                        last = nc.tensor.matmul(proj[:, t, :], yT[:, c, t * P:(t + 1) * P], wo[:, c, :],
                                                start=(c == 0), stop=(c == DC - 1))
                last.then_inc(o_rdy, 1)
                pe.wait_ge(xn_rdy, i + 1)
                for t in range(BT):
                    for c in range(DC):
                        last = nc.tensor.transpose(psum[:, 4 + c, t * P:(t + 1) * P], xn[:, t, c * P:(c + 1) * P],
                                                   ident[:])
                last.then_inc(xT_rdy, 1)
                pe.wait_ge(xT_sb, i + 1)
                pe.wait_ge(lg_used, i + 1)
                for t in range(BT):
                    for c in range(DC):
                        last = nc.tensor.matmul(lg[:, t, :], xT[:, c, t * P:(t + 1) * P], gw[:, c, :],
                                                start=(c == 0), stop=(c == DC - 1))
                last.then_inc(lg_rdy, 1)


def route(nc, w, logits, combT, combTf, psum):
    with ExitStack() as ctx:
        def sb(name, shape, dt=F32):
            return ctx.enter_context(nc.sbuf_tensor(name, shape, dt))

        def sem(name):
            return ctx.enter_context(nc.semaphore(name))

        PG = EXPERTS // GROUPS
        LOW = -3e38
        ident = sb("r_ident", [P, P])
        identb = sb("r_identb", [P, P], BF16)
        bias = sb("r_bias", [P, EXPERTS])
        before = sb("r_before", [P, GROUPS * GROUPS])
        order = sb("r_order", [P, EXPERTS])
        mx = sb("r_mx", [P, TILES])
        ex = sb("r_ex", [P, TILES, EXPERTS])
        tot = sb("r_tot", [P, TILES])
        orig = sb("r_orig", [P, TILES, EXPERTS])
        sc = sb("r_sc", [P, TILES, EXPERTS])
        hi = sb("r_hi", [P, TILES, GROUPS, 2])
        lo = sb("r_lo", [P, TILES, GROUPS, 2])
        top = sb("r_top", [P, TILES, GROUPS])
        sec = sb("r_sec", [P, TILES, GROUPS])
        sec2 = sb("r_sec2", [P, TILES, GROUPS])
        beat = sb("r_beat", [P, TILES, GROUPS, GROUPS])
        tie = sb("r_tie", [P, TILES, GROUPS, GROUPS])
        rank = sb("r_rank", [P, TILES, GROUPS])
        keep = sb("r_keep", [P, TILES, GROUPS])
        low = sb("r_low", [P, TILES, GROUPS])
        one = [sb(f"r_one{n}", [P, TILES, EXPERTS]) for n in range(2)]
        pos = sb("r_pos", [P, TILES, EXPERTS])
        comb = sb("r_comb", [P, TILES, EXPERTS + 1])
        rest = sb("r_rest", [P, TILES, EXPERTS])
        part = sb("r_part", [P, TILES, PARTS * EXPERTS], BF16)
        const_in, ex_in, ex_rdy, comb_rdy, part_rdy = (
            sem("r_" + n) for n in ("const_in", "ex_in", "ex_rdy", "comb_rdy", "part_rdy"))
        tr_rdy, tr_used, dve_step = sem("r_tr_rdy"), sem("r_tr_used"), sem("r_dve_step")
        CONSTS = 5
        all16 = [P, TILES, EXPERTS]
        GT = TILES // 8

        block = ctx.enter_context(nc.Block())

        @block.sync
        def _(sp):
            for dst, src in ((ident[:], w["ident"]), (identb[:], w["identb"]),
                             (bias[:], w["gate_b"].partition_broadcast(P)),
                             (before[:], w["before"].partition_broadcast(P)),
                             (order[:], w["order"].partition_broadcast(P))):
                sp.dma_start(dst, src).then_inc(const_in, 16)

        @block.scalar
        def _(act):
            act.wait_ge(ex_in, 1)
            nc.scalar.activation(ex[:], ex[:], ACT.Exp).then_inc(ex_rdy, 1)
            for n in range(8):
                act.wait_ge(tr_rdy, n + 1)
                nc.scalar.copy(combTf[0:EXPERTS + 1, n * BLK:(n + 1) * BLK],
                               psum[0:EXPERTS + 1, n, :]).then_inc(tr_used, 1)
            for n in range(4):
                act.wait_ge(tr_rdy, 9 + n)
                nc.scalar.copy(combT[0:PARTS * EXPERTS, n * 2 * BLK:(n + 1) * 2 * BLK],
                               psum[0:PARTS * EXPERTS, n, :].bitcast(BF16)).then_inc(tr_used, 1)

        @block.vector
        def _(dve):
            count = [0]

            def then(ins):
                count[0] += 1
                ins.then_inc(dve_step, 1)
                dve.wait_ge(dve_step, count[0])

            tt, red = nc.vector.tensor_tensor, nc.vector.tensor_reduce
            dve.wait_ge(const_in, 16 * CONSTS)
            then(red(mx[:], logits[:], AX.X, ALU.max))
            tt(ex[:], logits[:], mx[:, :, None].to_broadcast(all16), ALU.subtract).then_inc(ex_in, 1)
            dve.wait_ge(ex_rdy, 1)
            then(red(tot[:], ex[:], AX.X, ALU.add))
            then(nc.vector.reciprocal(tot[:], tot[:]))
            then(tt(orig[:], ex[:], tot[:, :, None].to_broadcast(all16), ALU.mult))
            then(tt(sc[:], orig[:], bias[:, None, :].to_broadcast(all16), ALU.add))
            s4 = sc[:].rearrange("p t (g e) -> p (t g) e", e=PG)
            pair = "p t g e -> p (t g) e"
            tt(hi[:].rearrange(pair), s4[:, :, 0:2], s4[:, :, 2:4], ALU.max)
            then(tt(lo[:].rearrange(pair), s4[:, :, 0:2], s4[:, :, 2:4], ALU.min))
            tt(top[:], hi[:, :, :, 0], hi[:, :, :, 1], ALU.max)
            tt(sec[:], hi[:, :, :, 0], hi[:, :, :, 1], ALU.min)
            then(tt(sec2[:], lo[:, :, :, 0], lo[:, :, :, 1], ALU.max))
            then(tt(sec[:], sec[:], sec2[:], ALU.max))
            then(tt(top[:], top[:], sec[:], ALU.add))
            grid = [P, TILES, GROUPS, GROUPS]
            mine, other = top[:, :, :, None].to_broadcast(grid), top[:, :, None, :].to_broadcast(grid)
            tt(beat[:], other, mine, ALU.is_gt)
            then(tt(tie[:], other, mine, ALU.is_equal))
            flat = "p t g h -> p t (g h)"
            then(tt(tie[:].rearrange(flat), tie[:].rearrange(flat),
                    before[:, None, :].to_broadcast([P, TILES, GROUPS * GROUPS]), ALU.mult))
            then(tt(beat[:], beat[:], tie[:], ALU.add))
            then(red(rank[:], beat[:], AX.X, ALU.add))
            then(nc.vector.tensor_scalar(keep[:], rank[:], 2.0, None, ALU.is_lt))
            then(nc.vector.tensor_scalar(low[:], keep[:], -LOW, LOW, ALU.mult, ALU.add))
            grid = [P, TILES, GROUPS, PG]
            s5 = sc[:].rearrange("p t (g e) -> p t g e", e=PG)
            then(tt(s5, s5, keep[:, :, :, None].to_broadcast(grid), ALU.mult))
            then(tt(s5, s5, low[:, :, :, None].to_broadcast(grid), ALU.add))
            for n in range(2):
                then(red(mx[:], sc[:], AX.X, ALU.max))
                then(tt(pos[:], sc[:], mx[:, :, None].to_broadcast(all16), ALU.is_equal))
                then(tt(pos[:], pos[:], order[:, None, :].to_broadcast(all16), ALU.mult))
                then(red(mx[:], pos[:], AX.X, ALU.max))
                then(tt(one[n][:], pos[:], mx[:, :, None].to_broadcast(all16), ALU.is_equal))
                if n == 0:
                    then(nc.vector.scalar_tensor_tensor(out=sc[:], in0=one[0][:], scalar=LOW, in1=sc[:],
                                                        op0=ALU.mult, op1=ALU.add))
            then(tt(one[0][:], one[0][:], one[1][:], ALU.add))
            nc.vector.memset(comb[:, :, EXPERTS:EXPERTS + 1], 1.0)
            ins = tt(comb[:, :, 0:EXPERTS], one[0][:], orig[:], ALU.mult)
            ins.then_inc(comb_rdy, 1)
            dve.wait_ge(comb_rdy, 1)
            c16 = comb[:, :, 0:EXPERTS]
            p0, p1, p2 = (part[:, :, a * EXPERTS:(a + 1) * EXPERTS] for a in range(PARTS))
            then(nc.vector.tensor_copy(p0, c16))
            then(tt(rest[:], c16, p0, ALU.subtract))
            then(nc.vector.tensor_copy(p1, rest[:]))
            tt(p2, rest[:], p1, ALU.subtract).then_inc(part_rdy, 1)

        @block.tensor
        def _(pe):
            pe.wait_ge(const_in, 16 * CONSTS)
            pe.wait_ge(comb_rdy, 1)
            for n in range(8):
                for t in range(GT):
                    last = nc.tensor.transpose(psum[0:EXPERTS + 1, n, t * P:(t + 1) * P], comb[:, n * GT + t, :],
                                               ident[:])
                last.then_inc(tr_rdy, 1)
            pe.wait_ge(part_rdy, 1)
            for n in range(4):
                pe.wait_ge(tr_used, n + 1)
                dst = psum[0:PARTS * EXPERTS, n, :].bitcast(BF16)
                for t in range(2 * GT):
                    last = nc.tensor.transpose(dst[:, t * P:(t + 1) * P], part[:, n * 2 * GT + t, :], identb[:])
                last.then_inc(tr_rdy, 1)


def experts(nc, w, W1, W3, W2, weights_in, X, XT, combT, combTf, psum, out):
    with ExitStack() as ctx:
        def sb(name, shape, dt=F32):
            return ctx.enter_context(nc.sbuf_tensor(name, shape, dt))

        def sem(name):
            return ctx.enter_context(nc.semaphore(name))

        select = sb("e_select", [PARTS * EXPERTS, EXPERTS, P], BF16)
        b1 = sb("e_b1", [P, ALL_EXPERTS])
        b3 = sb("e_b3", [P, ALL_EXPERTS])
        b2 = sb("e_b2", [EXPERTS + 1, DIM])
        comb = sb("e_comb", [EXPERTS + 1, BLK])
        act1 = sb("e_act1", [P, 2, BLK])
        gated = sb("e_gated", [P, 2, BLK])
        hid = sb("e_hid", [P, 2, BLK])
        res = sb("e_res", [P, BT, DIM])
        const_in, comb_sb, h_rdy, act_rdy, gated_rdy, hid_rdy = (
            sem("e_" + n) for n in ("const_in", "comb_sb", "h_rdy", "act_rdy", "gated_rdy", "hid_rdy"))
        y_rdy, y_done, y_used, out_done = (sem("e_" + n) for n in ("y_rdy", "y_done", "y_used", "out_done"))
        CONSTS = 4
        E = ALL_EXPERTS
        yacc = psum[:, 6:8, :].rearrange("p b (t d) -> p (b t) d", d=DIM)

        block = ctx.enter_context(nc.Block())

        @block.sync
        def _(sp):
            for dst, src in ((select[:], w["select"].rearrange("k (e p) -> k e p", p=P)), (b1[:], w["b1"]),
                             (b3[:], w["b3"]), (b2[:], w["b2"])):
                sp.dma_start(dst, src).then_inc(const_in, 16)
            sp.sem_inc(out_done, 16)
            with sp.Fori(0, BATCH) as b, sp.Fori(0, BPB) as j:
                sp.wait_ge(y_used, b * BPB + j + 2)
                sp.dma_start(out.rearrange("b (j t p) d -> b j p t d", p=P, t=BT)[bass.ds(b, 1), bass.ds(j, 1)],
                             res[:]).then_inc(out_done, 16)
            sp.wait_ge(out_done, 16 + 16 * BLOCKS)

        @block.gpsimd
        def _(pool):
            with pool.Fori(0, BLOCKS) as j:
                pool.wait_ge(y_rdy, j + 1)
                nc.gpsimd.tensor_copy(comb[:], combTf[0:EXPERTS + 1, bass.ds(j * BLK, BLK)]).then_inc(comb_sb, 1)

        @block.scalar
        def _(act):
            act.wait_ge(const_in, 16 * CONSTS)
            with act.Fori(0, BLOCKS) as j:
                for e in range(E):
                    act.wait_ge(h_rdy, j * E + e + 1)
                    act.wait_ge(gated_rdy, j * E + e + 1)
                    nc.scalar.activation(act1[:, e % 2, :], psum[:, (e % 2) * 3, :], ACT.Silu,
                                         bias=b1[:, e:e + 1]).then_inc(act_rdy, 1)

        @block.vector
        def _(dve):
            dve.sem_inc(gated_rdy, 2)
            dve.sem_inc(hid_rdy, 2)
            dve.sem_inc(y_used, 1)
            dve.wait_ge(const_in, 16 * CONSTS)
            with dve.Fori(0, BLOCKS) as j:
                for e in range(E):
                    s = e % 2
                    dve.wait_ge(act_rdy, j * E + e + 1)
                    dve.wait_ge(y_done, j * E + e + 1)
                    dst = gated if e < EXPERTS else hid
                    ins = nc.vector.scalar_tensor_tensor(out=dst[:, s, :], in0=psum[:, s * 3 + 1, :],
                                                         scalar=b3[:, e:e + 1], in1=act1[:, s, :],
                                                         op0=ALU.add, op1=ALU.mult)
                    ins.then_inc(gated_rdy, 1)
                    dve.wait_ge(gated_rdy, j * E + e + 3)
                    if e < EXPERTS:
                        nc.vector.tensor_tensor(hid[:, s, :], gated[:, s, :], psum[:, s * 3 + 2, :],
                                                ALU.mult).then_inc(hid_rdy, 1)
                    else:
                        dve.sem_inc(hid_rdy, 1)
                dve.wait_ge(y_done, (j + 1) * E + 2)
                dve.wait_ge(out_done, j * 16 + 16)
                nc.vector.tensor_tensor(res[:], X[:, bass.ds(j * BT, BT), :], yacc, ALU.add).then_inc(y_used, 1)

        @block.tensor
        def _(pe):
            pe.sem_inc(y_rdy, 1)
            pe.sem_inc(y_done, 2)
            pe.wait_ge(const_in, 16 * CONSTS)
            pe.wait_ge(weights_in, 48)
            with pe.Fori(0, BLOCKS) as j:

                def up(e):
                    pe.wait_ge(hid_rdy, j * E + e + 1)
                    for m, W in enumerate((W1, W3)):
                        for c in range(DC):
                            last = nc.tensor.matmul(psum[:, (e % 2) * 3 + m, :], W[:, e, c, :],
                                                    XT[:, c, bass.ds(j * BLK, BLK)],
                                                    start=(c == 0), stop=(c == DC - 1))
                    if e < EXPERTS:
                        last = nc.tensor.matmul(psum[:, (e % 2) * 3 + 2, :], select[:, e, :],
                                                combT[0:PARTS * EXPERTS, bass.ds(j * BLK, BLK)], start=True, stop=True)
                    last.then_inc(h_rdy, 1)

                def down(e):
                    pe.wait_ge(hid_rdy, j * E + e + 3)
                    for t in range(BT):
                        last = nc.tensor.matmul(yacc[:, t, :], hid[:, e % 2, t * P:(t + 1) * P], W2[:, e, :],
                                                start=False, stop=(e == E - 1), skip_group_check=True)
                    last.then_inc(y_done, 1)

                up(0)
                up(1)
                pe.wait_ge(comb_sb, j + 1)
                pe.wait_ge(y_used, j + 1)
                for t in range(BT):
                    last = nc.tensor.matmul(yacc[:, t, :], comb[:, t * P:(t + 1) * P], b2[:],
                                            start=(t % 2 == 0), stop=False, skip_group_check=True)
                last.then_inc(y_rdy, 1)
                for e in range(E):
                    down(e)
                    if e + 2 < E:
                        up(e + 2)


def layer(nc, w, out):
    w = {n: a.bitcast(BF16) if a.dtype == mybir.dt.uint16 else a for n, a in w.items()}
    with ExitStack() as ctx:
        def sb(name, shape, dt=F32, to=ctx):
            return to.enter_context(nc.sbuf_tensor(name, shape, dt))

        psum = ctx.enter_context(nc.psum_tensor("psum", [P, 8, 512], F32))
        weights_in = ctx.enter_context(nc.semaphore("weights_in"))
        q_parts = nc.dram_tensor("q_parts", [BATCH, HEADS * 2, PARTS, HALF, SEQ], BF16).ap()
        k_parts = nc.dram_tensor("k_parts", [BATCH, KV_HEADS * 2, PARTS, HALF, SEQ], BF16).ap()
        W1 = sb("W1", [P, ALL_EXPERTS, DC, INTER])
        W3 = sb("W3", [P, ALL_EXPERTS, DC, INTER])
        W2 = sb("W2", [P, ALL_EXPERTS, DIM])
        logits = sb("logits", [P, TILES, EXPERTS])
        Y = sb("Y", [P, TILES, DIM])
        for dst, name in ((W1, "w1"), (W3, "w3")):
            nc.sync.dma_start(dst[:], w[name].rearrange("e (c p) i -> p e c i", p=P)).then_inc(weights_in, 16)
        nc.sync.dma_start(W2[:], w["w2"].rearrange("e p d -> p e d")).then_inc(weights_in, 16)
        with ExitStack() as attention:
            V = sb("V", [P, TILES * 2 * KV_HEADS * VC], to=attention)
            project(nc, w, Y, V, psum, q_parts, k_parts)
            attend(nc, w, V, Y, psum, q_parts, k_parts)
        X = sb("X2", [P, TILES, DIM])
        XT = sb("XT", [P, DC, TOKENS])
        combT = sb("combT", [PARTS * EXPERTS, TOKENS], BF16)
        combTf = sb("combTf", [EXPERTS + 1, TOKENS])
        finish(nc, w, Y, X, XT, logits, psum)
        route(nc, w, logits, combT, combTf, psum)
        experts(nc, w, W1, W3, W2, weights_in, X, XT, combT, combTf, psum, out)



def _constants():
    freq = (np.arange(0, HD, 2, dtype=np.float32) / np.float32(HD)) * np.float32(np.pi)
    pos = np.arange(SEQ, dtype=np.float32)[:, None]
    radius = np.float32(1.0) / (np.float32(1.0) + pos * np.float32(0.01))
    cos = radius * np.cos(pos * freq[None, :])
    sin = radius * np.sin(pos * freq[None, :])
    key_after = np.arange(P)[None, :] > np.arange(P)[:, None]

    def bits(a):
        return (np.ascontiguousarray(a, np.float32).view(np.uint32) >> 16).astype(np.uint16)

    select = np.zeros((PARTS * EXPERTS, EXPERTS, P), np.float32)
    for e in range(EXPERTS):
        select[e::EXPERTS, e, :] = 1.0
    return {
        "ident": np.eye(P, dtype=np.float32),
        "identb": bits(np.eye(P)),
        "mask": bits(np.where(key_after, -BIG, 0.0)),
        "rot": np.concatenate([cos, cos, sin, -sin], axis=1).astype(np.float32),
        "before": (np.arange(GROUPS)[None, :] < np.arange(GROUPS)[:, None]).astype(np.float32).reshape(-1),
        "order": np.arange(EXPERTS, 0, -1).astype(np.float32),
        "ones_rows": bits(np.ones((PARTS, 2 * SEQ))),
        "select": bits(select.reshape(PARTS * EXPERTS, EXPERTS * P)),
    }


def _arrays(a):
    cat, c = np.concatenate, np.ascontiguousarray
    ffn = {k[len("L0_ffn_"):]: v for k, v in a.items() if k.startswith("L0_ffn_")}

    def shared_in(m):
        return m.reshape(DIM, SHARED, INTER).transpose(1, 0, 2)

    return {
        "x": c(a["L0_attn_x"]),
        "w_qkvg": c(cat([a["L0_attn_Wq"].T, a["L0_attn_Wk"].T, a["L0_attn_Wv"].T, a["L0_attn_Wg"].T], axis=1)),
        "w_o": c(a["L0_attn_Wo"].T),
        "q_gain": c(a["L0_attn_q_gain"]),
        "lam": c(a["L0_attn_lambda_param"]),
        "gate_w": c(ffn["gate_w"].T),
        "gate_b": c(ffn["gate_b"]),
        "w1": c(cat([ffn["We1"], shared_in(ffn["ws1"])])),
        "w3": c(cat([ffn["We3"], shared_in(ffn["ws3"])])),
        "w2": c(cat([ffn["We2"], ffn["ws2"].reshape(SHARED, INTER, DIM)])),
        "b1": c(cat([ffn["be1"], ffn["bs1"].reshape(SHARED, INTER)]).T),
        "b3": c(cat([ffn["be3"], ffn["bs3"].reshape(SHARED, INTER)]).T),
        "b2": c(cat([ffn["be2"], ffn["bs2"][None, :]])),
        **_constants(),
    }


def kernel(**inputs):
    import concourse.bacc as _bacc
    from concourse.bass_utils import run_bass_kernel_spmd as _run

    nc = _bacc.Bacc("TRN2", target_bir_lowering=False, num_devices=1)
    arrays = _arrays({k: np.asarray(v) for k, v in inputs.items()})
    w = {n: nc.dram_tensor(n, a.shape, mybir.dt.from_np(a.dtype), kind="ExternalInput").ap()
         for n, a in arrays.items()}
    out = nc.dram_tensor("out", (BATCH, SEQ, DIM), F32, kind="ExternalOutput").ap()
    layer(nc, w, out)
    return _run(nc, [arrays], core_ids=[0]).results[0]["out"]
```

```python
from contextlib import ExitStack

import numpy as np

import concourse.bass as bass
from concourse import mybir

ALU = mybir.AluOpType
ACT = mybir.ActivationFunctionType
F32 = mybir.dt.float32
BF16 = mybir.dt.bfloat16
AX = mybir.AxisListType

P = 128
BATCH, SEQ, DIM = 2, 2048, 256
HEADS, KV_HEADS, HD = 16, 4, 16
REP = HEADS // KV_HEADS
HALF = HD // 2
TOKENS = BATCH * SEQ
TILES = TOKENS // P
BLK = 512
BT = BLK // P
BLOCKS = TOKENS // BLK
BPB = SEQ // BLK
DC = DIM // P
NORMED = HEADS + KV_HEADS
QK = NORMED * HD
KV = KV_HEADS * HD
COLS = QK + 2 * KV
PARTS = 3
ROWS = PARTS * PARTS * HALF
ROWSM = ROWS + PARTS
VC = 32
EXPERTS, GROUPS, INTER = 16, 4, 128
SHARED = 2
ALL_EXPERTS = EXPERTS + SHARED
GAIN_LIMIT = 8.0
LN_EPS = 1e-5
RMS_EPS = float(np.finfo(np.float32).eps)
SCALE = 1.0 / float(np.sqrt(HALF))
BIG = 1e30


def project(nc, w, X, V, psum, q_parts, k_parts):
    with ExitStack() as ctx:
        def sb(name, shape, dt=F32):
            return ctx.enter_context(nc.sbuf_tensor(name, shape, dt))

        def sem(name):
            return ctx.enter_context(nc.semaphore(name))

        wt = sb("p_wt", [P, DC, COLS])
        ident = sb("p_ident", [P, P])
        identb = sb("p_identb", [P, P], BF16)
        rot = sb("p_rot", [P, TILES, 2 * HD])
        gain = sb("p_gain", [P, HEADS])
        stats = sb("p_stats", [P, BT, 6])
        mv = sb("p_mv", [P, BT, 2])
        vare = sb("p_vare", [P, BT])
        std = sb("p_std", [P, BT])
        rstd = sb("p_rstd", [P, BT])
        xn = sb("p_xn", [P, BT, DIM])
        xnT = sb("p_xnT", [P, DC, BLK])
        sq = sb("p_sq", [P, BT, QK])
        ss = sb("p_ss", [P, BT * NORMED])
        sse = sb("p_sse", [P, BT * NORMED])
        rms = sb("p_rms", [P, BT * NORMED])
        rr = sb("p_rr", [P, BT, NORMED])
        sg = sb("p_sg", [P, BT, KV])
        qn = sb("p_qn", [P, BT, NORMED, HD])
        ra = sb("p_ra", [P, BT, NORMED, HD])
        rb = sb("p_rb", [P, BT, NORMED, HD])
        f = sb("p_f", [P, BT, QK])
        r = sb("p_r", [P, BT, QK])
        part = sb("p_part", [P, PARTS, BT, QK], BF16)
        outq = sb("p_outq", [P, PARTS, 2, BLK], BF16)
        outk = sb("p_outk", [KV, PARTS, BLK], BF16)

        waited = sem("p_waited")
        const_in, x_in, v_set = sem("p_const_in"), sem("p_x_in"), sem("p_v_set")
        var_rdy, std_rdy, xn_rdy = sem("p_var_rdy"), sem("p_std_rdy"), sem("p_xn_rdy")
        xT_rdy, xT_used, pj_rdy, pj_used = sem("p_xT_rdy"), sem("p_xT_used"), sem("p_pj_rdy"), sem("p_pj_used")
        sq_rdy, sg_rdy, ss_rdy, rms_rdy = sem("p_sq_rdy"), sem("p_sg_rdy"), sem("p_ss_rdy"), sem("p_rms_rdy")
        qn_rdy, rb_rdy, f_rdy, r_rdy = sem("p_qn_rdy"), sem("p_rb_rdy"), sem("p_f_rdy"), sem("p_r_rdy")
        hi_rdy, mid_rdy, lo_rdy = sem("p_hi_rdy"), sem("p_mid_rdy"), sem("p_lo_rdy")
        tr_rdy, tr_used, parts_out = sem("p_tr_rdy"), sem("p_tr_used"), sem("p_parts_out")
        dve_step = sem("p_dve_step")

        xT = psum[:, 0:2, :]
        pj = psum[:, 2:6, :]
        pj_qk = pj[:, :, 0:QK]
        trb = [psum[:, 6 + s, :].bitcast(BF16).rearrange("p (c n) -> p c n", c=2) for s in range(2)]
        x_dram = w["x"].rearrange("b (t p) d -> p (b t) d", p=P)
        CONSTS = 6
        DVE_STEPS = 7

        block = ctx.enter_context(nc.Block())

        @block.sync
        def _(sp):
            for dst, src in ((wt[:], w["w_qkvg"].rearrange("(c p) n -> p c n", p=P)), (ident[:], w["ident"]),
                             (identb[:], w["identb"]), (gain[:], w["q_gain"].partition_broadcast(P)),
                             (rot[:, 0:TILES // 2, :], w["rot"].rearrange("(t p) n -> p t n", p=P)),
                             (rot[:, TILES // 2:TILES, :], w["rot"].rearrange("(t p) n -> p t n", p=P))):
                sp.dma_start(dst, src).then_inc(const_in, 16)
            with sp.Fori(0, BLOCKS) as i:
                sp.dma_start(X[:, bass.ds(i * BT, BT), :], x_dram[:, bass.ds(i * BT, BT), :]).then_inc(x_in, 16)
                sp.wait_ge(x_in, i * 16 + 16)
                sp.sem_inc(waited, 1)
            sp.sem_inc(parts_out, 16)
            with sp.Fori(0, BATCH) as b:
                with sp.Fori(0, BPB) as j:
                    tok = bass.ds(j * BLK, BLK)
                    for p in range(PARTS):
                        done = b * (BPB * 6) + j * 6 + 2 * p
                        sp.wait_ge(tr_used, done + 3)
                        for c in range(2):
                            sp.dma_start(q_parts[bass.ds(b, 1), c * 16:(c + 1) * 16, p, :, tok],
                                         outq[:, p, c, :]).then_inc(parts_out, 16)
                        sp.wait_ge(tr_used, done + 4)
                        sp.dma_start(k_parts[bass.ds(b, 1), :, p, :, tok], outk[:, p]).then_inc(parts_out, 16)
            sp.wait_ge(parts_out, 16 + BLOCKS * PARTS * 3 * 16)

        @block.gpsimd
        def _(pool):
            v5 = V[:].rearrange("p (n c) -> p n c", c=VC)
            nc.gpsimd.memset(v5[:, :, 0:HALF], 0.0)
            nc.gpsimd.memset(v5[:, :, HALF:HALF + 1], 1.0)
            nc.gpsimd.memset(v5[:, :, HALF + 1:VC], 0.0).then_inc(v_set, 1)
            pool.wait_ge(const_in, 16 * CONSTS)
            with pool.Fori(0, BLOCKS) as i:
                pool.wait_ge(qn_rdy, i + 1)
                for h, o in ((0, 1), (1, 0)):
                    last = nc.gpsimd.tensor_tensor(
                        rb[:, :, :, h * HALF:(h + 1) * HALF], qn[:, :, :, o * HALF:(o + 1) * HALF],
                        rot[:, bass.ds(i * BT, BT), None, HD + h * HALF:HD + (h + 1) * HALF]
                        .to_broadcast([P, BT, NORMED, HALF]), ALU.mult)
                last.then_inc(rb_rdy, 1)

        @block.scalar
        def _(act):
            act.sem_inc(tr_used, 2)
            with act.Fori(0, BLOCKS) as i:
                act.wait_ge(var_rdy, i + 1)
                nc.scalar.activation(std[:], vare[:], ACT.Sqrt).then_inc(std_rdy, 1)
                act.wait_ge(xT_rdy, i + 2)
                act.wait_ge(pj_rdy, i + 1)
                nc.scalar.copy(xnT[:], xT).then_inc(xT_used, 1)
                act.wait_ge(pj_rdy, i + 2)
                nc.scalar.activation(sq[:], pj_qk, ACT.Square).then_inc(sq_rdy, 1)
                nc.scalar.activation(sg[:], pj[:, :, QK + KV:COLS], ACT.Sigmoid).then_inc(sg_rdy, 1)
                act.wait_ge(ss_rdy, i + 1)
                nc.scalar.activation(rms[:], sse[:], ACT.Sqrt).then_inc(rms_rdy, 1)
                act.wait_ge(f_rdy, i + 1)
                act.wait_ge(tr_rdy, i * 6 + 1)
                nc.scalar.copy(part[:, 0], f[:]).then_inc(hi_rdy, 1)
                act.wait_ge(r_rdy, i + 1)
                nc.scalar.copy(part[:, 1], r[:]).then_inc(mid_rdy, 1)
                act.wait_ge(parts_out, i * 144 + 16)
                for p in range(PARTS):
                    act.wait_ge(tr_rdy, i * 6 + 2 * p + 2)
                    nc.scalar.copy(outq[:, p], trb[0]).then_inc(tr_used, 1)
                    act.wait_ge(tr_rdy, i * 6 + 2 * p + 3)
                    nc.scalar.copy(outk[:, p], trb[1][0:KV, 0, :]).then_inc(tr_used, 1)

        @block.vector
        def _(dve):
            dve.sem_inc(pj_used, 1)
            dve.wait_ge(const_in, 16 * CONSTS)
            dve.wait_ge(v_set, 1)
            with dve.Fori(0, BLOCKS) as i:
                steps = [0]

                def then(ins):
                    steps[0] += 1
                    ins.then_inc(dve_step, 1)
                    dve.wait_ge(dve_step, i * DVE_STEPS + steps[0])

                dve.wait_ge(x_in, i * 16 + 16)
                dve.sem_inc(waited, 1)
                for t in range(BT):
                    last = nc.vector.bn_stats(stats[:, t, :], X[:, bass.ds(i * BT + t, 1), :])
                then(last)
                dve.sem_inc(waited, 1)
                for t in range(BT):
                    last = nc.vector.bn_aggr(mv[:, t, :], stats[:, t, :])
                then(last)
                nc.vector.tensor_scalar(vare[:], mv[:, :, 1], LN_EPS, None, ALU.add).then_inc(var_rdy, 1)
                dve.wait_ge(std_rdy, i + 1)
                then(nc.vector.reciprocal(rstd[:], std[:]))
                dve.wait_ge(xT_rdy, i + 1)
                for t in range(BT):
                    last = nc.vector.tensor_scalar(xn[:, t, :], X[:, bass.ds(i * BT + t, 1), :], mv[:, t, 0:1],
                                                   rstd[:, t:t + 1], ALU.subtract, ALU.mult)
                last.then_inc(xn_rdy, 1)
                dve.wait_ge(sq_rdy, i + 1)
                then(nc.vector.tensor_reduce(ss[:], sq[:].rearrange("p t (h d) -> p (t h) d", d=HD), AX.X, ALU.add))
                nc.vector.tensor_scalar(sse[:], ss[:], 1.0 / HD, RMS_EPS, ALU.mult, ALU.add).then_inc(ss_rdy, 1)
                dve.wait_ge(rms_rdy, i + 1)
                then(nc.vector.reciprocal(rr[:].rearrange("p t h -> p (t h)"), rms[:]))
                then(nc.vector.tensor_tensor(rr[:, :, 0:HEADS], rr[:, :, 0:HEADS],
                                             gain[:, None, :].to_broadcast([P, BT, HEADS]), ALU.mult))
                dve.wait_ge(sg_rdy, i + 1)
                nc.vector.tensor_tensor(qn[:], pj_qk.rearrange("p t (h d) -> p t h d", d=HD),
                                        rr[:, :, :, None].to_broadcast([P, BT, NORMED, HD]),
                                        ALU.mult).then_inc(qn_rdy, 1)
                for t in range(BT):
                    last = nc.vector.tensor_tensor(
                        V[:, bass.ds((i * BT + t) * 2 * KV_HEADS * VC, 2 * KV_HEADS * VC)]
                        .rearrange("p (n c) -> p n c", c=VC)[:, :, 0:HALF],
                        pj[:, t, QK:QK + KV].rearrange("p (n c) -> p n c", c=HALF),
                        sg[:, t, :].rearrange("p (n c) -> p n c", c=HALF), ALU.mult)
                last.then_inc(pj_used, 1)
                dve.wait_ge(qn_rdy, i + 1)
                then(nc.vector.tensor_tensor(
                    ra[:], qn[:], rot[:, bass.ds(i * BT, BT), None, 0:HD].to_broadcast([P, BT, NORMED, HD]), ALU.mult))
                dve.wait_ge(rb_rdy, i + 1)
                nc.vector.tensor_tensor(f[:], ra[:].rearrange("p t h d -> p t (h d)"),
                                        rb[:].rearrange("p t h d -> p t (h d)"), ALU.add).then_inc(f_rdy, 1)
                dve.wait_ge(hi_rdy, i + 1)
                nc.vector.tensor_tensor(r[:], f[:], part[:, 0], ALU.subtract).then_inc(r_rdy, 1)
                dve.wait_ge(mid_rdy, i + 1)
                nc.vector.tensor_tensor(part[:, 2], r[:], part[:, 1], ALU.subtract).then_inc(lo_rdy, 1)
                assert steps[0] == DVE_STEPS, steps

        @block.tensor
        def _(pe):
            pe.sem_inc(xT_rdy, 1)
            pe.sem_inc(pj_rdy, 1)
            pe.sem_inc(tr_rdy, 1)
            pe.wait_ge(const_in, 16 * CONSTS)
            with pe.Fori(0, BLOCKS) as i:
                pe.wait_ge(xn_rdy, i + 1)
                for t in range(BT):
                    for c in range(DC):
                        last = nc.tensor.transpose(xT[:, c, t * P:(t + 1) * P], xn[:, t, c * P:(c + 1) * P], ident[:])
                last.then_inc(xT_rdy, 1)
                pe.wait_ge(xT_used, i + 1)
                pe.wait_ge(pj_used, i + 1)
                for t in range(BT):
                    for c in range(DC):
                        last = nc.tensor.matmul(pj[:, t, 0:COLS], xnT[:, c, t * P:(t + 1) * P], wt[:, c, :],
                                                start=(c == 0), stop=(c == DC - 1))
                last.then_inc(pj_rdy, 1)
                for p, ready in enumerate((hi_rdy, mid_rdy, lo_rdy)):
                    pe.wait_ge(ready, i + 1)
                    for g in range(2):
                        pe.wait_ge(tr_used, i * 6 + 2 * p + g + 1)
                        pe.sem_inc(waited, 1)
                        for c in range(2 if g == 0 else 1):
                            for t in range(BT):
                                cols = (c * P, (c + 1) * P) if g == 0 else (HEADS * HD, QK)
                                last = nc.tensor.transpose(trb[g][0:cols[1] - cols[0], c, t * P:(t + 1) * P],
                                                           part[:, p, t, cols[0]:cols[1]], identb[:])
                        last.then_inc(tr_rdy, 1)

def attend(nc, w, V, Y, psum, q_parts, k_parts):
    with ExitStack() as ctx:
        def sb(name, shape, dt=F32):
            return ctx.enter_context(nc.sbuf_tensor(name, shape, dt))

        def sem(name):
            return ctx.enter_context(nc.semaphore(name))

        QT = SEQ // P
        NQ = SEQ // BLK
        RUNS = BATCH * KV_HEADS
        PAIRS = REP // 2
        S_BUFS, P_BUFS = 3, 4
        ACC = 2 * S_BUFS
        units = [(J, i) for J in range(NQ) for i in range((J + 1) * BT)]
        UNITS = len(units)
        last_unit = [max(t for t, (j, _) in enumerate(units) if j == J) for J in range(NQ)]
        TURN = 3
        MAXES = REP * QT
        chunks = [(m, c) for m in range(MAXES) for c in range(m % QT // BT + 1)]
        CHUNKS = len(chunks)
        C_BUFS = 2 * S_BUFS

        ident = sb("a_ident", [P, P])
        identb = sb("a_identb", [P, P], BF16)
        mask = sb("a_mask", [P, P], BF16)
        lam = sb("a_lam", [P, BATCH, HEADS])
        gain = sb("a_gain", [P, HEADS])
        gain_max = sb("a_gain_max", [P, 1])
        bounded = sb("a_bounded", [P, 1], mybir.dt.int32)
        qrows = [sb(f"a_qrows{h}", [ROWSM, REP, SEQ], BF16) for h in range(2)]
        krows = [sb(f"a_krows{h}", [ROWSM, SEQ], BF16) for h in range(2)]
        vals = [sb(f"a_vals{h}", [P, QT, VC]) for h in range(2)]
        probs = sb("a_probs", [P, P_BUFS, 2, BLK])
        chunkmax = sb("a_chunkmax", [P, MAXES, NQ])
        negmax = sb("a_negmax", [P, MAXES])
        rest = sb("a_rest", [P, MAXES])
        maxpart = sb("a_maxpart", [P, PARTS, MAXES], BF16)
        maxT = sb("a_maxT", [MAXES, PARTS, P], BF16)
        outT = sb("a_outT", [P, 2, BLK])
        inv = sb("a_inv", [P, BT, REP])
        invl = sb("a_invl", [P, BT, REP])
        a1 = sb("a_a1", [P, QT, REP, HALF])
        a2 = sb("a_a2", [P, BT, REP, HALF])

        waited = sem("a_waited")
        const_in, flag_rdy, low_set, max_rdy = (sem("a_" + n) for n in ("const_in", "flag_rdy", "low_set", "max_rdy"))
        rows_in = [sem(f"a_rows_in{h}") for h in range(2)]
        max_in = [sem(f"a_max_in{h}") for h in range(2)]
        step_done = [sem(f"a_step_done{h}") for h in range(2)]
        vals_rdy = sem("a_vals_rdy")
        mx_rdy, mx_used, max_step = sem("a_mx_rdy"), sem("a_mx_used"), sem("a_max_step")
        mp_rdy, mt_rdy, mt_sb = sem("a_mp_rdy"), sem("a_mt_rdy"), sem("a_mt_sb")
        s_rdy, exp_rdy, av_done = sem("a_s_rdy"), sem("a_exp_rdy"), sem("a_av_done")
        ot_rdy, tm_rdy, tm_used = sem("a_ot_rdy"), sem("a_tm_rdy"), sem("a_tm_used")
        dve_step = sem("a_dve_step")
        ROWS_IN = (PARTS + PARTS * PARTS) * 16

        q_src = q_parts.rearrange("b (k r h) p d s -> (b k) h (p d) r s", k=KV_HEADS, h=2)
        k_src = k_parts.rearrange("b (k h) p d s -> (b k) h p d s", h=2)
        V4 = V[:].rearrange("p (t n c) -> p t n c", n=2 * KV_HEADS, c=VC)
        maxt = psum[0:MAXES, 0, 0:PARTS * P // 2].bitcast(BF16).rearrange("m (a q) -> m a q", a=PARTS)
        consts = ((gain[:], w["q_gain"].partition_broadcast(P)), (ident[:], w["ident"]), (identb[:], w["identb"]),
                  (mask[:], w["mask"]), (lam[:, 0, :], w["lam"].partition_broadcast(P)),
                  (lam[:, 1, :], w["lam"].partition_broadcast(P)),
                  (krows[0][ROWS:ROWSM, :], w["ones_rows"][:, 0:SEQ]),
                  (krows[1][ROWS:ROWSM, :], w["ones_rows"][:, SEQ:2 * SEQ]),
                  (qrows[0][ROWS:ROWSM, :, :], w["zero_rows"].rearrange("a (r s) -> a r s", r=REP)),
                  (qrows[1][ROWS:ROWSM, :, :], w["zero_rows"].rearrange("a (r s) -> a r s", r=REP)))
        CONSTS = len(consts)

        def is_bounded(eng):
            eng.wait_ge(flag_rdy, 1)
            return eng.value_load(bounded[0:1, 0:1], min_val=0, max_val=1)

        block = ctx.enter_context(nc.Block())

        @block.sync
        def _(sp):
            for dst, src in consts:
                sp.dma_start(dst, src).then_inc(const_in, 16)
            for h in range(2):
                sp.sem_inc(step_done[h], 1)
            with sp.Fori(0, RUNS) as n:
                for h in range(2):
                    sp.wait_ge(step_done[h], n + 1)
                    for a in range(PARTS):
                        rows = slice(a * PARTS * HALF, (a + 1) * PARTS * HALF)
                        sp.dma_start(qrows[h][rows, :, :], q_src[bass.ds(n, 1), h]).then_inc(rows_in[h], 16)
                        for p in range(PARTS):
                            row = (a * PARTS + p) * HALF
                            sp.dma_start(krows[h][row:row + HALF, :], k_src[bass.ds(n, 1), h, a, :, :]
                                         ).then_inc(rows_in[h], 16)

        @block.gpsimd
        def _(pool):
            with pool.Fori(0, BATCH) as b:
                with pool.Fori(0, KV_HEADS) as k:
                    for h in range(2):
                        pool.wait_ge(step_done[h], b * KV_HEADS + k + 1)
                        nc.gpsimd.tensor_copy(
                            vals[h][:], V4[:, bass.ds(b * QT, QT), bass.ds(k * 2 + h, 1), :]).then_inc(vals_rdy, 1)

        @block.scalar
        def _(act):
            within = is_bounded(act)

            def bring_maxima(step, h):
                act.wait_ge(mt_rdy, step + 1)
                nc.scalar.copy(maxT[:], maxt).then_inc(mt_sb, 1)
                act.wait_ge(mt_sb, step + 1)
                for a in range(PARTS):
                    act.dma_start(qrows[h][ROWS + a:ROWS + a + 1, :, :], maxT[:, a, :]).then_inc(max_in[h], 16)

            with act.Fori(0, RUNS) as n:
                for h in range(2):
                    step = n * 2 + h
                    with act.If(within < 1):
                        bring_maxima(step, h)
                    for t, (J, i) in enumerate(units):
                        N = BLK - max(0, i - J * BT) * P
                        act.wait_ge(av_done, step * UNITS + t + 1)
                        for g in range(PAIRS):
                            u = t * PAIRS + g
                            s = u % S_BUFS
                            act.wait_ge(s_rdy, step * (UNITS * PAIRS) + u + 1)
                            nc.scalar.activation(probs[:, u % P_BUFS, :, 0:N], psum[:, s * 2:s * 2 + 2, 0:N],
                                                 ACT.Exp, scale=SCALE).then_inc(exp_rdy, 1)

        @block.vector
        def _(dve):
            dve.sem_inc(mx_used, C_BUFS)
            dve.sem_inc(tm_used, 2)
            dve.wait_ge(const_in, 16 * CONSTS)
            nc.vector.tensor_reduce(gain_max[:], gain[:], AX.X, ALU.max,
                                    apply_absolute_value=True).then_inc(max_rdy, 1)
            dve.wait_ge(max_rdy, 1)
            nc.vector.tensor_scalar(bounded[:], gain_max[:], GAIN_LIMIT, None, ALU.is_le).then_inc(flag_rdy, 1)
            nc.vector.memset(chunkmax[:], -BIG).then_inc(low_set, 1)
            within = is_bounded(dve)
            dve.wait_ge(low_set, 1)
            MAX_STEPS, TURN_STEPS = 4, [1, 3]
            RUN_STEPS = NQ * sum(TURN_STEPS)

            def find_maxima(step):
                for x, (m, c) in enumerate(chunks):
                    N = min(BLK, (m % QT + 1) * P - c * BLK)
                    dve.wait_ge(mx_rdy, step * CHUNKS + x + 1)
                    nc.vector.tensor_reduce(chunkmax[:, m, c:c + 1], psum[:, x % C_BUFS, 0:N], AX.X,
                                            ALU.max).then_inc(mx_used, 1)
                dve.wait_ge(mx_used, (step + 1) * CHUNKS + C_BUFS)
                for s, ins in enumerate((
                        lambda: nc.vector.tensor_reduce(negmax[:], chunkmax[:], AX.X, ALU.max, negate=True),
                        lambda: nc.vector.tensor_copy(maxpart[:, 0, :], negmax[:]),
                        lambda: nc.vector.tensor_tensor(rest[:], negmax[:], maxpart[:, 0, :], ALU.subtract),
                        lambda: nc.vector.tensor_copy(maxpart[:, 1, :], rest[:]))):
                    ins().then_inc(max_step, 1)
                    dve.wait_ge(max_step, step * MAX_STEPS + s + 1)
                nc.vector.tensor_tensor(maxpart[:, 2, :], rest[:], maxpart[:, 1, :], ALU.subtract).then_inc(mp_rdy, 1)

            def copy_out(step, J):
                dve.wait_ge(av_done, step * UNITS + last_unit[J] + 3)
                nc.vector.tensor_copy(outT[:, J % 2, :], psum[:, ACC + J % 2, :]).then_inc(ot_rdy, 1)

            def normalise(n, h, J):
                step = n * 2 + h
                at = n * RUN_STEPS + (NQ * TURN_STEPS[0] if h else 0) + J * TURN_STEPS[h]
                tok = psum[:, ACC + J % 2, :].rearrange("p (q h c) -> p q h c", h=REP, c=VC)
                dve.wait_ge(tm_rdy, step * NQ + J + 1)
                nc.vector.reciprocal(inv[:], tok[:, :, :, HALF]).then_inc(dve_step, 1)
                dve.wait_ge(dve_step, at + 1)
                if h == 0:
                    nc.vector.tensor_tensor(a1[:, J * BT:(J + 1) * BT], tok[:, :, :, 0:HALF],
                                            inv[:, :, :, None].to_broadcast([P, BT, REP, HALF]),
                                            ALU.mult).then_inc(tm_used, 1)
                    return
                lam2 = lam[:].rearrange("p b h -> p (b h)")[:, None, bass.ds(n * REP, REP)]
                nc.vector.tensor_tensor(invl[:], inv[:], lam2.to_broadcast([P, BT, REP]),
                                        ALU.mult).then_inc(dve_step, 1)
                dve.wait_ge(dve_step, at + 2)
                nc.vector.tensor_tensor(a2[:], tok[:, :, :, 0:HALF],
                                        invl[:, :, :, None].to_broadcast([P, BT, REP, HALF]),
                                        ALU.mult).then_inc(tm_used, 1)
                dve.wait_ge(tm_used, step * NQ + J + 3)
                y = Y[:, bass.ds(n, 1), J * BT:(J + 1) * BT, :, :].rearrange("p n t h c -> p (n t) h c")
                nc.vector.tensor_tensor(y[:, :, :, 0:HALF], a1[:, J * BT:(J + 1) * BT], a2[:], ALU.subtract)
                nc.vector.tensor_tensor(y[:, :, :, HALF:HD], a1[:, J * BT:(J + 1) * BT], a2[:],
                                        ALU.add).then_inc(dve_step, 1)
                dve.wait_ge(dve_step, at + 3)

            def run(n, first_run):
                for h in range(2):
                    step = n * 2 + h
                    with dve.If(within < 1):
                        find_maxima(step)
                    if not (first_run and h == 0):
                        normalise(n if h else n - 1, 1 - h, NQ - 1)
                    for J in range(NQ):
                        copy_out(step, J)
                        if J < NQ - 1:
                            normalise(n, h, J)

            run(0, True)
            with dve.Fori(1, RUNS) as n:
                run(n, False)
            normalise(RUNS - 1, 1, NQ - 1)

        @block.tensor
        def _(pe):
            pe.sem_inc(exp_rdy, S_BUFS)
            pe.sem_inc(av_done, 2)
            within = is_bounded(pe)

            def maxima(step, h, n):
                pe.wait_ge(exp_rdy, step * UNITS * PAIRS + S_BUFS)
                for x, (m, c) in enumerate(chunks):
                    head, q = divmod(m, QT)
                    N = min(BLK, (q + 1) * P - c * BLK)
                    diag = c == q // BT
                    out = psum[:, x % C_BUFS, :]
                    pe.wait_ge(mx_used, step * CHUNKS + x + 1)
                    last = nc.tensor.matmul(out[:, 0:N], qrows[h][0:ROWS, head, q * P:(q + 1) * P],
                                            krows[h][0:ROWS, c * BLK:c * BLK + N], start=True, stop=not diag)
                    if diag:
                        last = nc.tensor.matmul(out[:, N - P:N], identb[:], mask[:], start=False, stop=True)
                    last.then_inc(mx_rdy, 1)
                pe.wait_ge(mp_rdy, step + 1)
                pe.sem_inc(waited, 1)
                for a in range(PARTS):
                    last = nc.tensor.transpose(maxt[:, a, :], maxpart[:, a, :], identb[:])
                last.then_inc(mt_rdy, 1)
                pe.wait_ge(max_in[h], (n + 1) * 48)

            def scores(step, h, t):
                J, i = units[t]
                lo = max(0, i - J * BT) * P
                for g in range(PAIRS):
                    u = t * PAIRS + g
                    pe.wait_ge(exp_rdy, step * (UNITS * PAIRS) + u + (2 if u < 2 else 1))
                    for e in range(2):
                        out = psum[:, (u % S_BUFS) * 2 + e, :]
                        last = nc.tensor.matmul(out[:, 0:BLK - lo], krows[h][:, i * P:(i + 1) * P],
                                                qrows[h][:, g * 2 + e, J * BLK + lo:(J + 1) * BLK],
                                                start=True, stop=i < J * BT)
                        if i >= J * BT:
                            last = nc.tensor.matmul(out[:, 0:P], mask[:], identb[:], start=False, stop=True)
                    last.then_inc(s_rdy, 1)

            def values(step, h, t):
                J, i = units[t]
                lo = max(0, i - J * BT) * P
                if i == 0:
                    pe.wait_ge(tm_used, step * NQ + J + 1)
                pe.wait_ge(exp_rdy, step * (UNITS * PAIRS) + t * PAIRS + PAIRS + S_BUFS)
                for head in range(REP):
                    u = t * PAIRS + head // 2
                    last = nc.tensor.matmul(psum[head * VC:(head + 1) * VC, ACC + J % 2, lo:BLK],
                                            vals[h][:, i, :], probs[:, u % P_BUFS, head % 2, 0:BLK - lo],
                                            start=(i == 0), stop=(i == (J + 1) * BT - 1))
                last.then_inc(av_done, 1)

            def turn(step, h, J):
                pe.wait_ge(ot_rdy, step * NQ + J + 1)
                for q in range(BT):
                    last = nc.tensor.transpose(psum[:, ACC + J % 2, q * P:(q + 1) * P],
                                               outT[:, J % 2, q * P:(q + 1) * P], ident[:])
                    if J == NQ - 1 and q == 0:
                        last.then_inc(step_done[h], 1)
                last.then_inc(tm_rdy, 1)

            def run(n, first_run):
                for h in range(2):
                    step = n * 2 + h
                    pe.wait_ge(rows_in[h], (n + 1) * ROWS_IN)
                    with pe.If(within < 1):
                        maxima(step, h, n)
                    pe.wait_ge(vals_rdy, step + 1)
                    for t in range(UNITS + 1):
                        if t < UNITS:
                            scores(step, h, t)
                        if t > 0:
                            values(step, h, t - 1)
                        if t == 2 and not (first_run and h == 0):
                            turn(step - 1, 1 - h, NQ - 1)
                        for J in range(NQ - 1):
                            if t == last_unit[J] + TURN:
                                turn(step, h, J)

            run(0, True)
            with pe.Fori(1, RUNS) as n:
                run(n, False)
            turn(2 * RUNS - 1, 1, NQ - 1)


def finish(nc, w, Y, X, XT, logits, psum):
    with ExitStack() as ctx:
        def sb(name, shape, dt=F32):
            return ctx.enter_context(nc.sbuf_tensor(name, shape, dt))

        def sem(name):
            return ctx.enter_context(nc.semaphore(name))

        wo = sb("f_wo", [P, DC, DIM])
        gw = sb("f_gw", [P, DC, EXPERTS])
        ident = sb("f_ident", [P, P])
        y = sb("f_y", [P, BT, DIM])
        yT = sb("f_yT", [P, DC, BLK])
        stats = sb("f_stats", [P, BT, 6])
        mv = sb("f_mv", [P, BT, 2])
        vare = sb("f_vare", [P, BT])
        std = sb("f_std", [P, BT])
        rstd = sb("f_rstd", [P, BT])
        xn = sb("f_xn", [P, BT, DIM])
        xT = sb("f_xT", [P, DC, BLK])

        waited = sem("f_waited")
        const_in, x_in = sem("f_const_in"), sem("f_x_in")
        y_rdy, yT_rdy, yT_sb, o_rdy, res_rdy = (sem("f_" + n) for n in ("y_rdy", "yT_rdy", "yT_sb", "o_rdy", "res_rdy"))
        var_rdy, std_rdy, xn_rdy, xT_rdy, xT_sb = (
            sem("f_" + n) for n in ("var_rdy", "std_rdy", "xn_rdy", "xT_rdy", "xT_sb"))
        xT_kept, lg_rdy, lg_used, dve_step = (sem("f_" + n) for n in ("xT_kept", "lg_rdy", "lg_used", "dve_step"))
        DVE_STEPS = 3
        CONSTS = 3
        x_dram = w["x"].rearrange("b (t p) d -> p (b t) d", p=P)
        proj = psum[:, 2:4, :].rearrange("p b (t d) -> p (b t) d", d=DIM)
        lg = psum[:, 6, 0:BT * EXPERTS].rearrange("p (t e) -> p t e", e=EXPERTS)

        block = ctx.enter_context(nc.Block())

        @block.sync
        def _(sp):
            for dst, src in ((wo[:], w["w_o"].rearrange("(c p) n -> p c n", p=P)), (ident[:], w["ident"]),
                             (gw[:], w["gate_w"].rearrange("(c p) n -> p c n", p=P))):
                sp.dma_start(dst, src).then_inc(const_in, 16)
            with sp.Fori(0, BLOCKS) as i:
                sp.dma_start(X[:, bass.ds(i * BT, BT), :], x_dram[:, bass.ds(i * BT, BT), :]).then_inc(x_in, 16)
                sp.wait_ge(x_in, i * 16 + 16)
                sp.sem_inc(waited, 1)

        @block.gpsimd
        def _(pool):
            with pool.Fori(0, BLOCKS) as i:
                pool.wait_ge(xT_sb, i + 1)
                nc.gpsimd.tensor_copy(XT[:, :, bass.ds(i * BLK, BLK)], xT[:]).then_inc(xT_kept, 1)

        @block.scalar
        def _(act):
            act.sem_inc(xT_kept, 1)
            act.sem_inc(lg_rdy, 1)
            with act.Fori(0, BATCH) as b, act.Fori(0, BPB) as j:
                i = b * BPB + j
                act.wait_ge(yT_rdy, i + 1)
                nc.scalar.copy(y[:].rearrange("p t (k c) -> p k t c", c=KV),
                               Y[:, bass.ds(b * KV_HEADS, KV_HEADS), bass.ds(j * BT, BT), :, :]
                               .rearrange("p k t h c -> p k t (h c)")).then_inc(y_rdy, 1)
                act.wait_ge(yT_rdy, i + 2)
                nc.scalar.copy(yT[:], psum[:, 0:2, :]).then_inc(yT_sb, 1)
                act.wait_ge(var_rdy, i + 1)
                nc.scalar.activation(std[:], vare[:], ACT.Sqrt).then_inc(std_rdy, 1)
                act.wait_ge(xT_rdy, i + 2)
                act.wait_ge(xT_kept, i + 1)
                act.wait_ge(lg_rdy, i + 1)
                nc.scalar.copy(xT[:], psum[:, 4:6, :]).then_inc(xT_sb, 1)

        @block.vector
        def _(dve):
            dve.sem_inc(lg_used, 1)
            with dve.Fori(0, BLOCKS) as i:
                steps = [0]

                def then(ins):
                    steps[0] += 1
                    ins.then_inc(dve_step, 1)
                    dve.wait_ge(dve_step, i * DVE_STEPS + steps[0])

                dve.wait_ge(x_in, i * 16 + 16)
                dve.wait_ge(o_rdy, i + 2)
                nc.vector.tensor_tensor(X[:, bass.ds(i * BT, BT), :], X[:, bass.ds(i * BT, BT), :], proj,
                                        ALU.add).then_inc(res_rdy, 1)
                dve.wait_ge(res_rdy, i + 1)
                dve.sem_inc(waited, 1)
                for t in range(BT):
                    last = nc.vector.bn_stats(stats[:, t, :], X[:, bass.ds(i * BT + t, 1), :])
                then(last)
                dve.sem_inc(waited, 1)
                for t in range(BT):
                    last = nc.vector.bn_aggr(mv[:, t, :], stats[:, t, :])
                then(last)
                nc.vector.tensor_scalar(vare[:], mv[:, :, 1], LN_EPS, None, ALU.add).then_inc(var_rdy, 1)
                dve.wait_ge(std_rdy, i + 1)
                then(nc.vector.reciprocal(rstd[:], std[:]))
                dve.wait_ge(xT_rdy, i + 1)
                for t in range(BT):
                    last = nc.vector.tensor_scalar(xn[:, t, :], X[:, bass.ds(i * BT + t, 1), :], mv[:, t, 0:1],
                                                   rstd[:, t:t + 1], ALU.subtract, ALU.mult)
                last.then_inc(xn_rdy, 1)
                dve.wait_ge(lg_rdy, i + 2)
                nc.vector.tensor_copy(logits[:, bass.ds(i * BT, BT), :], lg).then_inc(lg_used, 1)
                assert steps[0] == DVE_STEPS, steps

        @block.tensor
        def _(pe):
            pe.sem_inc(yT_rdy, 1)
            pe.sem_inc(xT_rdy, 1)
            pe.sem_inc(o_rdy, 1)
            pe.wait_ge(const_in, 16 * CONSTS)
            with pe.Fori(0, BLOCKS) as i:
                pe.wait_ge(y_rdy, i + 1)
                for t in range(BT):
                    for c in range(DC):
                        last = nc.tensor.transpose(psum[:, c, t * P:(t + 1) * P], y[:, t, c * P:(c + 1) * P], ident[:])
                last.then_inc(yT_rdy, 1)
                pe.wait_ge(yT_sb, i + 1)
                for t in range(BT):
                    for c in range(DC):
                        last = nc.tensor.matmul(proj[:, t, :], yT[:, c, t * P:(t + 1) * P], wo[:, c, :],
                                                start=(c == 0), stop=(c == DC - 1))
                last.then_inc(o_rdy, 1)
                pe.wait_ge(xn_rdy, i + 1)
                for t in range(BT):
                    for c in range(DC):
                        last = nc.tensor.transpose(psum[:, 4 + c, t * P:(t + 1) * P], xn[:, t, c * P:(c + 1) * P],
                                                   ident[:])
                last.then_inc(xT_rdy, 1)
                pe.wait_ge(xT_sb, i + 1)
                pe.wait_ge(lg_used, i + 1)
                for t in range(BT):
                    for c in range(DC):
                        last = nc.tensor.matmul(lg[:, t, :], xT[:, c, t * P:(t + 1) * P], gw[:, c, :],
                                                start=(c == 0), stop=(c == DC - 1))
                last.then_inc(lg_rdy, 1)


def route(nc, w, logits, combT, combTf, psum):
    with ExitStack() as ctx:
        def sb(name, shape, dt=F32):
            return ctx.enter_context(nc.sbuf_tensor(name, shape, dt))

        def sem(name):
            return ctx.enter_context(nc.semaphore(name))

        PG = EXPERTS // GROUPS
        LOW = -3e38
        ident = sb("r_ident", [P, P])
        identb = sb("r_identb", [P, P], BF16)
        bias = sb("r_bias", [P, EXPERTS])
        before = sb("r_before", [P, GROUPS * GROUPS])
        order = sb("r_order", [P, EXPERTS])
        mx = sb("r_mx", [P, TILES])
        ex = sb("r_ex", [P, TILES, EXPERTS])
        tot = sb("r_tot", [P, TILES])
        orig = sb("r_orig", [P, TILES, EXPERTS])
        sc = sb("r_sc", [P, TILES, EXPERTS])
        hi = sb("r_hi", [P, TILES, GROUPS, 2])
        lo = sb("r_lo", [P, TILES, GROUPS, 2])
        top = sb("r_top", [P, TILES, GROUPS])
        sec = sb("r_sec", [P, TILES, GROUPS])
        sec2 = sb("r_sec2", [P, TILES, GROUPS])
        beat = sb("r_beat", [P, TILES, GROUPS, GROUPS])
        tie = sb("r_tie", [P, TILES, GROUPS, GROUPS])
        rank = sb("r_rank", [P, TILES, GROUPS])
        keep = sb("r_keep", [P, TILES, GROUPS])
        low = sb("r_low", [P, TILES, GROUPS])
        one = [sb(f"r_one{n}", [P, TILES, EXPERTS]) for n in range(2)]
        pos = sb("r_pos", [P, TILES, EXPERTS])
        comb = sb("r_comb", [P, TILES, EXPERTS + 1])
        rest = sb("r_rest", [P, TILES, EXPERTS])
        part = sb("r_part", [P, TILES, PARTS * EXPERTS], BF16)
        const_in, ex_in, ex_rdy, comb_rdy, part_rdy = (
            sem("r_" + n) for n in ("const_in", "ex_in", "ex_rdy", "comb_rdy", "part_rdy"))
        tr_rdy, tr_used, dve_step = sem("r_tr_rdy"), sem("r_tr_used"), sem("r_dve_step")
        CONSTS = 5
        all16 = [P, TILES, EXPERTS]
        GT = TILES // 8

        block = ctx.enter_context(nc.Block())

        @block.sync
        def _(sp):
            for dst, src in ((ident[:], w["ident"]), (identb[:], w["identb"]),
                             (bias[:], w["gate_b"].partition_broadcast(P)),
                             (before[:], w["before"].partition_broadcast(P)),
                             (order[:], w["order"].partition_broadcast(P))):
                sp.dma_start(dst, src).then_inc(const_in, 16)

        @block.scalar
        def _(act):
            act.wait_ge(ex_in, 1)
            nc.scalar.activation(ex[:], ex[:], ACT.Exp).then_inc(ex_rdy, 1)
            for n in range(8):
                act.wait_ge(tr_rdy, n + 1)
                nc.scalar.copy(combTf[0:EXPERTS + 1, n * BLK:(n + 1) * BLK],
                               psum[0:EXPERTS + 1, n, :]).then_inc(tr_used, 1)
            for n in range(4):
                act.wait_ge(tr_rdy, 9 + n)
                nc.scalar.copy(combT[0:PARTS * EXPERTS, n * 2 * BLK:(n + 1) * 2 * BLK],
                               psum[0:PARTS * EXPERTS, n, :].bitcast(BF16)).then_inc(tr_used, 1)

        @block.vector
        def _(dve):
            count = [0]

            def then(ins):
                count[0] += 1
                ins.then_inc(dve_step, 1)
                dve.wait_ge(dve_step, count[0])

            tt, red = nc.vector.tensor_tensor, nc.vector.tensor_reduce
            dve.wait_ge(const_in, 16 * CONSTS)
            then(red(mx[:], logits[:], AX.X, ALU.max))
            tt(ex[:], logits[:], mx[:, :, None].to_broadcast(all16), ALU.subtract).then_inc(ex_in, 1)
            dve.wait_ge(ex_rdy, 1)
            then(red(tot[:], ex[:], AX.X, ALU.add))
            then(nc.vector.reciprocal(tot[:], tot[:]))
            then(tt(orig[:], ex[:], tot[:, :, None].to_broadcast(all16), ALU.mult))
            then(tt(sc[:], orig[:], bias[:, None, :].to_broadcast(all16), ALU.add))
            s4 = sc[:].rearrange("p t (g e) -> p (t g) e", e=PG)
            pair = "p t g e -> p (t g) e"
            tt(hi[:].rearrange(pair), s4[:, :, 0:2], s4[:, :, 2:4], ALU.max)
            then(tt(lo[:].rearrange(pair), s4[:, :, 0:2], s4[:, :, 2:4], ALU.min))
            tt(top[:], hi[:, :, :, 0], hi[:, :, :, 1], ALU.max)
            tt(sec[:], hi[:, :, :, 0], hi[:, :, :, 1], ALU.min)
            then(tt(sec2[:], lo[:, :, :, 0], lo[:, :, :, 1], ALU.max))
            then(tt(sec[:], sec[:], sec2[:], ALU.max))
            then(tt(top[:], top[:], sec[:], ALU.add))
            grid = [P, TILES, GROUPS, GROUPS]
            mine, other = top[:, :, :, None].to_broadcast(grid), top[:, :, None, :].to_broadcast(grid)
            tt(beat[:], other, mine, ALU.is_gt)
            then(tt(tie[:], other, mine, ALU.is_equal))
            flat = "p t g h -> p t (g h)"
            then(tt(tie[:].rearrange(flat), tie[:].rearrange(flat),
                    before[:, None, :].to_broadcast([P, TILES, GROUPS * GROUPS]), ALU.mult))
            then(tt(beat[:], beat[:], tie[:], ALU.add))
            then(red(rank[:], beat[:], AX.X, ALU.add))
            then(nc.vector.tensor_scalar(keep[:], rank[:], 2.0, None, ALU.is_lt))
            then(nc.vector.tensor_scalar(low[:], keep[:], -LOW, LOW, ALU.mult, ALU.add))
            grid = [P, TILES, GROUPS, PG]
            s5 = sc[:].rearrange("p t (g e) -> p t g e", e=PG)
            then(tt(s5, s5, keep[:, :, :, None].to_broadcast(grid), ALU.mult))
            then(tt(s5, s5, low[:, :, :, None].to_broadcast(grid), ALU.add))
            for n in range(2):
                then(red(mx[:], sc[:], AX.X, ALU.max))
                then(tt(pos[:], sc[:], mx[:, :, None].to_broadcast(all16), ALU.is_equal))
                then(tt(pos[:], pos[:], order[:, None, :].to_broadcast(all16), ALU.mult))
                then(red(mx[:], pos[:], AX.X, ALU.max))
                then(tt(one[n][:], pos[:], mx[:, :, None].to_broadcast(all16), ALU.is_equal))
                if n == 0:
                    then(nc.vector.scalar_tensor_tensor(out=sc[:], in0=one[0][:], scalar=LOW, in1=sc[:],
                                                        op0=ALU.mult, op1=ALU.add))
            then(tt(one[0][:], one[0][:], one[1][:], ALU.add))
            nc.vector.memset(comb[:, :, EXPERTS:EXPERTS + 1], 1.0)
            ins = tt(comb[:, :, 0:EXPERTS], one[0][:], orig[:], ALU.mult)
            ins.then_inc(comb_rdy, 1)
            dve.wait_ge(comb_rdy, 1)
            c16 = comb[:, :, 0:EXPERTS]
            p0, p1, p2 = (part[:, :, a * EXPERTS:(a + 1) * EXPERTS] for a in range(PARTS))
            then(nc.vector.tensor_copy(p0, c16))
            then(tt(rest[:], c16, p0, ALU.subtract))
            then(nc.vector.tensor_copy(p1, rest[:]))
            tt(p2, rest[:], p1, ALU.subtract).then_inc(part_rdy, 1)

        @block.tensor
        def _(pe):
            pe.wait_ge(const_in, 16 * CONSTS)
            pe.wait_ge(comb_rdy, 1)
            for n in range(8):
                for t in range(GT):
                    last = nc.tensor.transpose(psum[0:EXPERTS + 1, n, t * P:(t + 1) * P], comb[:, n * GT + t, :],
                                               ident[:])
                last.then_inc(tr_rdy, 1)
            pe.wait_ge(part_rdy, 1)
            for n in range(4):
                pe.wait_ge(tr_used, n + 1)
                dst = psum[0:PARTS * EXPERTS, n, :].bitcast(BF16)
                for t in range(2 * GT):
                    last = nc.tensor.transpose(dst[:, t * P:(t + 1) * P], part[:, n * 2 * GT + t, :], identb[:])
                last.then_inc(tr_rdy, 1)


def experts(nc, w, W1, W3, W2, weights_in, X, XT, combT, combTf, psum, out):
    with ExitStack() as ctx:
        def sb(name, shape, dt=F32):
            return ctx.enter_context(nc.sbuf_tensor(name, shape, dt))

        def sem(name):
            return ctx.enter_context(nc.semaphore(name))

        select = sb("e_select", [PARTS * EXPERTS, EXPERTS, P], BF16)
        b1 = sb("e_b1", [P, ALL_EXPERTS])
        b3 = sb("e_b3", [P, ALL_EXPERTS])
        b2 = sb("e_b2", [EXPERTS + 1, DIM])
        comb = sb("e_comb", [EXPERTS + 1, BLK])
        act1 = sb("e_act1", [P, 2, BLK])
        gated = sb("e_gated", [P, 2, BLK])
        hid = sb("e_hid", [P, 2, BLK])
        res = sb("e_res", [P, BT, DIM])
        const_in, comb_sb, h_rdy, act_rdy, gated_rdy, hid_rdy = (
            sem("e_" + n) for n in ("const_in", "comb_sb", "h_rdy", "act_rdy", "gated_rdy", "hid_rdy"))
        y_rdy, y_done, y_used, out_done = (sem("e_" + n) for n in ("y_rdy", "y_done", "y_used", "out_done"))
        CONSTS = 4
        E = ALL_EXPERTS
        yacc = psum[:, 6:8, :].rearrange("p b (t d) -> p (b t) d", d=DIM)

        block = ctx.enter_context(nc.Block())

        @block.sync
        def _(sp):
            for dst, src in ((select[:], w["select"].rearrange("k (e p) -> k e p", p=P)), (b1[:], w["b1"]),
                             (b3[:], w["b3"]), (b2[:], w["b2"])):
                sp.dma_start(dst, src).then_inc(const_in, 16)
            sp.sem_inc(out_done, 16)
            with sp.Fori(0, BATCH) as b, sp.Fori(0, BPB) as j:
                sp.wait_ge(y_used, b * BPB + j + 2)
                sp.dma_start(out.rearrange("b (j t p) d -> b j p t d", p=P, t=BT)[bass.ds(b, 1), bass.ds(j, 1)],
                             res[:]).then_inc(out_done, 16)
            sp.wait_ge(out_done, 16 + 16 * BLOCKS)

        @block.gpsimd
        def _(pool):
            with pool.Fori(0, BLOCKS) as j:
                pool.wait_ge(y_rdy, j + 1)
                nc.gpsimd.tensor_copy(comb[:], combTf[0:EXPERTS + 1, bass.ds(j * BLK, BLK)]).then_inc(comb_sb, 1)

        @block.scalar
        def _(act):
            act.wait_ge(const_in, 16 * CONSTS)
            with act.Fori(0, BLOCKS) as j:
                for e in range(E):
                    act.wait_ge(h_rdy, j * E + e + 1)
                    act.wait_ge(gated_rdy, j * E + e + 1)
                    nc.scalar.activation(act1[:, e % 2, :], psum[:, (e % 2) * 3, :], ACT.Silu,
                                         bias=b1[:, e:e + 1]).then_inc(act_rdy, 1)

        @block.vector
        def _(dve):
            dve.sem_inc(gated_rdy, 2)
            dve.sem_inc(hid_rdy, 2)
            dve.sem_inc(y_used, 1)
            dve.wait_ge(const_in, 16 * CONSTS)
            with dve.Fori(0, BLOCKS) as j:
                for e in range(E):
                    s = e % 2
                    dve.wait_ge(act_rdy, j * E + e + 1)
                    dve.wait_ge(y_done, j * E + e + 1)
                    dst = gated if e < EXPERTS else hid
                    ins = nc.vector.scalar_tensor_tensor(out=dst[:, s, :], in0=psum[:, s * 3 + 1, :],
                                                         scalar=b3[:, e:e + 1], in1=act1[:, s, :],
                                                         op0=ALU.add, op1=ALU.mult)
                    ins.then_inc(gated_rdy, 1)
                    dve.wait_ge(gated_rdy, j * E + e + 3)
                    if e < EXPERTS:
                        nc.vector.tensor_tensor(hid[:, s, :], gated[:, s, :], psum[:, s * 3 + 2, :],
                                                ALU.mult).then_inc(hid_rdy, 1)
                    else:
                        dve.sem_inc(hid_rdy, 1)
                dve.wait_ge(y_done, (j + 1) * E + 2)
                dve.wait_ge(out_done, j * 16 + 16)
                nc.vector.tensor_tensor(res[:], X[:, bass.ds(j * BT, BT), :], yacc, ALU.add).then_inc(y_used, 1)

        @block.tensor
        def _(pe):
            pe.sem_inc(y_rdy, 1)
            pe.sem_inc(y_done, 2)
            pe.wait_ge(const_in, 16 * CONSTS)
            pe.wait_ge(weights_in, 48)
            with pe.Fori(0, BLOCKS) as j:

                def up(e):
                    pe.wait_ge(hid_rdy, j * E + e + 1)
                    for m, W in enumerate((W1, W3)):
                        for c in range(DC):
                            last = nc.tensor.matmul(psum[:, (e % 2) * 3 + m, :], W[:, e, c, :],
                                                    XT[:, c, bass.ds(j * BLK, BLK)],
                                                    start=(c == 0), stop=(c == DC - 1))
                    if e < EXPERTS:
                        last = nc.tensor.matmul(psum[:, (e % 2) * 3 + 2, :], select[:, e, :],
                                                combT[0:PARTS * EXPERTS, bass.ds(j * BLK, BLK)], start=True, stop=True)
                    last.then_inc(h_rdy, 1)

                def down(e):
                    pe.wait_ge(hid_rdy, j * E + e + 3)
                    for t in range(BT):
                        last = nc.tensor.matmul(yacc[:, t, :], hid[:, e % 2, t * P:(t + 1) * P], W2[:, e, :],
                                                start=False, stop=(e == E - 1), skip_group_check=True)
                    last.then_inc(y_done, 1)

                up(0)
                up(1)
                pe.wait_ge(comb_sb, j + 1)
                pe.wait_ge(y_used, j + 1)
                for t in range(BT):
                    last = nc.tensor.matmul(yacc[:, t, :], comb[:, t * P:(t + 1) * P], b2[:],
                                            start=(t % 2 == 0), stop=False, skip_group_check=True)
                last.then_inc(y_rdy, 1)
                for e in range(E):
                    down(e)
                    if e + 2 < E:
                        up(e + 2)


def layer(nc, w, out):
    w = {n: a.bitcast(BF16) if a.dtype == mybir.dt.uint16 else a for n, a in w.items()}
    with ExitStack() as ctx:
        def sb(name, shape, dt=F32, to=ctx):
            return to.enter_context(nc.sbuf_tensor(name, shape, dt))

        psum = ctx.enter_context(nc.psum_tensor("psum", [P, 8, 512], F32))
        weights_in = ctx.enter_context(nc.semaphore("weights_in"))
        q_parts = nc.dram_tensor("q_parts", [BATCH, HEADS * 2, PARTS, HALF, SEQ], BF16).ap()
        k_parts = nc.dram_tensor("k_parts", [BATCH, KV_HEADS * 2, PARTS, HALF, SEQ], BF16).ap()
        W1 = sb("W1", [P, ALL_EXPERTS, DC, INTER])
        W3 = sb("W3", [P, ALL_EXPERTS, DC, INTER])
        W2 = sb("W2", [P, ALL_EXPERTS, DIM])
        logits = sb("logits", [P, TILES, EXPERTS])
        Y = sb("Y", [P, BATCH * KV_HEADS, SEQ // P, REP, HD])
        for dst, name in ((W1, "w1"), (W3, "w3")):
            nc.sync.dma_start(dst[:], w[name].rearrange("e (c p) i -> p e c i", p=P)).then_inc(weights_in, 16)
        nc.sync.dma_start(W2[:], w["w2"].rearrange("e p d -> p e d")).then_inc(weights_in, 16)
        with ExitStack() as attention:
            V = sb("V", [P, TILES * 2 * KV_HEADS * VC], to=attention)
            project(nc, w, Y[:].rearrange("p n t h c -> p (n t h c)").rearrange("p (t d) -> p t d", d=DIM), V, psum, q_parts, k_parts)
            attend(nc, w, V, Y, psum, q_parts, k_parts)
        X = sb("X2", [P, TILES, DIM])
        XT = sb("XT", [P, DC, TOKENS])
        combT = sb("combT", [PARTS * EXPERTS, TOKENS], BF16)
        combTf = sb("combTf", [EXPERTS + 1, TOKENS])
        finish(nc, w, Y, X, XT, logits, psum)
        route(nc, w, logits, combT, combTf, psum)
        experts(nc, w, W1, W3, W2, weights_in, X, XT, combT, combTf, psum, out)



def _constants():
    freq = (np.arange(0, HD, 2, dtype=np.float32) / np.float32(HD)) * np.float32(np.pi)
    pos = np.arange(SEQ, dtype=np.float32)[:, None]
    radius = np.float32(1.0) / (np.float32(1.0) + pos * np.float32(0.01))
    cos = radius * np.cos(pos * freq[None, :])
    sin = radius * np.sin(pos * freq[None, :])
    key_after = np.arange(P)[None, :] > np.arange(P)[:, None]

    def bits(a):
        return (np.ascontiguousarray(a, np.float32).view(np.uint32) >> 16).astype(np.uint16)

    select = np.zeros((PARTS * EXPERTS, EXPERTS, P), np.float32)
    for e in range(EXPERTS):
        select[e::EXPERTS, e, :] = 1.0
    return {
        "ident": np.eye(P, dtype=np.float32),
        "identb": bits(np.eye(P)),
        "mask": bits(np.where(key_after, -BIG, 0.0)),
        "rot": np.concatenate([cos, cos, sin, -sin], axis=1).astype(np.float32),
        "before": (np.arange(GROUPS)[None, :] < np.arange(GROUPS)[:, None]).astype(np.float32).reshape(-1),
        "order": np.arange(EXPERTS, 0, -1).astype(np.float32),
        "zero_rows": bits(np.zeros((PARTS, REP * SEQ))),
        "ones_rows": bits(np.ones((PARTS, 2 * SEQ))),
        "select": bits(select.reshape(PARTS * EXPERTS, EXPERTS * P)),
    }


def _arrays(a):
    cat, c = np.concatenate, np.ascontiguousarray
    ffn = {k[len("L0_ffn_"):]: v for k, v in a.items() if k.startswith("L0_ffn_")}

    def shared_in(m):
        return m.reshape(DIM, SHARED, INTER).transpose(1, 0, 2)

    return {
        "x": c(a["L0_attn_x"]),
        "w_qkvg": c(cat([a["L0_attn_Wq"].T, a["L0_attn_Wk"].T, a["L0_attn_Wv"].T, a["L0_attn_Wg"].T], axis=1)),
        "w_o": c(a["L0_attn_Wo"].T),
        "q_gain": c(a["L0_attn_q_gain"]),
        "lam": c(a["L0_attn_lambda_param"]),
        "gate_w": c(ffn["gate_w"].T),
        "gate_b": c(ffn["gate_b"]),
        "w1": c(cat([ffn["We1"], shared_in(ffn["ws1"])])),
        "w3": c(cat([ffn["We3"], shared_in(ffn["ws3"])])),
        "w2": c(cat([ffn["We2"], ffn["ws2"].reshape(SHARED, INTER, DIM)])),
        "b1": c(cat([ffn["be1"], ffn["bs1"].reshape(SHARED, INTER)]).T),
        "b3": c(cat([ffn["be3"], ffn["bs3"].reshape(SHARED, INTER)]).T),
        "b2": c(cat([ffn["be2"], ffn["bs2"][None, :]])),
        **_constants(),
    }


def kernel(**inputs):
    import concourse.bacc as _bacc
    from concourse.bass_utils import run_bass_kernel_spmd as _run

    nc = _bacc.Bacc("TRN2", target_bir_lowering=False, num_devices=1)
    arrays = _arrays({k: np.asarray(v) for k, v in inputs.items()})
    w = {n: nc.dram_tensor(n, a.shape, mybir.dt.from_np(a.dtype), kind="ExternalInput").ap()
         for n, a in arrays.items()}
    out = nc.dram_tensor("out", (BATCH, SEQ, DIM), F32, kind="ExternalOutput").ap()
    layer(nc, w, out)
    return _run(nc, [arrays], core_ids=[0]).results[0]["out"]
```

```python
from contextlib import ExitStack

import numpy as np

import concourse.bass as bass
from concourse import mybir

ALU = mybir.AluOpType
ACT = mybir.ActivationFunctionType
F32 = mybir.dt.float32
BF16 = mybir.dt.bfloat16
AX = mybir.AxisListType

P = 128
BATCH, SEQ, DIM = 2, 2048, 256
HEADS, KV_HEADS, HD = 16, 4, 16
REP = HEADS // KV_HEADS
HALF = HD // 2
TOKENS = BATCH * SEQ
TILES = TOKENS // P
BLK = 512
BT = BLK // P
BLOCKS = TOKENS // BLK
BPB = SEQ // BLK
DC = DIM // P
NORMED = HEADS + KV_HEADS
QK = NORMED * HD
KV = KV_HEADS * HD
COLS = QK + 2 * KV
PARTS = 3
ROWS = PARTS * PARTS * HALF
ROWSM = ROWS + PARTS
VC = 32
EXPERTS, GROUPS, INTER = 16, 4, 128
SHARED = 2
ALL_EXPERTS = EXPERTS + SHARED
TOP = 2
ET = P
E_TILES = TOP * TOKENS // ET + EXPERTS
SLOTS = E_TILES * ET
EW = 2 * DC * INTER + DIM + 2
AT_W2, AT_B1, AT_B3 = 2 * DC * INTER, EW - 2, EW - 1
GAIN_LIMIT = 8.0
LN_EPS = 1e-5
RMS_EPS = float(np.finfo(np.float32).eps)
SCALE = 1.0 / float(np.sqrt(HALF))
BIG = 1e30


def load_rows(eng, q_rows, k_rows, q_parts, k_parts, n, h, signal):
    q_src = q_parts.rearrange("b (k r h) p d s -> (b k) h (p d) r s", k=KV_HEADS, h=2)
    k_src = k_parts.rearrange("b (k h) p d s -> (b k) h p d s", h=2)
    for a in range(PARTS):
        rows = slice(a * PARTS * HALF, (a + 1) * PARTS * HALF)
        eng.dma_start(q_rows[rows, :, :], q_src[bass.ds(n, 1), h]).then_inc(signal, 16)
        for p in range(PARTS):
            row = (a * PARTS + p) * HALF
            eng.dma_start(k_rows[row:row + HALF, :], k_src[bass.ds(n, 1), h, a, :, :]).then_inc(signal, 16)


def project(nc, w, X, V, psum, q_parts, k_parts, first_rows):
    with ExitStack() as ctx:
        def sb(name, shape, dt=F32):
            return ctx.enter_context(nc.sbuf_tensor(name, shape, dt))

        def sem(name):
            return ctx.enter_context(nc.semaphore(name))

        wt = sb("p_wt", [P, DC, COLS])
        ident = sb("p_ident", [P, P])
        identb = sb("p_identb", [P, P], BF16)
        rot = sb("p_rot", [P, TILES, 2 * HD])
        gain = sb("p_gain", [P, HEADS])
        stats = sb("p_stats", [P, BT, 6])
        mv = sb("p_mv", [P, BT, 2])
        vare = sb("p_vare", [P, BT])
        std = sb("p_std", [P, BT])
        rstd = sb("p_rstd", [P, BT])
        xn = sb("p_xn", [P, BT, DIM])
        xnT = sb("p_xnT", [P, DC, BLK])
        sq = sb("p_sq", [P, BT, QK])
        ss = sb("p_ss", [P, BT * NORMED])
        sse = sb("p_sse", [P, BT * NORMED])
        rms = sb("p_rms", [P, BT * NORMED])
        rr = sb("p_rr", [P, BT, NORMED])
        sg = sb("p_sg", [P, BT, KV])
        qn = sb("p_qn", [P, BT, NORMED, HD])
        ra = sb("p_ra", [P, BT, NORMED, HD])
        rb = sb("p_rb", [P, BT, NORMED, HD])
        f = sb("p_f", [P, BT, QK])
        r = sb("p_r", [P, BT, QK])
        part = sb("p_part", [P, PARTS, BT, QK], BF16)
        outq = sb("p_outq", [P, PARTS, 2, BLK], BF16)
        outk = sb("p_outk", [KV, PARTS, BLK], BF16)

        waited = sem("p_waited")
        weights_in, const_in, x_in, v_set = sem("p_weights_in"), sem("p_const_in"), sem("p_x_in"), sem("p_v_set")
        var_rdy, std_rdy, xn_rdy = sem("p_var_rdy"), sem("p_std_rdy"), sem("p_xn_rdy")
        xT_rdy, xT_used, pj_rdy, pj_used = sem("p_xT_rdy"), sem("p_xT_used"), sem("p_pj_rdy"), sem("p_pj_used")
        sq_rdy, sg_rdy, ss_rdy, rms_rdy = sem("p_sq_rdy"), sem("p_sg_rdy"), sem("p_ss_rdy"), sem("p_rms_rdy")
        qn_rdy, rb_rdy, f_rdy, r_rdy = sem("p_qn_rdy"), sem("p_rb_rdy"), sem("p_f_rdy"), sem("p_r_rdy")
        hi_rdy, mid_rdy, lo_rdy = sem("p_hi_rdy"), sem("p_mid_rdy"), sem("p_lo_rdy")
        tr_rdy, tr_used, parts_out = sem("p_tr_rdy"), sem("p_tr_used"), sem("p_parts_out")
        ln_step, qk_step = sem("p_ln_step"), sem("p_qk_step")

        xT = psum[:, 0:2, :]
        pj = psum[:, 2:6, :]
        pj_qk = pj[:, :, 0:QK]
        trb = [psum[:, 6 + s, :].bitcast(BF16).rearrange("p (c n) -> p c n", c=2) for s in range(2)]
        x_dram = w["x"].rearrange("b (t p) d -> p (b t) d", p=P)
        WEIGHTS, CONSTS = 3, 3

        block = ctx.enter_context(nc.Block())

        @block.sync
        def _(sp):
            with sp.Fori(0, BLOCKS) as i:
                sp.dma_start(X[:, bass.ds(i * BT, BT), :], x_dram[:, bass.ds(i * BT, BT), :]).then_inc(x_in, 16)
                sp.wait_ge(x_in, i * 16 + 16)
                sp.sem_inc(waited, 1)
            sp.sem_inc(parts_out, 16)
            for b in range(BATCH):
                with sp.Fori(0, BPB) as j:
                    tok = bass.ds(j * BLK, BLK)
                    for p in range(PARTS):
                        done = b * (BPB * 6) + j * 6 + 2 * p
                        sp.wait_ge(tr_used, done + 3)
                        for c in range(2):
                            sp.dma_start(q_parts[b, c * 16:(c + 1) * 16, p, :, tok],
                                         outq[:, p, c, :]).then_inc(parts_out, 16)
                        sp.wait_ge(tr_used, done + 4)
                        sp.dma_start(k_parts[b, :, p, :, tok], outk[:, p]).then_inc(parts_out, 16)
                if b == 0:
                    q_rows, k_rows, rows_in = first_rows
                    sp.wait_ge(parts_out, 16 + BPB * PARTS * 3 * 16)
                    load_rows(sp, q_rows, k_rows, q_parts, k_parts, 0, 0, rows_in)
            sp.wait_ge(parts_out, 16 + BLOCKS * PARTS * 3 * 16)

        @block.gpsimd
        def _(pool):
            v5 = V[:].rearrange("p (n c) -> p n c", c=VC)
            nc.gpsimd.memset(v5[:, :, 0:HALF], 0.0)
            nc.gpsimd.memset(v5[:, :, HALF:HALF + 1], 1.0)
            nc.gpsimd.memset(v5[:, :, HALF + 1:VC], 0.0).then_inc(v_set, 1)
            pool.wait_ge(const_in, 16 * CONSTS)
            with pool.Fori(0, BLOCKS) as i:
                pool.wait_ge(qn_rdy, i + 1)
                for h, o in ((0, 1), (1, 0)):
                    last = nc.gpsimd.tensor_tensor(
                        rb[:, :, :, h * HALF:(h + 1) * HALF], qn[:, :, :, o * HALF:(o + 1) * HALF],
                        rot[:, bass.ds(i * BT, BT), None, HD + h * HALF:HD + (h + 1) * HALF]
                        .to_broadcast([P, BT, NORMED, HALF]), ALU.mult)
                last.then_inc(rb_rdy, 1)

        @block.scalar
        def _(act):
            for dst, src in ((ident[:], w["ident"]), (wt[:], w["w_qkvg"].rearrange("(c p) n -> p c n", p=P)),
                             (identb[:], w["identb"])):
                act.dma_start(dst, src).then_inc(weights_in, 16)
            for dst, src in ((gain[:], w["q_gain"].partition_broadcast(P)),
                             (rot[:, 0:TILES // 2, :], w["rot"].rearrange("(t p) n -> p t n", p=P)),
                             (rot[:, TILES // 2:TILES, :], w["rot"].rearrange("(t p) n -> p t n", p=P))):
                act.dma_start(dst, src).then_inc(const_in, 16)
            act.sem_inc(tr_used, 2)

            def root(i):
                act.wait_ge(var_rdy, i + 1)
                nc.scalar.activation(std[:], vare[:], ACT.Sqrt).then_inc(std_rdy, 1)

            def take_xT(i):
                act.wait_ge(xT_rdy, i + 2)
                act.wait_ge(pj_rdy, i + 1)
                nc.scalar.copy(xnT[:], xT).then_inc(xT_used, 1)

            def squares(i):
                act.wait_ge(pj_rdy, i + 2)
                nc.scalar.activation(sg[:], pj[:, :, QK + KV:COLS], ACT.Sigmoid).then_inc(sg_rdy, 1)
                nc.scalar.activation(sq[:], pj_qk, ACT.Square).then_inc(sq_rdy, 1)

            def root_of_squares(i):
                act.wait_ge(ss_rdy, i + 1)
                nc.scalar.activation(rms[:], sse[:], ACT.Sqrt).then_inc(rms_rdy, 1)

            def take_parts(i):
                act.wait_ge(parts_out, i * 144 + 16)
                for p in range(PARTS):
                    act.wait_ge(tr_rdy, i * 6 + 2 * p + 2)
                    nc.scalar.copy(outq[:, p], trb[0]).then_inc(tr_used, 1)
                    act.wait_ge(tr_rdy, i * 6 + 2 * p + 3)
                    nc.scalar.copy(outk[:, p], trb[1][0:KV, 0, :]).then_inc(tr_used, 1)

            def split(i, upper):
                if upper:
                    act.wait_ge(f_rdy, i + 1)
                    act.wait_ge(tr_rdy, i * 6 + 1)
                    nc.scalar.copy(part[:, 0], f[:]).then_inc(hi_rdy, 1)
                else:
                    act.wait_ge(r_rdy, i + 1)
                    nc.scalar.copy(part[:, 1], r[:]).then_inc(mid_rdy, 1)

            def step(i, first=False, left=2):
                squares(i)
                if left > 0:
                    take_xT(i + 1)
                root_of_squares(i)
                if not first:
                    take_parts(i - 1)
                split(i, upper=True)
                if left > 1:
                    root(i + 2)
                split(i, upper=False)

            root(0)
            take_xT(0)
            root(1)
            step(0, first=True)
            with act.Fori(1, BLOCKS - 2) as i:
                step(i)
            step(BLOCKS - 2, left=1)
            step(BLOCKS - 1, left=0)
            take_parts(BLOCKS - 1)

        @block.vector
        def _(dve):
            dve.sem_inc(pj_used, 1)
            LN_STEPS, QK_STEPS = 3, 4

            def then(ins, signal, count):
                ins.then_inc(signal, 1)
                dve.wait_ge(signal, count)

            def moments(i):
                dve.wait_ge(x_in, i * 16 + 16)
                dve.sem_inc(waited, 1)
                for t in range(BT):
                    last = nc.vector.bn_stats(stats[:, t, :], X[:, bass.ds(i * BT + t, 1), :])
                then(last, ln_step, i * LN_STEPS + 1)
                dve.sem_inc(waited, 1)
                for t in range(BT):
                    last = nc.vector.bn_aggr(mv[:, t, :], stats[:, t, :])
                then(last, ln_step, i * LN_STEPS + 2)
                nc.vector.tensor_scalar(vare[:], mv[:, :, 1], LN_EPS, None, ALU.add).then_inc(var_rdy, 1)

            def normalise(i):
                dve.wait_ge(std_rdy, i + 1)
                then(nc.vector.reciprocal(rstd[:], std[:]), ln_step, i * LN_STEPS + 3)
                dve.wait_ge(xT_rdy, i + 1)
                for t in range(BT):
                    last = nc.vector.tensor_scalar(xn[:, t, :], X[:, bass.ds(i * BT + t, 1), :], mv[:, t, 0:1],
                                                   rstd[:, t:t + 1], ALU.subtract, ALU.mult)
                last.then_inc(xn_rdy, 1)

            def sums(i):
                dve.wait_ge(sq_rdy, i + 1)
                then(nc.vector.tensor_reduce(ss[:], sq[:].rearrange("p t (h d) -> p (t h) d", d=HD), AX.X, ALU.add),
                     qk_step, i * QK_STEPS + 1)
                nc.vector.tensor_scalar(sse[:], ss[:], 1.0 / HD, RMS_EPS, ALU.mult, ALU.add).then_inc(ss_rdy, 1)

            def rms_norm(i):
                dve.wait_ge(rms_rdy, i + 1)
                then(nc.vector.reciprocal(rr[:].rearrange("p t h -> p (t h)"), rms[:]), qk_step, i * QK_STEPS + 2)
                then(nc.vector.tensor_tensor(rr[:, :, 0:HEADS], rr[:, :, 0:HEADS],
                                             gain[:, None, :].to_broadcast([P, BT, HEADS]), ALU.mult),
                     qk_step, i * QK_STEPS + 3)
                dve.wait_ge(sg_rdy, i + 1)
                nc.vector.tensor_tensor(qn[:], pj_qk.rearrange("p t (h d) -> p t h d", d=HD),
                                        rr[:, :, :, None].to_broadcast([P, BT, NORMED, HD]),
                                        ALU.mult).then_inc(qn_rdy, 1)
                for t in range(BT):
                    last = nc.vector.tensor_tensor(
                        V[:, bass.ds((i * BT + t) * 2 * KV_HEADS * VC, 2 * KV_HEADS * VC)]
                        .rearrange("p (n c) -> p n c", c=VC)[:, :, 0:HALF],
                        pj[:, t, QK:QK + KV].rearrange("p (n c) -> p n c", c=HALF),
                        sg[:, t, :].rearrange("p (n c) -> p n c", c=HALF), ALU.mult)
                last.then_inc(pj_used, 1)

            def rotate(i):
                dve.wait_ge(qn_rdy, i + 1)
                then(nc.vector.tensor_tensor(
                    ra[:], qn[:], rot[:, bass.ds(i * BT, BT), None, 0:HD].to_broadcast([P, BT, NORMED, HD]), ALU.mult),
                     qk_step, i * QK_STEPS + 4)
                dve.wait_ge(rb_rdy, i + 1)
                nc.vector.tensor_tensor(f[:], ra[:].rearrange("p t h d -> p t (h d)"),
                                        rb[:].rearrange("p t h d -> p t (h d)"), ALU.add).then_inc(f_rdy, 1)

            def step(i, left=2):
                sums(i)
                rms_norm(i)
                rotate(i)
                if left > 1:
                    moments(i + 2)
                dve.wait_ge(hi_rdy, i + 1)
                nc.vector.tensor_tensor(r[:], f[:], part[:, 0], ALU.subtract).then_inc(r_rdy, 1)
                if left > 1:
                    normalise(i + 2)
                dve.wait_ge(mid_rdy, i + 1)
                nc.vector.tensor_tensor(part[:, 2], r[:], part[:, 1], ALU.subtract).then_inc(lo_rdy, 1)

            for i in range(2):
                moments(i)
                normalise(i)
            dve.wait_ge(const_in, 16 * CONSTS)
            dve.wait_ge(v_set, 1)
            with dve.Fori(0, BLOCKS - 2) as i:
                step(i)
            step(BLOCKS - 2, left=1)
            step(BLOCKS - 1, left=0)

        @block.tensor
        def _(pe):
            pe.sem_inc(xT_rdy, 1)
            pe.sem_inc(pj_rdy, 1)
            pe.sem_inc(tr_rdy, 1)
            pe.wait_ge(weights_in, 16 * WEIGHTS)

            def transpose_x(i):
                pe.wait_ge(xn_rdy, i + 1)
                for t in range(BT):
                    for c in range(DC):
                        last = nc.tensor.transpose(xT[:, c, t * P:(t + 1) * P], xn[:, t, c * P:(c + 1) * P], ident[:])
                last.then_inc(xT_rdy, 1)

            def projections(i):
                pe.wait_ge(xT_used, i + 1)
                pe.wait_ge(pj_used, i + 1)
                for t in range(BT):
                    for c in range(DC):
                        last = nc.tensor.matmul(pj[:, t, 0:COLS], xnT[:, c, t * P:(t + 1) * P], wt[:, c, :],
                                                start=(c == 0), stop=(c == DC - 1))
                last.then_inc(pj_rdy, 1)

            def transpose_parts(i):
                for p, ready in enumerate((hi_rdy, mid_rdy, lo_rdy)):
                    pe.wait_ge(ready, i + 1)
                    for g in range(2):
                        pe.wait_ge(tr_used, i * 6 + 2 * p + g + 1)
                        pe.sem_inc(waited, 1)
                        for c in range(2 if g == 0 else 1):
                            for t in range(BT):
                                cols = (c * P, (c + 1) * P) if g == 0 else (HEADS * HD, QK)
                                last = nc.tensor.transpose(trb[g][0:cols[1] - cols[0], c, t * P:(t + 1) * P],
                                                           part[:, p, t, cols[0]:cols[1]], identb[:])
                        last.then_inc(tr_rdy, 1)

            def step(i, first=False, last=False):
                projections(i)
                if not last:
                    transpose_x(i + 1)
                if not first:
                    transpose_parts(i - 1)

            transpose_x(0)
            step(0, first=True)
            with pe.Fori(1, BLOCKS - 1) as i:
                step(i)
            step(BLOCKS - 1, last=True)
            transpose_parts(BLOCKS - 1)


def attend(nc, w, V, Y, psum, q_parts, k_parts, first_rows, background):
    with ExitStack() as ctx:
        def sb(name, shape, dt=F32):
            return ctx.enter_context(nc.sbuf_tensor(name, shape, dt))

        def sem(name):
            return ctx.enter_context(nc.semaphore(name))

        QT = SEQ // P
        NQ = SEQ // BLK
        RUNS = BATCH * KV_HEADS
        PAIRS = REP // 2
        S_BUFS, P_BUFS = 3, 6
        ACC = 2 * S_BUFS
        units = [(J, tiles) for J in range(NQ)
                 for tiles in [(i,) for i in range(J * BT + 1)] + [(J * BT + 1, J * BT + 3), (J * BT + 2,)]]
        UNITS = len(units)
        last_unit = [max(t for t, (j, _) in enumerate(units) if j == J) for J in range(NQ)]
        LAG = P_BUFS // PAIRS - 1
        TURN = LAG + 2
        SUMS = HALF + 1
        MAXES = REP * QT
        chunks = [(m, c) for m in range(MAXES) for c in range(m % QT // BT + 1)]
        CHUNKS = len(chunks)
        diagonal = [t for t, (J, tiles) in enumerate(units) if tiles[0] >= J * BT]
        assert UNITS * PAIRS % S_BUFS == 0 and UNITS * PAIRS % P_BUFS == 0
        C_BUFS = 2 * S_BUFS

        def spans(J, tiles):
            at, found = 0, []
            for i in tiles:
                lo = max(0, i - J * BT) * P
                found.append((i, lo, at))
                at += BLK - lo
            return found, at

        useful = sb("a_useful", [P, REP * SUMS])
        identb = sb("a_identb", [P, P], BF16)
        mask = sb("a_mask", [P, P], BF16)
        cap = sb("a_cap", [P, P])
        lam = sb("a_lam", [P, BATCH, HEADS])
        gain = sb("a_gain", [P, HEADS])
        gain_max = sb("a_gain_max", [P, 1])
        bounded = sb("a_bounded", [P, 1], mybir.dt.int32)
        qrows = [first_rows[0], sb("a_qrows1", [ROWSM, REP, SEQ], BF16)]
        krows = [first_rows[1], sb("a_krows1", [ROWSM, SEQ], BF16)]
        vals = [sb(f"a_vals{h}", [P, QT, VC]) for h in range(2)]
        probs = sb("a_probs", [P, P_BUFS, 2, BLK])
        chunkmax = sb("a_chunkmax", [P, MAXES, NQ])
        negmax = sb("a_negmax", [P, MAXES])
        rest = sb("a_rest", [P, MAXES])
        maxpart = sb("a_maxpart", [P, PARTS, MAXES], BF16)
        maxT = sb("a_maxT", [MAXES, PARTS, P], BF16)
        outT = sb("a_outT", [P, 2, BLK])
        inv = sb("a_inv", [P, BT, REP])
        invl = sb("a_invl", [P, BT, REP])
        a1 = sb("a_a1", [P, QT, REP, HALF])
        a2 = sb("a_a2", [P, BT, REP, HALF])

        waited = sem("a_waited")
        early_in = sem("a_early_in")
        const_in, flag_rdy, low_set, max_rdy = (sem("a_" + n) for n in ("const_in", "flag_rdy", "low_set", "max_rdy"))
        rows_in = [first_rows[2], sem("a_rows_in1")]
        max_in = [sem(f"a_max_in{h}") for h in range(2)]
        step_done = [sem(f"a_step_done{h}") for h in range(2)]
        vals_rdy = sem("a_vals_rdy")
        mx_rdy, mx_used, max_step = sem("a_mx_rdy"), sem("a_mx_used"), sem("a_max_step")
        mp_rdy, mt_rdy, mt_sb = sem("a_mp_rdy"), sem("a_mt_rdy"), sem("a_mt_sb")
        s_rdy, exp_rdy, av_done = sem("a_s_rdy"), sem("a_exp_rdy"), sem("a_av_done")
        cut_rdy = sem("a_cut_rdy")
        ot_rdy, tm_rdy, tm_used = sem("a_ot_rdy"), sem("a_tm_rdy"), sem("a_tm_used")
        dve_step = sem("a_dve_step")
        ROWS_IN = (PARTS + PARTS * PARTS) * 16

        V4 = V[:].rearrange("p (t n c) -> p t n c", n=2 * KV_HEADS, c=VC)
        maxt = psum[0:MAXES, 0, 0:PARTS * P // 2].bitcast(BF16).rearrange("m (a q) -> m a q", a=PARTS)
        def constant_rows(h):
            return ((krows[h][ROWS:ROWSM, :], w["ones_rows"][:, h * SEQ:(h + 1) * SEQ]),
                    (qrows[h][ROWS:ROWSM, :, :], w["zero_rows"].rearrange("a (r s) -> a r s", r=REP)))

        early = ((gain[:], w["q_gain"].partition_broadcast(P)), (cap[:], w["cap"]), *constant_rows(0))
        consts = ((useful[:], w["useful"]), (identb[:], w["identb"]), (mask[:], w["mask"]), *constant_rows(1),
                  (lam[:, 0, :], w["lam"].partition_broadcast(P)), (lam[:, 1, :], w["lam"].partition_broadcast(P)))
        EARLY, CONSTS = len(early), len(consts)

        def is_bounded(eng):
            eng.wait_ge(flag_rdy, 1)
            return eng.value_load(bounded[0:1, 0:1], min_val=0, max_val=1)

        block = ctx.enter_context(nc.Block())

        @block.sync
        def _(sp):
            for h in range(2):
                sp.sem_inc(step_done[h], 1)
            load_rows(sp, qrows[1], krows[1], q_parts, k_parts, 0, 1, rows_in[1])
            with sp.Fori(1, RUNS) as n:
                for h in range(2):
                    sp.wait_ge(step_done[h], n + 1)
                    load_rows(sp, qrows[h], krows[h], q_parts, k_parts, n, h, rows_in[h])

        @block.gpsimd
        def _(pool):
            def take_values(n, h):
                b, k = n // KV_HEADS, n % KV_HEADS
                pool.wait_ge(step_done[h], n + 1)
                nc.gpsimd.tensor_copy(
                    vals[h][:], V4[:, bass.ds(b * QT, QT), bass.ds(k * 2 + h, 1), :]).then_inc(vals_rdy, 1)

            for h in range(2):
                take_values(0, h)
            for h in range(2):
                pool.wait_ge(rows_in[h], ROWS_IN)
            for dst, src, signal in background:
                nc.gpsimd.dma_start(dst, src).then_inc(signal, 16)
            with pool.Fori(1, RUNS) as n:
                for h in range(2):
                    take_values(n, h)

        @block.scalar
        def _(act):
            for dst, src in early:
                act.dma_start(dst, src).then_inc(early_in, 16)
            for dst, src in consts:
                act.dma_start(dst, src).then_inc(const_in, 16)
            within = is_bounded(act)

            def bring_maxima(step, h):
                act.wait_ge(mt_rdy, step + 1)
                nc.scalar.copy(maxT[:], maxt).then_inc(mt_sb, 1)
                act.wait_ge(mt_sb, step + 1)
                for a in range(PARTS):
                    act.dma_start(qrows[h][ROWS + a:ROWS + a + 1, :, :], maxT[:, a, :]).then_inc(max_in[h], 16)

            def run(n):
                for h in range(2):
                    step = n * 2 + h
                    with act.If(within < 1):
                        bring_maxima(step, h)
                    for t, (J, tiles) in enumerate(units):
                        N = spans(J, tiles)[1]
                        act.wait_ge(av_done, step * UNITS + t + 1)
                        for g in range(PAIRS):
                            u = t * PAIRS + g
                            s = u % S_BUFS
                            act.wait_ge(s_rdy, step * (UNITS * PAIRS) + u + 1)
                            nc.scalar.activation(probs[:, u % P_BUFS, :, 0:N], psum[:, s * 2:s * 2 + 2, 0:N],
                                                 ACT.Exp, scale=SCALE).then_inc(exp_rdy, 1)

            run(0)
            with act.Fori(1, RUNS) as n:
                run(n)

        @block.vector
        def _(dve):
            dve.sem_inc(mx_used, C_BUFS)
            dve.sem_inc(tm_used, 2)
            dve.wait_ge(early_in, 16 * EARLY)
            nc.vector.tensor_reduce(gain_max[:], gain[:], AX.X, ALU.max,
                                    apply_absolute_value=True).then_inc(max_rdy, 1)
            dve.wait_ge(max_rdy, 1)
            nc.vector.tensor_scalar(bounded[:], gain_max[:], GAIN_LIMIT, None, ALU.is_le).then_inc(flag_rdy, 1)
            nc.vector.memset(chunkmax[:], -BIG).then_inc(low_set, 1)
            within = is_bounded(dve)
            dve.wait_ge(low_set, 1)
            MAX_STEPS, TURN_STEPS = 4, [1, 3]
            RUN_STEPS = NQ * sum(TURN_STEPS)

            def find_maxima(step):
                for x, (m, c) in enumerate(chunks):
                    N = min(BLK, (m % QT + 1) * P - c * BLK)
                    dve.wait_ge(mx_rdy, step * CHUNKS + x + 1)
                    nc.vector.tensor_reduce(chunkmax[:, m, c:c + 1], psum[:, x % C_BUFS, 0:N], AX.X,
                                            ALU.max).then_inc(mx_used, 1)
                dve.wait_ge(mx_used, (step + 1) * CHUNKS + C_BUFS)
                for s, ins in enumerate((
                        lambda: nc.vector.tensor_reduce(negmax[:], chunkmax[:], AX.X, ALU.max, negate=True),
                        lambda: nc.vector.tensor_copy(maxpart[:, 0, :], negmax[:]),
                        lambda: nc.vector.tensor_tensor(rest[:], negmax[:], maxpart[:, 0, :], ALU.subtract),
                        lambda: nc.vector.tensor_copy(maxpart[:, 1, :], rest[:]))):
                    ins().then_inc(max_step, 1)
                    dve.wait_ge(max_step, step * MAX_STEPS + s + 1)
                nc.vector.tensor_tensor(maxpart[:, 2, :], rest[:], maxpart[:, 1, :], ALU.subtract).then_inc(mp_rdy, 1)

            def cut(step, t):
                J, tiles = units[t]
                for g in range(PAIRS):
                    u = t * PAIRS + g
                    dve.wait_ge(exp_rdy, step * (UNITS * PAIRS) + u + 1 + S_BUFS)
                    for i, lo, at in spans(J, tiles)[0]:
                        square = probs[:, u % P_BUFS, :, at:at + P]
                        last = nc.vector.tensor_tensor(square, square, cap[:, None, :].to_broadcast([P, 2, P]),
                                                       ALU.min)
                last.then_inc(cut_rdy, 1)

            def copy_out(step, J):
                dve.wait_ge(av_done, step * UNITS + last_unit[J] + LAG + 2)
                nc.vector.tensor_copy(outT[:, J % 2, :], psum[:, ACC + J % 2, :]).then_inc(ot_rdy, 1)

            def normalise(n, h, J):
                step = n * 2 + h
                at = n * RUN_STEPS + (NQ * TURN_STEPS[0] if h else 0) + J * TURN_STEPS[h]
                tok = psum[:, ACC + J % 2, 0:BT * REP * SUMS].rearrange("p (q h c) -> p q h c", h=REP, c=SUMS)
                dve.wait_ge(tm_rdy, step * NQ + J + 1)
                nc.vector.reciprocal(inv[:], tok[:, :, :, HALF]).then_inc(dve_step, 1)
                dve.wait_ge(dve_step, at + 1)
                if h == 0:
                    nc.vector.tensor_tensor(a1[:, J * BT:(J + 1) * BT], tok[:, :, :, 0:HALF],
                                            inv[:, :, :, None].to_broadcast([P, BT, REP, HALF]),
                                            ALU.mult).then_inc(tm_used, 1)
                    return
                lam2 = lam[:].rearrange("p b h -> p (b h)")[:, None, bass.ds(n * REP, REP)]
                nc.vector.tensor_tensor(invl[:], inv[:], lam2.to_broadcast([P, BT, REP]),
                                        ALU.mult).then_inc(dve_step, 1)
                dve.wait_ge(dve_step, at + 2)
                nc.vector.tensor_tensor(a2[:], tok[:, :, :, 0:HALF],
                                        invl[:, :, :, None].to_broadcast([P, BT, REP, HALF]),
                                        ALU.mult).then_inc(tm_used, 1)
                dve.wait_ge(tm_used, step * NQ + J + 3)
                y = Y[:, bass.ds(n, 1), J * BT:(J + 1) * BT, :, :].rearrange("p n t h c -> p (n t) h c")
                nc.vector.tensor_tensor(y[:, :, :, 0:HALF], a1[:, J * BT:(J + 1) * BT], a2[:], ALU.subtract)
                nc.vector.tensor_tensor(y[:, :, :, HALF:HD], a1[:, J * BT:(J + 1) * BT], a2[:],
                                        ALU.add).then_inc(dve_step, 1)
                dve.wait_ge(dve_step, at + 3)

            def run(n, first_run):
                for h in range(2):
                    step = n * 2 + h
                    if first_run and h == 1:
                        dve.wait_ge(const_in, 16 * CONSTS)
                    with dve.If(within < 1):
                        find_maxima(step)
                    for t in range(UNITS):
                        if t in diagonal:
                            cut(step, t)
                        if t == 0 and not (first_run and h == 0):
                            copy_out(step - 1, NQ - 1)
                        if t == LAG and not (first_run and h == 0):
                            normalise(n if h else n - 1, 1 - h, NQ - 1)
                        if t in last_unit[:NQ - 1]:
                            copy_out(step, last_unit.index(t))
                            normalise(n, h, last_unit.index(t))

            run(0, True)
            with dve.Fori(1, RUNS) as n:
                run(n, False)
            copy_out(2 * RUNS - 1, NQ - 1)
            normalise(RUNS - 1, 1, NQ - 1)

        @block.tensor
        def _(pe):
            pe.sem_inc(exp_rdy, S_BUFS)
            pe.sem_inc(av_done, LAG + 1)
            within = is_bounded(pe)

            def maxima(step, h, n):
                pe.wait_ge(exp_rdy, step * UNITS * PAIRS + S_BUFS)
                for x, (m, c) in enumerate(chunks):
                    head, q = divmod(m, QT)
                    N = min(BLK, (q + 1) * P - c * BLK)
                    diag = c == q // BT
                    out = psum[:, x % C_BUFS, :]
                    pe.wait_ge(mx_used, step * CHUNKS + x + 1)
                    last = nc.tensor.matmul(out[:, 0:N], qrows[h][0:ROWS, head, q * P:(q + 1) * P],
                                            krows[h][0:ROWS, c * BLK:c * BLK + N], start=True, stop=not diag)
                    if diag:
                        last = nc.tensor.matmul(out[:, N - P:N], identb[:], mask[:], start=False, stop=True)
                    last.then_inc(mx_rdy, 1)
                pe.wait_ge(mp_rdy, step + 1)
                pe.sem_inc(waited, 1)
                for a in range(PARTS):
                    last = nc.tensor.transpose(maxt[:, a, :], maxpart[:, a, :], identb[:])
                last.then_inc(mt_rdy, 1)
                pe.wait_ge(max_in[h], (n + 1) * 48)

            def scores(step, h, t, bounded):
                J, tiles = units[t]
                for g in range(PAIRS):
                    u = t * PAIRS + g
                    pe.wait_ge(exp_rdy, step * (UNITS * PAIRS) + u + 1)
                    for e in range(2):
                        out = psum[:, (u % S_BUFS) * 2 + e, :]
                        for i, lo, at in spans(J, tiles)[0]:
                            masked = i >= J * BT and not bounded
                            final = i == tiles[-1]
                            last = nc.tensor.matmul(out[:, at:at + BLK - lo], krows[h][:, i * P:(i + 1) * P],
                                                    qrows[h][:, g * 2 + e, J * BLK + lo:(J + 1) * BLK],
                                                    start=(at == 0), stop=final and not masked, skip_group_check=True)
                            if masked:
                                last = nc.tensor.matmul(out[:, at:at + P], mask[:], identb[:], start=False, stop=final,
                                                        skip_group_check=True)
                    last.then_inc(s_rdy, 1)

            def values(step, h, t):
                J, tiles = units[t]
                if tiles[0] == 0:
                    pe.wait_ge(tm_used, step * NQ + J + 1)
                pe.wait_ge(exp_rdy, step * (UNITS * PAIRS) + t * PAIRS + PAIRS + S_BUFS)
                if t in diagonal:
                    pe.wait_ge(cut_rdy, step * len(diagonal) + diagonal.index(t) + 1)
                for i, lo, at in spans(J, tiles)[0]:
                    for head in range(REP):
                        u = t * PAIRS + head // 2
                        last = nc.tensor.matmul(psum[head * VC:(head + 1) * VC, ACC + J % 2, lo:BLK],
                                                vals[h][:, i, :], probs[:, u % P_BUFS, head % 2, at:at + BLK - lo],
                                                start=(i == 0), stop=(t == last_unit[J]))
                last.then_inc(av_done, 1)

            def turn(step, h, J):
                pe.wait_ge(ot_rdy, step * NQ + J + 1)
                for q in range(BT):
                    last = nc.tensor.matmul(psum[:, ACC + J % 2, q * REP * SUMS:(q + 1) * REP * SUMS],
                                            outT[:, J % 2, q * P:(q + 1) * P], useful[:],
                                            start=(q == 0), stop=True, skip_group_check=True)
                    if J == NQ - 1 and q == 0:
                        last.then_inc(step_done[h], 1)
                last.then_inc(tm_rdy, 1)

            def run(n, first_run, bounded):
                for h in range(2):
                    step = n * 2 + h
                    pe.wait_ge(rows_in[h], (n + 1) * ROWS_IN)
                    if not bounded:
                        maxima(step, h, n)
                    pe.wait_ge(vals_rdy, step + 1)
                    for t in range(UNITS):
                        scores(step, h, t, bounded)
                        if bounded and first_run and h == 0 and t == LAG:
                            pe.wait_ge(const_in, 16 * CONSTS)
                        if t >= LAG:
                            values(step, h, t - LAG)
                        elif not (first_run and h == 0):
                            values(step - 1, 1 - h, UNITS + t - LAG)
                        if t == TURN - 1 and not (first_run and h == 0):
                            turn(step - 1, 1 - h, NQ - 1)
                        for J in range(NQ - 1):
                            if t == last_unit[J] + TURN:
                                turn(step, h, J)

            def all_runs(bounded):
                if not bounded:
                    pe.wait_ge(const_in, 16 * CONSTS)
                run(0, True, bounded)
                with pe.Fori(1, RUNS) as n:
                    run(n, False, bounded)

            with pe.If(within < 1):
                all_runs(bounded=False)
            with pe.Else():
                all_runs(bounded=True)
            for t in range(UNITS - LAG, UNITS):
                values(2 * RUNS - 1, 1, t)
            turn(2 * RUNS - 1, 1, NQ - 1)


def finish(nc, w, Y, X, XT, xn_rows, logits, psum):
    with ExitStack() as ctx:
        def sb(name, shape, dt=F32):
            return ctx.enter_context(nc.sbuf_tensor(name, shape, dt))

        def sem(name):
            return ctx.enter_context(nc.semaphore(name))

        wo = sb("f_wo", [P, DC, DIM])
        gw = sb("f_gw", [P, DC, EXPERTS])
        ident = sb("f_ident", [P, P])
        y = sb("f_y", [P, BT, DIM])
        yT = sb("f_yT", [P, DC, BLK])
        stats = sb("f_stats", [P, BT, 6])
        mv = sb("f_mv", [P, BT, 2])
        vare = sb("f_vare", [P, BT])
        std = sb("f_std", [P, BT])
        rstd = sb("f_rstd", [P, BT])
        xn = sb("f_xn", [P, BT, DIM])
        xT = sb("f_xT", [P, DC, BLK])

        waited = sem("f_waited")
        const_in, x_in = sem("f_const_in"), sem("f_x_in")
        y_rdy, yT_rdy, yT_sb, o_rdy, res_rdy = (sem("f_" + n) for n in ("y_rdy", "yT_rdy", "yT_sb", "o_rdy", "res_rdy"))
        var_rdy, std_rdy, xn_rdy, xT_rdy, xT_sb = (
            sem("f_" + n) for n in ("var_rdy", "std_rdy", "xn_rdy", "xT_rdy", "xT_sb"))
        xT_kept, xn_kept, lg_rdy, lg_used, dve_step = (
            sem("f_" + n) for n in ("xT_kept", "xn_kept", "lg_rdy", "lg_used", "dve_step"))
        DVE_STEPS = 3
        CONSTS = 3
        x_dram = w["x"].rearrange("b (t p) d -> p (b t) d", p=P)
        proj = psum[:, 2:4, :].rearrange("p b (t d) -> p (b t) d", d=DIM)
        lg = psum[:, 6, 0:BT * EXPERTS].rearrange("p (t e) -> p t e", e=EXPERTS)

        block = ctx.enter_context(nc.Block())

        @block.sync
        def _(sp):
            for dst, src in ((wo[:], w["w_o"].rearrange("(c p) n -> p c n", p=P)), (ident[:], w["ident"]),
                             (gw[:], w["gate_w"].rearrange("(c p) n -> p c n", p=P))):
                sp.dma_start(dst, src).then_inc(const_in, 16)
            with sp.Fori(0, BLOCKS) as i:
                sp.dma_start(X[:, bass.ds(i * BT, BT), :], x_dram[:, bass.ds(i * BT, BT), :]).then_inc(x_in, 16)
                sp.wait_ge(x_in, i * 16 + 16)
                sp.sem_inc(waited, 1)

        @block.gpsimd
        def _(pool):
            rows = xn_rows.rearrange("(i t p) d -> i p t d", t=BT, p=P)
            with pool.Fori(0, BLOCKS) as i:
                pool.wait_ge(xn_rdy, i + 1)
                nc.gpsimd.dma_start(rows[bass.ds(i, 1)], xn[:]).then_inc(xn_kept, 16)
            pool.wait_ge(xn_kept, 16 * BLOCKS)

        @block.scalar
        def _(act):
            def take_y(i):
                b, j = i // BPB, i % BPB
                act.wait_ge(yT_rdy, i + 1)
                nc.scalar.copy(y[:].rearrange("p t (k c) -> p k t c", c=KV),
                               Y[:, bass.ds(b * KV_HEADS, KV_HEADS), bass.ds(j * BT, BT), :, :]
                               .rearrange("p k t h c -> p k t (h c)")).then_inc(y_rdy, 1)

            def take_yT(i):
                act.wait_ge(yT_rdy, i + 2)
                act.wait_ge(o_rdy, i + 1)
                nc.scalar.copy(yT[:], psum[:, 0:2, :]).then_inc(yT_sb, 1)

            def root(i):
                act.wait_ge(var_rdy, i + 1)
                nc.scalar.activation(std[:], vare[:], ACT.Sqrt).then_inc(std_rdy, 1)

            def take_xT(i):
                act.wait_ge(xT_rdy, i + 2)
                act.wait_ge(lg_rdy, i + 1)
                nc.scalar.copy(xT[:], psum[:, 4:6, :]).then_inc(xT_sb, 1)
                nc.scalar.copy(XT[:, :, bass.ds(i * BLK, BLK)], psum[:, 4:6, :]).then_inc(xT_kept, 1)

            def step(i, first=False, last=False):
                if not first:
                    root(i - 1)
                if not last:
                    take_y(i + 1)
                if not first:
                    take_xT(i - 1)
                if not last:
                    take_yT(i + 1)

            take_y(0)
            take_yT(0)
            step(0, first=True)
            with act.Fori(1, BLOCKS - 1) as i:
                step(i)
            step(BLOCKS - 1, last=True)
            root(BLOCKS - 1)
            take_xT(BLOCKS - 1)

        @block.vector
        def _(dve):
            dve.sem_inc(lg_used, 1)
            dve.sem_inc(res_rdy, 1)

            def take_logits(i):
                dve.wait_ge(lg_rdy, i + 2)
                nc.vector.tensor_copy(logits[:, bass.ds(i * BT, BT), :], lg).then_inc(lg_used, 1)

            def step(i, first=False):
                count = [0]

                def then(ins):
                    count[0] += 1
                    ins.then_inc(dve_step, 1)
                    dve.wait_ge(dve_step, i * DVE_STEPS + count[0])

                dve.wait_ge(x_in, i * 16 + 16)
                dve.wait_ge(o_rdy, i + 2)
                nc.vector.tensor_tensor(X[:, bass.ds(i * BT, BT), :], X[:, bass.ds(i * BT, BT), :], proj,
                                        ALU.add).then_inc(res_rdy, 1)
                dve.wait_ge(res_rdy, i + 2)
                dve.sem_inc(waited, 1)
                for t in range(BT):
                    last = nc.vector.bn_stats(stats[:, t, :], X[:, bass.ds(i * BT + t, 1), :])
                then(last)
                dve.sem_inc(waited, 1)
                for t in range(BT):
                    last = nc.vector.bn_aggr(mv[:, t, :], stats[:, t, :])
                then(last)
                nc.vector.tensor_scalar(vare[:], mv[:, :, 1], LN_EPS, None, ALU.add).then_inc(var_rdy, 1)
                if not first:
                    take_logits(i - 1)
                dve.wait_ge(std_rdy, i + 1)
                then(nc.vector.reciprocal(rstd[:], std[:]))
                dve.wait_ge(xT_rdy, i + 1)
                if not first:
                    dve.wait_ge(xn_kept, i * 16)
                for t in range(BT):
                    last = nc.vector.tensor_scalar(xn[:, t, :], X[:, bass.ds(i * BT + t, 1), :], mv[:, t, 0:1],
                                                   rstd[:, t:t + 1], ALU.subtract, ALU.mult)
                last.then_inc(xn_rdy, 1)
                assert count[0] == DVE_STEPS, count

            step(0, first=True)
            with dve.Fori(1, BLOCKS) as i:
                step(i)
            take_logits(BLOCKS - 1)

        @block.tensor
        def _(pe):
            pe.sem_inc(yT_rdy, 1)
            pe.sem_inc(xT_rdy, 1)
            pe.sem_inc(o_rdy, 1)
            pe.sem_inc(lg_rdy, 1)
            pe.wait_ge(const_in, 16 * CONSTS)

            def transpose_y(i):
                pe.wait_ge(y_rdy, i + 1)
                for t in range(BT):
                    for c in range(DC):
                        last = nc.tensor.transpose(psum[:, c, t * P:(t + 1) * P], y[:, t, c * P:(c + 1) * P], ident[:])
                last.then_inc(yT_rdy, 1)

            def project_y(i):
                pe.wait_ge(yT_sb, i + 1)
                pe.wait_ge(res_rdy, i + 1)
                for t in range(BT):
                    for c in range(DC):
                        last = nc.tensor.matmul(proj[:, t, :], yT[:, c, t * P:(t + 1) * P], wo[:, c, :],
                                                start=(c == 0), stop=(c == DC - 1))
                last.then_inc(o_rdy, 1)

            def transpose_x(i):
                pe.wait_ge(xn_rdy, i + 1)
                pe.wait_ge(xT_kept, i + 1)
                for t in range(BT):
                    for c in range(DC):
                        last = nc.tensor.transpose(psum[:, 4 + c, t * P:(t + 1) * P], xn[:, t, c * P:(c + 1) * P],
                                                   ident[:])
                last.then_inc(xT_rdy, 1)

            def gate(i):
                pe.wait_ge(xT_sb, i + 1)
                pe.wait_ge(lg_used, i + 1)
                for t in range(BT):
                    for c in range(DC):
                        last = nc.tensor.matmul(lg[:, t, :], xT[:, c, t * P:(t + 1) * P], gw[:, c, :],
                                                start=(c == 0), stop=(c == DC - 1))
                last.then_inc(lg_rdy, 1)

            def step(i, first=False, last=False):
                project_y(i)
                if not first:
                    transpose_x(i - 1)
                if not last:
                    transpose_y(i + 1)
                if not first:
                    gate(i - 1)

            pe.sem_inc(xT_kept, 1)
            transpose_y(0)
            step(0, first=True)
            with pe.Fori(1, BLOCKS - 1) as i:
                step(i)
            step(BLOCKS - 1, last=True)
            transpose_x(BLOCKS - 1)
            gate(BLOCKS - 1)


def route(nc, w, logits, b2, scratch, pairs, weight, slot, tile_expert, token, psum):
    with ExitStack() as ctx:
        def sb(name, shape, dt=F32):
            return ctx.enter_context(nc.sbuf_tensor(name, shape, dt))

        def sem(name):
            return ctx.enter_context(nc.semaphore(name))

        PG = EXPERTS // GROUPS
        LOW = -3e38
        all16 = [P, TILES, EXPERTS]
        upper = sb("r_upper", [P, P], BF16)
        ones = sb("r_ones", [P, P], BF16)
        bias = sb("r_bias", [P, EXPERTS])
        before = sb("r_before", [P, GROUPS * GROUPS])
        order = sb("r_order", [P, EXPERTS])
        starts = sb("r_starts", [P, TOKENS // ET])
        upto = sb("r_upto", [P, EXPERTS * EXPERTS])
        tile_no = sb("r_tile_no", [P, E_TILES])
        mx = sb("r_mx", [P, TILES])
        tot = sb("r_tot", [P, TILES])
        ex, sc, orig, pos, one0, one1, place, spare = (
            scratch[:, n * TILES * EXPERTS:(n + 1) * TILES * EXPERTS].rearrange("p (t e) -> p t e", e=EXPERTS)
            for n in range(8))
        one = (one0, one1)
        owner = scratch[:, 0:E_TILES * EXPERTS].rearrange("p (t e) -> p t e", e=EXPERTS)
        hi = sb("r_hi", [P, TILES, GROUPS, 2])
        lo = sb("r_lo", [P, TILES, GROUPS, 2])
        top = sb("r_top", [P, TILES, GROUPS])
        sec = sb("r_sec", [P, TILES, GROUPS])
        sec2 = sb("r_sec2", [P, TILES, GROUPS])
        beat = sb("r_beat", [P, TILES, GROUPS, GROUPS])
        tie = sb("r_tie", [P, TILES, GROUPS, GROUPS])
        rank = sb("r_rank", [P, TILES, GROUPS])
        keep = sb("r_keep", [P, TILES, GROUPS])
        low = sb("r_low", [P, TILES, GROUPS])
        chosen = sb("r_chosen", [P, TILES, EXPERTS], BF16)
        count = sb("r_count", [P, EXPERTS])
        n_tiles = sb("r_n_tiles", [P, EXPERTS])
        end = sb("r_end", [P, EXPERTS])
        first = sb("r_first", [P, EXPERTS])
        slotf = sb("r_slotf", [P, TOP, TILES])
        owner_f = sb("r_owner_f", [P, E_TILES])
        within = sb("r_within", [P, TOP, TILES])
        low_bits = sb("r_low_bits", [P, TOP, TILES], mybir.dt.uint32)
        tile_at = sb("r_tile_at", [P, TOP, TILES])
        column = sb("r_column", [P, ET])
        tile_start = sb("r_tile_start", [P, E_TILES])
        index = sb("r_index", [P, TILES])
        const_in, ones_set, ex_in, ex_rdy = (sem("r_" + n) for n in ("const_in", "ones_set", "ex_in", "ex_rdy"))
        chosen_rdy, count_rdy, rank_rdy, dve_step = (
            sem("r_" + n) for n in ("chosen_rdy", "count_rdy", "rank_rdy", "dve_step"))
        choice_in = sem("r_choice_in")
        b2_in, pair_rdy, pair_used = (sem("r_" + n) for n in ("b2_in", "pair_rdy", "pair_used"))
        CHOICE, CONSTS = 3, 7
        ranks = psum[:, 0, :].rearrange("p (t e) -> p t e", e=EXPERTS)
        counts = psum[:, 1, 0:EXPERTS]
        tokens = psum[:, 2, 0:E_TILES]
        PAIR = ET + E_TILES
        PAIR_BUFS = 32
        one_hot = [pairs[:, r * PAIR:(r + 1) * PAIR] for r in range(PAIR_BUFS)]

        block = ctx.enter_context(nc.Block())

        @block.sync
        def _(sp):
            for dst, src in ((bias[:], w["gate_b"].partition_broadcast(P)),
                             (before[:], w["before"].partition_broadcast(P)),
                             (order[:], w["order"].partition_broadcast(P))):
                sp.dma_start(dst, src).then_inc(choice_in, 16)
            for dst, src in ((upper[:], w["upper"]), (starts[:], w["starts"].partition_broadcast(P)),
                             (upto[:], w["upto"].partition_broadcast(P)),
                             (tile_no[:], w["tile_no"].partition_broadcast(P)),
                             (column[:], w["column"].partition_broadcast(P)),
                             (tile_start[:], w["tile_start"].partition_broadcast(P)),
                             (index[:], w["index"])):
                sp.dma_start(dst, src).then_inc(const_in, 16)
            sp.dma_start(b2, w["b2"].rearrange("e d -> (e d)").partition_broadcast(P)
                         .rearrange("p (e d) -> p e d", d=DIM)).then_inc(b2_in, 16)
            sp.wait_ge(b2_in, 16)

        @block.gpsimd
        def _(pool):
            nc.gpsimd.memset(ones[:], 1.0).then_inc(ones_set, 1)

        @block.scalar
        def _(act):
            act.wait_ge(ex_in, 1)
            nc.scalar.activation(ex, ex, ACT.Exp).then_inc(ex_rdy, 1)


        @block.vector
        def _(dve):
            count_ = [0]

            def then(ins):
                count_[0] += 1
                ins.then_inc(dve_step, 1)
                dve.wait_ge(dve_step, count_[0])

            tt, red = nc.vector.tensor_tensor, nc.vector.tensor_reduce
            dve.sem_inc(pair_used, PAIR_BUFS)
            then(red(mx[:], logits[:], AX.X, ALU.max))
            tt(ex, logits[:], mx[:, :, None].to_broadcast(all16), ALU.subtract).then_inc(ex_in, 1)
            dve.wait_ge(ex_rdy, 1)
            then(red(tot[:], ex, AX.X, ALU.add))
            then(nc.vector.reciprocal(tot[:], tot[:]))
            then(tt(orig, ex, tot[:, :, None].to_broadcast(all16), ALU.mult))
            dve.wait_ge(choice_in, 16 * CHOICE)
            then(tt(sc, orig, bias[:, None, :].to_broadcast(all16), ALU.add))
            s4 = sc.rearrange("p t (g e) -> p (t g) e", e=PG)
            pair = "p t g e -> p (t g) e"
            tt(hi[:].rearrange(pair), s4[:, :, 0:2], s4[:, :, 2:4], ALU.max)
            then(tt(lo[:].rearrange(pair), s4[:, :, 0:2], s4[:, :, 2:4], ALU.min))
            tt(top[:], hi[:, :, :, 0], hi[:, :, :, 1], ALU.max)
            tt(sec[:], hi[:, :, :, 0], hi[:, :, :, 1], ALU.min)
            then(tt(sec2[:], lo[:, :, :, 0], lo[:, :, :, 1], ALU.max))
            then(tt(sec[:], sec[:], sec2[:], ALU.max))
            then(tt(top[:], top[:], sec[:], ALU.add))
            grid = [P, TILES, GROUPS, GROUPS]
            mine, other = top[:, :, :, None].to_broadcast(grid), top[:, :, None, :].to_broadcast(grid)
            tt(beat[:], other, mine, ALU.is_gt)
            then(tt(tie[:], other, mine, ALU.is_equal))
            flat = "p t g h -> p t (g h)"
            then(tt(tie[:].rearrange(flat), tie[:].rearrange(flat),
                    before[:, None, :].to_broadcast([P, TILES, GROUPS * GROUPS]), ALU.mult))
            then(tt(beat[:], beat[:], tie[:], ALU.add))
            then(red(rank[:], beat[:], AX.X, ALU.add))
            then(nc.vector.tensor_scalar(keep[:], rank[:], 2.0, None, ALU.is_lt))
            then(nc.vector.tensor_scalar(low[:], keep[:], -LOW, LOW, ALU.mult, ALU.add))
            grid = [P, TILES, GROUPS, PG]
            s5 = sc.rearrange("p t (g e) -> p t g e", e=PG)
            then(tt(s5, s5, keep[:, :, :, None].to_broadcast(grid), ALU.mult))
            then(tt(s5, s5, low[:, :, :, None].to_broadcast(grid), ALU.add))
            for n in range(2):
                then(red(mx[:], sc, AX.X, ALU.max))
                then(tt(pos, sc, mx[:, :, None].to_broadcast(all16), ALU.is_equal))
                then(tt(pos, pos, order[:, None, :].to_broadcast(all16), ALU.mult))
                then(red(mx[:], pos, AX.X, ALU.max))
                then(tt(one[n], pos, mx[:, :, None].to_broadcast(all16), ALU.is_equal))
                if n == 0:
                    then(nc.vector.scalar_tensor_tensor(out=sc, in0=one[0], scalar=LOW, in1=sc,
                                                        op0=ALU.mult, op1=ALU.add))
            then(tt(chosen[:], one[0], one[1], ALU.add))
            dve.sem_inc(chosen_rdy, 1)
            for n in range(TOP):
                then(tt(pos, one[n], orig, ALU.mult))
                then(red(weight[:, n, :], pos, AX.X, ALU.add))
            dve.wait_ge(const_in, 16 * CONSTS)
            dve.wait_ge(count_rdy, 1)
            then(nc.vector.tensor_copy(count[:], counts))
            square = [P, EXPERTS, EXPERTS]
            grid = spare[:, 0:EXPERTS, :]
            wide = [P, EXPERTS, TOKENS // ET]
            many = spare.rearrange("p t e -> p (t e)").rearrange("p (e n) -> p e n", e=EXPERTS)
            then(tt(many, count[:, :, None].to_broadcast(wide), starts[:, None, :].to_broadcast(wide), ALU.is_gt))
            then(red(n_tiles[:], many, AX.X, ALU.add))
            then(tt(grid, n_tiles[:, None, :].to_broadcast(square),
                    upto[:].rearrange("p (e f) -> p e f", f=EXPERTS), ALU.mult))
            then(red(end[:], grid, AX.X, ALU.add))
            then(tt(first[:], end[:], n_tiles[:], ALU.subtract))
            dve.wait_ge(rank_rdy, 1)
            then(nc.vector.scalar_tensor_tensor(out=place, in0=first[:, None, :].to_broadcast(all16),
                                                scalar=float(ET), in1=ranks, op0=ALU.mult, op1=ALU.add))
            for n in range(TOP):
                then(tt(pos, one[n], place, ALU.mult))
                then(red(slotf[:, n, :], pos, AX.X, ALU.add))
            then(nc.vector.tensor_copy(slot[:], slotf[:]))
            then(nc.vector.tensor_scalar(low_bits[:], slot[:], ET - 1, None, ALU.bitwise_and))
            then(nc.vector.tensor_copy(within[:], low_bits[:]))
            then(tt(tile_at[:], slotf[:], within[:], ALU.subtract))
            for k in range(TOP * TILES):
                n, t = k % TOP, k // TOP
                dve.wait_ge(pair_used, k + 1)
                row = one_hot[k % PAIR_BUFS]
                nc.vector.tensor_scalar(row[:, 0:ET], column[:], within[:, n, t:t + 1], None, ALU.is_equal)
                nc.vector.tensor_scalar(row[:, ET:PAIR], tile_start[:], tile_at[:, n, t:t + 1], index[:, t:t + 1],
                                        ALU.is_equal, ALU.mult).then_inc(pair_rdy, 1)
            wide = [P, E_TILES, EXPERTS]
            then(tt(owner, end[:, None, :].to_broadcast(wide), tile_no[:, :, None].to_broadcast(wide), ALU.is_le))
            then(red(owner_f[:], owner, AX.X, ALU.add))
            then(nc.vector.tensor_scalar(tile_expert[:], owner_f[:], float(EXPERTS - 1), None, ALU.min))

            dve.wait_ge(pair_used, TOP * TILES + PAIR_BUFS)
            then(nc.vector.tensor_copy(token[:], tokens))

        @block.tensor
        def _(pe):
            pe.wait_ge(const_in, 16 * CONSTS)
            pe.wait_ge(ones_set, 1)
            pe.wait_ge(chosen_rdy, 1)
            for t in range(TILES):
                last = nc.tensor.matmul(counts, ones[:], chosen[:, t, :], start=(t == 0), stop=(t == TILES - 1))
            last.then_inc(count_rdy, 1)
            nc.tensor.matmul(psum[:, 0, :], upper[:], chosen[:].rearrange("p t e -> p (t e)"), start=True, stop=False,
                             skip_group_check=True)
            for t in range(TILES - 1):
                later = TILES - 1 - t
                last = nc.tensor.matmul(ranks[:, t + 1:TILES, :], ones[:],
                                        chosen[:, t:t + 1, :].to_broadcast([P, later, EXPERTS]),
                                        start=False, stop=(t == TILES - 2), skip_group_check=True)
            last.then_inc(rank_rdy, 1)
            for k in range(TOP * TILES):
                pe.wait_ge(pair_rdy, k + 1)
                row = one_hot[k % PAIR_BUFS]
                nc.tensor.matmul(tokens, row[:, 0:ET], row[:, ET:PAIR], start=(k == 0),
                                 stop=(k == TOP * TILES - 1)).then_inc(pair_used, 1)


def experts(nc, w, W, b2, memory, tile_expert, token, xn_rows, sorted_y, psum):
    with ExitStack() as ctx:
        def sb(name, shape, dt=F32):
            return ctx.enter_context(nc.sbuf_tensor(name, shape, dt))

        def sem(name):
            return ctx.enter_context(nc.semaphore(name))

        RING = 4
        ident = sb("e_ident", [P, P])
        xs, ys = (memory[:, k * RING * DIM:(k + 1) * RING * DIM].rearrange("p (r d) -> p r d", d=DIM) for k in range(2))
        wt = memory[:, 2 * RING * DIM:RING * (3 * DIM + EW)].rearrange("p (r n) -> p r n", n=EW + DIM)
        xsT = sb("e_xsT", [P, 2, DC, ET])
        act1 = sb("e_act1", [P, 2, ET])
        hid = sb("e_hid", [P, 2, ET])
        const_in = sem("e_const_in")
        x_in = [sem(f"e_x_in{r}") for r in range(RING)]
        y_out = [sem(f"e_y_out{r}") for r in range(RING)]
        tr_rdy, xT_rdy, wt_rdy, h_rdy = (sem("e_" + n) for n in ("tr_rdy", "xT_rdy", "wt_rdy", "h_rdy"))
        act_rdy, hid_rdy, y_rdy, ys_rdy = (sem("e_" + n) for n in ("act_rdy", "hid_rdy", "y_rdy", "ys_rdy"))
        ROUNDS = E_TILES // RING
        rows_out = sorted_y.rearrange("(g r p) d -> g r p d", r=RING, p=P)

        block = ctx.enter_context(nc.Block())

        @block.sync
        def _(sp):
            sp.dma_start(ident[:], w["ident"]).then_inc(const_in, 16)
            for r in range(RING):
                sp.sem_inc(y_out[r], 16)

            with sp.Fori(0, ROUNDS) as g:
                for r in range(RING):
                    sp.wait_ge(ys_rdy, g * RING + r + RING + 1)
                    sp.dma_start(rows_out[bass.ds(g, 1), r], ys[:, r]).then_inc(y_out[r], 16)
            for r in range(RING):
                sp.wait_ge(y_out[r], 16 * (ROUNDS + 1))

        @block.gpsimd
        def _(pool):
            for t in range(E_TILES):
                if t >= RING:
                    pool.wait_ge(tr_rdy, t - RING + 3)
                nc.gpsimd.indirect_dma_start(
                    xs[:, t % RING, :], None,
                    xn_rows, bass.IndirectOffsetOnAxis(ap=token[:, t:t + 1], axis=0)).then_inc(x_in[t % RING], 16)

        @block.scalar
        def _(act):
            def take(t, r):
                e = act.value_load(tile_expert[0:1, bass.ds(t, 1)], min_val=0, max_val=EXPERTS - 1)
                act.wait_ge(ys_rdy, t + 1)
                nc.scalar.copy(wt[:, r, 0:EW], W[:, bass.ds(e, 1), :])
                nc.scalar.copy(wt[:, r, EW:EW + DIM], b2[:, bass.ds(e, 1), :]).then_inc(wt_rdy, 1)

            def silu(t, r):
                s = r % 2
                act.wait_ge(h_rdy, t + 3)
                act.wait_ge(hid_rdy, t + 1)
                act.wait_ge(wt_rdy, t + 1)
                nc.scalar.activation(act1[:, s, :], psum[:, 2 + s, 0:ET], ACT.Silu,
                                     bias=wt[:, r, AT_B1:AT_B1 + 1]).then_inc(act_rdy, 1)

            take(0, 0)
            take(1, 1)

            def round_(g, last=False):
                for r in range(RING):
                    silu(g * RING + r, r)
                    if not last or r + 2 < RING:
                        take(g * RING + r + 2, (r + 2) % RING)

            round_(0)
            with act.Fori(1, ROUNDS - 1) as g:
                round_(g)
            round_(ROUNDS - 1, last=True)

        @block.vector
        def _(dve):
            dve.sem_inc(hid_rdy, 2)
            dve.sem_inc(ys_rdy, RING)
            dve.sem_inc(xT_rdy, 2)

            def take_xT(t, s):
                dve.wait_ge(tr_rdy, t + 3)
                dve.wait_ge(h_rdy, t + 1)
                nc.vector.tensor_copy(xsT[:, s], psum[:, s, 0:DC * ET]).then_inc(xT_rdy, 1)

            def through(g, r, ahead):
                t, s = g * RING + r, r % 2
                dve.wait_ge(act_rdy, t + 1)
                dve.wait_ge(y_rdy, t + RING - 1)
                nc.vector.scalar_tensor_tensor(out=hid[:, s, :], in0=psum[:, 2 + s, ET:2 * ET],
                                               scalar=wt[:, r, AT_B3:AT_B3 + 1], in1=act1[:, s, :],
                                               op0=ALU.add, op1=ALU.mult).then_inc(hid_rdy, 1)
                if ahead:
                    take_xT(t + 2, s)
                dve.wait_ge(y_rdy, t + RING + 1)
                dve.wait_ge(y_out[r], g * 16 + 16)
                nc.vector.tensor_tensor(ys[:, r, :], psum[:, 4 + s, 0:DIM], wt[:, r, EW:EW + DIM],
                                        ALU.add).then_inc(ys_rdy, 1)

            take_xT(0, 0)
            take_xT(1, 1)
            with dve.Fori(0, ROUNDS - 1) as g:
                for r in range(RING):
                    through(g, r, ahead=True)
            for r in range(RING):
                through(ROUNDS - 1, r, ahead=r + 2 < RING)

        @block.tensor
        def _(pe):
            pe.sem_inc(y_rdy, RING)
            pe.wait_ge(const_in, 16)
            pe.sem_inc(tr_rdy, 2)
            pe.sem_inc(h_rdy, 2)

            def transpose(t, g, r):
                s = r % 2
                pe.wait_ge(x_in[r], g * 16 + 16)
                pe.wait_ge(xT_rdy, t + 1)
                for c in range(DC):
                    last = nc.tensor.transpose(psum[:, s, c * ET:(c + 1) * ET], xs[:, r, c * P:(c + 1) * P], ident[:])
                last.then_inc(tr_rdy, 1)

            def up(t, r):
                s = r % 2
                pe.wait_ge(xT_rdy, t + 3)
                pe.wait_ge(wt_rdy, t + 1)
                pe.wait_ge(hid_rdy, t + 1)
                for m in range(2):
                    for c in range(DC):
                        a = (m * DC + c) * INTER
                        last = nc.tensor.matmul(psum[:, 2 + s, m * ET:(m + 1) * ET], wt[:, r, a:a + INTER],
                                                xsT[:, s, c, :], start=(m == 0 and c == 0), stop=(c == DC - 1),
                                                skip_group_check=True)
                last.then_inc(h_rdy, 1)

            def down(t, r):
                s = r % 2
                pe.wait_ge(hid_rdy, t + 3)
                pe.wait_ge(ys_rdy, t + RING - 1)
                nc.tensor.matmul(psum[:, 4 + s, 0:DIM], hid[:, s, :], wt[:, r, AT_W2:AT_W2 + DIM],
                                 start=True, stop=True).then_inc(y_rdy, 1)

            transpose(0, 0, 0)
            transpose(1, 0, 1)
            up(0, 0)
            with pe.Fori(0, ROUNDS - 1) as g:
                for r in range(RING):
                    t = g * RING + r
                    transpose(t + 2, g + (r + 2) // RING, (r + 2) % RING)
                    up(t + 1, (r + 1) % RING)
                    down(t, r)
            for r in range(RING):
                t = (ROUNDS - 1) * RING + r
                if r + 2 < RING:
                    transpose(t + 2, ROUNDS - 1, r + 2)
                if r + 1 < RING:
                    up(t + 1, r + 1)
                down(t, r)


def combine(nc, w, W, X, XT, picked, weight, slot, sorted_y, weights_in, psum, out):
    with ExitStack() as ctx:
        def sb(name, shape, dt=F32):
            return ctx.enter_context(nc.sbuf_tensor(name, shape, dt))

        def sem(name):
            return ctx.enter_context(nc.semaphore(name))

        bias = sb("c_bias", [P, DIM])
        act1 = sb("c_act1", [P, SHARED, BLK])
        hid = sb("c_hid", [P, SHARED, BLK])
        const_in, bias_rdy, out_done = sem("c_const_in"), sem("c_bias_rdy"), sem("c_out_done")
        h_rdy, act_rdy, hid_rdy, y_rdy, y_used = (
            sem("c_" + n) for n in ("h_rdy", "act_rdy", "hid_rdy", "y_rdy", "y_used"))
        first_rdy, both_rdy = sem("c_first_rdy"), sem("c_both_rdy")
        fetched = [sem(f"c_fetched{j}") for j in range(BLOCKS)]
        out_rows = out.rearrange("b (j t p) d -> b j p t d", p=P, t=BT)
        y_sum = [psum[:, b:b + 2, :].rearrange("p b (t d) -> p (b t) d", d=DIM) for b in (6, 0)]

        block = ctx.enter_context(nc.Block())

        @block.sync
        def _(sp):
            sp.dma_start(bias[:], w["bs2"].partition_broadcast(P)).then_inc(const_in, 16)
            for j in range(BLOCKS):
                sp.wait_ge(both_rdy, BT * (j + 1))
                sp.dma_start(out_rows[j // BPB, j % BPB], X[:, j * BT:(j + 1) * BT, :]).then_inc(out_done, 16)
            sp.wait_ge(out_done, 16 * BLOCKS)

        @block.gpsimd
        def _(pool):
            for j in range(BLOCKS):
                for t in range(j * BT, (j + 1) * BT):
                    for n in range(TOP):
                        nc.gpsimd.indirect_dma_start(
                            picked[n][:, t * DIM:(t + 1) * DIM], None,
                            sorted_y, bass.IndirectOffsetOnAxis(ap=slot[:, n, t:t + 1], axis=0)
                        ).then_inc(fetched[j], 16)

        @block.scalar
        def _(act):
            def silu(j):
                for s in range(SHARED):
                    n = j * SHARED + s
                    act.wait_ge(h_rdy, n + 1)
                    act.wait_ge(hid_rdy, n + 1)
                    nc.scalar.activation(act1[:, s, :], psum[:, 2 + 2 * s, :], ACT.Silu,
                                         bias=W[:, EXPERTS + s, AT_B1:AT_B1 + 1]).then_inc(act_rdy, 1)

            silu(0)
            with act.Fori(1, BLOCKS) as j:
                silu(j)

        @block.vector
        def _(dve):
            dve.sem_inc(hid_rdy, 2)
            dve.sem_inc(y_used, 2)
            dve.wait_ge(const_in, 16)

            def gated(j, s):
                n = j * SHARED + s
                dve.wait_ge(act_rdy, n + 1)
                dve.wait_ge(y_rdy, n + 1)
                nc.vector.scalar_tensor_tensor(out=hid[:, s, :], in0=psum[:, 3 + 2 * s, :],
                                               scalar=W[:, EXPERTS + s, AT_B3:AT_B3 + 1], in1=act1[:, s, :],
                                               op0=ALU.add, op1=ALU.mult).then_inc(hid_rdy, 1)

            for s in range(SHARED):
                gated(0, s)
            for j in range(BLOCKS):
                rows = X[:, j * BT:(j + 1) * BT, :]
                nc.vector.tensor_tensor(rows, rows, bias[:, None, :].to_broadcast([P, BT, DIM]),
                                        ALU.add).then_inc(bias_rdy, 1)
                dve.wait_ge(bias_rdy, j + 1)
                dve.wait_ge(y_rdy, (j + 1) * SHARED + 2)
                nc.vector.tensor_tensor(rows, rows, y_sum[j % 2], ALU.add).then_inc(y_used, 1)
                dve.wait_ge(y_used, j + 3)
                if j + 1 < BLOCKS:
                    for s in range(SHARED):
                        gated(j + 1, s)
                dve.wait_ge(fetched[j], 16 * BT * TOP)
                for n, done in ((0, first_rdy), (1, both_rdy)):
                    for t in range(j * BT, (j + 1) * BT):
                        nc.vector.scalar_tensor_tensor(out=X[:, t, :], in0=picked[n][:, t * DIM:(t + 1) * DIM],
                                                       scalar=weight[:, n, t:t + 1], in1=X[:, t, :],
                                                       op0=ALU.mult, op1=ALU.add).then_inc(done, 1)
                    if n == 0:
                        dve.wait_ge(first_rdy, BT * (j + 1))

        @block.tensor
        def _(pe):
            pe.wait_ge(weights_in, 16)
            pe.sem_inc(y_rdy, 2)

            def up(n, j, s):
                pe.wait_ge(hid_rdy, n + 1)
                for m in range(2):
                    for c in range(DC):
                        a = (m * DC + c) * INTER
                        last = nc.tensor.matmul(psum[:, 2 + 2 * s + m, :], W[:, EXPERTS + s, a:a + INTER],
                                                XT[:, c, bass.ds(j * BLK, BLK)], start=(c == 0), stop=(c == DC - 1))
                last.then_inc(h_rdy, 1)

            def down(n, j, s, u):
                pe.wait_ge(hid_rdy, n + 3)
                if s == 0:
                    pe.wait_ge(y_used, j + 1)
                for t in range(BT):
                    last = nc.tensor.matmul(y_sum[u][:, t, :], hid[:, s, t * P:(t + 1) * P],
                                            W[:, EXPERTS + s, AT_W2:AT_W2 + DIM],
                                            start=(s == 0 and t % 2 == 0), stop=(s == SHARED - 1),
                                            skip_group_check=True)
                last.then_inc(y_rdy, 1)

            up(0, 0, 0)
            up(1, 0, 1)
            with pe.Fori(0, BLOCKS // 2 - 1) as g:
                for u in range(2):
                    for s in range(SHARED):
                        n = g * (2 * SHARED) + u * SHARED + s
                        down(n, g * 2 + u, s, u)
                        up(n + 2, g * 2 + u + 1, s)
            for u in range(2):
                for s in range(SHARED):
                    n, j = (BLOCKS - 2 + u) * SHARED + s, BLOCKS - 2 + u
                    down(n, j, s, u)
                    if u == 0:
                        up(n + 2, j + 1, s)


def layer(nc, w, out):
    w = {n: a.bitcast(BF16) if a.dtype == mybir.dt.uint16 else a for n, a in w.items()}
    with ExitStack() as ctx:
        def sb(name, shape, dt=F32, to=ctx):
            return to.enter_context(nc.sbuf_tensor(name, shape, dt))

        psum = ctx.enter_context(nc.psum_tensor("psum", [P, 8, 512], F32))
        weights_in = ctx.enter_context(nc.semaphore("weights_in"))
        q_parts = nc.dram_tensor("q_parts", [BATCH, HEADS * 2, PARTS, HALF, SEQ], BF16).ap()
        k_parts = nc.dram_tensor("k_parts", [BATCH, KV_HEADS * 2, PARTS, HALF, SEQ], BF16).ap()
        xn_rows = nc.dram_tensor("xn_rows", [TOKENS, DIM], F32).ap()
        sorted_y = nc.dram_tensor("sorted_y", [SLOTS, DIM], F32).ap()
        W = sb("W", [P, ALL_EXPERTS, EW])
        logits = sb("logits", [P, TILES, EXPERTS])
        Y = sb("Y", [P, BATCH * KV_HEADS, SEQ // P, REP, HD])
        flat = Y[:].rearrange("p n t h c -> p (n t h c)")
        background = ((W[:], w["experts"].rearrange("e p n -> p e n"), weights_in),)
        with ExitStack() as attention:
            first_rows = (sb("first_qrows", [ROWSM, REP, SEQ], BF16, to=attention),
                          sb("first_krows", [ROWSM, SEQ], BF16, to=attention),
                          attention.enter_context(nc.semaphore("first_rows_in")))
            V = sb("V", [P, TILES * 2 * KV_HEADS * VC], to=attention)
            x = flat.rearrange("p (t d) -> p t d", d=DIM)
            project(nc, w, x, V, psum, q_parts, k_parts, first_rows)
            attend(nc, w, V, Y, psum, q_parts, k_parts, first_rows, background)
        X = sb("X2", [P, TILES, DIM])
        XT = sb("XT", [P, DC, TOKENS])
        finish(nc, w, Y, X, XT, xn_rows, logits, psum)
        b2 = flat[:, 0:EXPERTS * DIM].rearrange("p (e d) -> p e d", d=DIM)
        scratch = flat[:, EXPERTS * DIM:]
        weight = sb("weight", [P, TOP, TILES])
        slot = sb("slot", [P, TOP, TILES], mybir.dt.uint32)
        token = sb("token", [P, E_TILES], mybir.dt.uint32)
        tile_expert = sb("tile_expert", [P, E_TILES], mybir.dt.int32)
        work = sb("work", [P, TILES * DIM])
        route(nc, w, logits, b2, scratch, work, weight, slot, tile_expert, token, psum)
        experts(nc, w, W, b2, work, tile_expert, token, xn_rows, sorted_y, psum)
        combine(nc, w, W, X, XT, (work, flat), weight, slot, sorted_y, weights_in, psum, out)


def _constants():
    freq = (np.arange(0, HD, 2, dtype=np.float32) / np.float32(HD)) * np.float32(np.pi)
    pos = np.arange(SEQ, dtype=np.float32)[:, None]
    radius = np.float32(1.0) / (np.float32(1.0) + pos * np.float32(0.01))
    cos = radius * np.cos(pos * freq[None, :])
    sin = radius * np.sin(pos * freq[None, :])
    key_after = np.arange(P)[None, :] > np.arange(P)[:, None]

    def bits(a):
        return (np.ascontiguousarray(a, np.float32).view(np.uint32) >> 16).astype(np.uint16)

    useful = np.eye(P, dtype=np.float32).reshape(P, REP, VC)[:, :, :HALF + 1]
    return {
        "useful": np.ascontiguousarray(useful.reshape(P, -1)),
        "ident": np.eye(P, dtype=np.float32),
        "identb": bits(np.eye(P)),
        "cap": np.where(key_after.T, 0.0, np.finfo(np.float32).max).astype(np.float32),
        "mask": bits(np.where(key_after, -BIG, 0.0)),
        "rot": np.concatenate([cos, cos, sin, -sin], axis=1).astype(np.float32),
        "before": (np.arange(GROUPS)[None, :] < np.arange(GROUPS)[:, None]).astype(np.float32).reshape(-1),
        "order": np.arange(EXPERTS, 0, -1).astype(np.float32),
        "zero_rows": bits(np.zeros((PARTS, REP * SEQ))),
        "ones_rows": bits(np.ones((PARTS, 2 * SEQ))),
        "upper": bits(key_after),
        "starts": (np.arange(TOKENS // ET) * ET).astype(np.float32),
        "upto": np.tril(np.ones((EXPERTS, EXPERTS), np.float32)).reshape(-1),
        "tile_no": np.arange(E_TILES).astype(np.float32),
        "tile_start": (np.arange(E_TILES) * ET).astype(np.float32),
        "column": np.arange(ET).astype(np.float32),
        "index": np.ascontiguousarray(np.arange(TOKENS).reshape(TILES, P).T.astype(np.float32)),
    }


def _arrays(a):
    cat, c = np.concatenate, np.ascontiguousarray
    ffn = {k[len("L0_ffn_"):]: v for k, v in a.items() if k.startswith("L0_ffn_")}

    def on_partitions(routed, shared):
        m = cat([routed, shared.reshape(DIM, SHARED, INTER).transpose(1, 0, 2)])
        return m.reshape(ALL_EXPERTS, DC, P, INTER).transpose(0, 2, 1, 3).reshape(ALL_EXPERTS, P, DC * INTER)

    def bias(routed, shared):
        return cat([routed, shared.reshape(SHARED, INTER)])[:, :, None]

    return {
        "x": c(a["L0_attn_x"]),
        "w_qkvg": c(cat([a["L0_attn_Wq"].T, a["L0_attn_Wk"].T, a["L0_attn_Wv"].T, a["L0_attn_Wg"].T], axis=1)),
        "w_o": c(a["L0_attn_Wo"].T),
        "q_gain": c(a["L0_attn_q_gain"]),
        "lam": c(a["L0_attn_lambda_param"]),
        "gate_w": c(ffn["gate_w"].T),
        "gate_b": c(ffn["gate_b"]),
        "experts": c(cat([on_partitions(ffn["We1"], ffn["ws1"]), on_partitions(ffn["We3"], ffn["ws3"]),
                          cat([ffn["We2"], ffn["ws2"].reshape(SHARED, INTER, DIM)]),
                          bias(ffn["be1"], ffn["bs1"]), bias(ffn["be3"], ffn["bs3"])], axis=2)),
        "b2": c(ffn["be2"]),
        "bs2": c(ffn["bs2"]),
        **_constants(),
    }


def kernel(**inputs):
    import concourse.bacc as _bacc
    from concourse.bass_utils import run_bass_kernel_spmd as _run

    nc = _bacc.Bacc("TRN2", target_bir_lowering=False, num_devices=1)
    arrays = _arrays({k: np.asarray(v) for k, v in inputs.items()})
    w = {n: nc.dram_tensor(n, a.shape, mybir.dt.from_np(a.dtype), kind="ExternalInput").ap()
         for n, a in arrays.items()}
    out = nc.dram_tensor("out", (BATCH, SEQ, DIM), F32, kind="ExternalOutput").ap()
    layer(nc, w, out)
    return _run(nc, [arrays], core_ids=[0]).results[0]["out"]
```
